# Optimizing a Trainium2 kernel written in Bass

```python
import numpy as np
import jax
import jax.numpy as jnp

def _softmax(x, axis=-1):
    return jax.nn.softmax(x, axis=axis)

def _gelu(x):
    return jax.nn.gelu(x, approximate=True)

def _silu(x):
    return jax.nn.silu(x)

def _sigmoid(x):
    return jax.nn.sigmoid(x)

def _layernorm(x, axis=-1, eps=1e-05):
    m = jnp.mean(x, axis=axis, keepdims=True)
    v = jnp.var(x, axis=axis, keepdims=True)
    return (x - m) / jnp.sqrt(v + eps)

def _scatter_add(tgt, idx, src, axis=0):
    return tgt.at[idx].add(src)

def _segment_sum(src, seg, n):
    return jax.ops.segment_sum(src, seg, n)
kernel_name = 'mk_conv_attn_hybrid_d2_conv_nhwc384_r4_b7fde9'

def setup_inputs(seed: int=0):
    np.random.seed(seed)
    _w = jnp.asarray

    def _rec_inputs():
        import jax
        import jax.numpy as jnp
        _gk = jax.random.key(seed)
        x = -0.0002221 + 1 * jax.random.normal(jax.random.fold_in(_gk, 1), (16, 16, 16, 96), jnp.float32)
        return x
    x = _rec_inputs()

    def _L0_conv_setup():
        import jax, jax.numpy as jnp
        import numpy as np
        import math
        WS = (8, 8)
        SHIFT = (4, 4)
        HEADS = 12
        C_DIM = 96

        def _rel_position_bias(cpb_w1, cpb_b1, cpb_w2):
            ws0, ws1 = WS
            ch = jnp.arange(-(ws0 - 1), ws0, dtype=jnp.float32)
            cw = jnp.arange(-(ws1 - 1), ws1, dtype=jnp.float32)
            table = jnp.stack(jnp.meshgrid(ch, cw, indexing='ij'), axis=-1)
            table = table / jnp.array([ws0 - 1, ws1 - 1], jnp.float32) * 8.0
            table = jnp.sign(table) * jnp.log2(jnp.abs(table) + 1.0) / 3.0
            h = jax.nn.relu(table @ cpb_w1.T + cpb_b1)
            bias_table = (h @ cpb_w2.T).reshape(-1, HEADS)
            coords = np.stack(np.meshgrid(np.arange(ws0), np.arange(ws1), indexing='ij'))
            coords = coords.reshape(2, -1)
            rel = (coords[:, :, None] - coords[:, None, :]).transpose(1, 2, 0)
            rel[..., 0] += ws0 - 1
            rel[..., 1] += ws1 - 1
            rel[..., 0] *= 2 * ws1 - 1
            idx = jnp.asarray(rel.sum(-1))
            bias = bias_table[idx]
            bias = jnp.transpose(bias, (2, 0, 1))
            return 16.0 * jax.nn.sigmoid(bias)

        def _shift_attn_mask(pad_H, pad_W):
            ws0, ws1 = WS
            s0, s1 = SHIFT
            m = np.zeros((pad_H, pad_W), dtype=np.float32)
            cnt = 0
            h_slices = ((0, pad_H - ws0), (pad_H - ws0, pad_H - s0), (pad_H - s0, pad_H))
            w_slices = ((0, pad_W - ws1), (pad_W - ws1, pad_W - s1), (pad_W - s1, pad_W))
            for h0, h1 in h_slices:
                for w0, w1 in w_slices:
                    m[h0:h1, w0:w1] = cnt
                    cnt += 1
            m = m.reshape(pad_H // ws0, ws0, pad_W // ws1, ws1)
            m = m.transpose(0, 2, 1, 3).reshape(-1, ws0 * ws1)
            diff = m[:, None, :] - m[:, :, None]
            mask = np.where(diff != 0, -100.0, 0.0).astype(np.float32)
            return jnp.asarray(mask)
        key = jax.random.key(seed)
        ks = jax.random.split(key, 7)
        C = C_DIM
        x = jax.random.normal(ks[0], (16, 16, 16, C), jnp.float32)
        qkv_w = jax.random.normal(ks[1], (3 * C, C), jnp.float32) * 0.02
        qkv_b = jax.random.normal(ks[2], (3 * C,), jnp.float32) * 0.02
        proj_w = jax.random.normal(ks[3], (C, C), jnp.float32) * 0.02
        proj_b = jax.random.normal(ks[4], (C,), jnp.float32) * 0.02
        logit_scale = jnp.full((HEADS, 1, 1), math.log(10.0), jnp.float32)
        cpb_w1 = jax.random.normal(ks[5], (128, 2), jnp.float32) * 0.02
        cpb_b1 = jnp.zeros((128,), jnp.float32)
        cpb_w2 = jax.random.normal(ks[6], (HEADS, 128), jnp.float32) * 0.02
        return {'x': x, 'qkv_w': qkv_w, 'qkv_b': qkv_b, 'proj_w': proj_w, 'proj_b': proj_b, 'logit_scale': logit_scale, 'cpb_w1': cpb_w1, 'cpb_b1': cpb_b1, 'cpb_w2': cpb_w2}
    _L0_conv_all = _L0_conv_setup()
    _L0_conv_in = {k: v for k, v in _L0_conv_all.items() if k in ('qkv_w', 'qkv_b', 'proj_w', 'proj_b', 'logit_scale', 'cpb_w1', 'cpb_b1', 'cpb_w2')}
    del _L0_conv_all

    def _L1_attn_setup():
        import jax, jax.numpy as jnp
        import numpy as np
        B, T, C = (64, 64, 96)
        HEADS = 6
        HEAD_DIM = C // HEADS
        WINDOW = 16
        key = jax.random.key(seed)
        ks = jax.random.split(key, 5)
        scale = 0.02
        return {'x': jax.random.normal(ks[0], (B, T, C), dtype=jnp.float32), 'qkv_w': jax.random.normal(ks[1], (C, 3 * C), dtype=jnp.float32) * scale, 'qkv_b': jax.random.normal(ks[2], (3 * C,), dtype=jnp.float32) * scale, 'proj_w': jax.random.normal(ks[3], (C, C), dtype=jnp.float32) * scale, 'proj_b': jax.random.normal(ks[4], (C,), dtype=jnp.float32) * scale, 'gate': jnp.ones((C,), dtype=jnp.float32)}
    _L1_attn_all = _L1_attn_setup()
    _L1_attn_in = {k: v for k, v in _L1_attn_all.items() if k in ('qkv_w', 'qkv_b', 'proj_w', 'proj_b', 'gate')}
    del _L1_attn_all

    def _L1_ffn_setup():
        import jax, jax.numpy as jnp
        import numpy as np
        NUM_EXPERTS = 4
        TOP_K = 2
        DIM = 96
        HID = 4 * DIM
        key = jax.random.key(seed)
        ks = jax.random.split(key, 5)
        B, S = (16, 512)
        scale_in = 1.0 / np.sqrt(DIM)
        scale_hid = 1.0 / np.sqrt(HID)
        return {'x': jax.random.normal(ks[0], (B, S, DIM), dtype=jnp.float32), 'gate_w': jax.random.normal(ks[1], (DIM, NUM_EXPERTS), dtype=jnp.float32) * scale_in, 'gate_b': jnp.zeros((NUM_EXPERTS,), dtype=jnp.float32), 'w1': jax.random.normal(ks[2], (NUM_EXPERTS, DIM, HID), dtype=jnp.float32) * scale_in, 'b1': jnp.zeros((NUM_EXPERTS, HID), dtype=jnp.float32), 'w2': jax.random.normal(ks[3], (NUM_EXPERTS, HID, DIM), dtype=jnp.float32) * scale_hid, 'b2': jnp.zeros((NUM_EXPERTS, DIM), dtype=jnp.float32)}
    _L1_ffn_all = _L1_ffn_setup()
    _L1_ffn_in = {k: v for k, v in _L1_ffn_all.items() if k in ('gate_w', 'gate_b', 'w1', 'b1', 'w2', 'b2')}
    del _L1_ffn_all
    return {'x': x, 'L0_conv_qkv_w': _L0_conv_in['qkv_w'], 'L0_conv_qkv_b': _L0_conv_in['qkv_b'], 'L0_conv_proj_w': _L0_conv_in['proj_w'], 'L0_conv_proj_b': _L0_conv_in['proj_b'], 'L0_conv_logit_scale': _L0_conv_in['logit_scale'], 'L0_conv_cpb_w1': _L0_conv_in['cpb_w1'], 'L0_conv_cpb_b1': _L0_conv_in['cpb_b1'], 'L0_conv_cpb_w2': _L0_conv_in['cpb_w2'], 'L1_attn_qkv_w': _L1_attn_in['qkv_w'], 'L1_attn_qkv_b': _L1_attn_in['qkv_b'], 'L1_attn_proj_w': _L1_attn_in['proj_w'], 'L1_attn_proj_b': _L1_attn_in['proj_b'], 'L1_attn_gate': _L1_attn_in['gate'], 'L1_ffn_gate_w': _L1_ffn_in['gate_w'], 'L1_ffn_gate_b': _L1_ffn_in['gate_b'], 'L1_ffn_w1': _L1_ffn_in['w1'], 'L1_ffn_b1': _L1_ffn_in['b1'], 'L1_ffn_w2': _L1_ffn_in['w2'], 'L1_ffn_b2': _L1_ffn_in['b2']}

def reference(x, L0_conv_qkv_w, L0_conv_qkv_b, L0_conv_proj_w, L0_conv_proj_b, L0_conv_logit_scale, L0_conv_cpb_w1, L0_conv_cpb_b1, L0_conv_cpb_w2, L1_attn_qkv_w, L1_attn_qkv_b, L1_attn_proj_w, L1_attn_proj_b, L1_attn_gate, L1_ffn_gate_w, L1_ffn_gate_b, L1_ffn_w1, L1_ffn_b1, L1_ffn_w2, L1_ffn_b2):
    import jax
    import jax.numpy as jnp

    def _L0_conv_ref(x, qkv_w, qkv_b, proj_w, proj_b, logit_scale, cpb_w1, cpb_b1, cpb_w2):
        import jax, jax.numpy as jnp
        import numpy as np
        import math
        WS = (8, 8)
        SHIFT = (4, 4)
        HEADS = 12
        C_DIM = 96

        def _rel_position_bias(cpb_w1, cpb_b1, cpb_w2):
            ws0, ws1 = WS
            ch = jnp.arange(-(ws0 - 1), ws0, dtype=jnp.float32)
            cw = jnp.arange(-(ws1 - 1), ws1, dtype=jnp.float32)
            table = jnp.stack(jnp.meshgrid(ch, cw, indexing='ij'), axis=-1)
            table = table / jnp.array([ws0 - 1, ws1 - 1], jnp.float32) * 8.0
            table = jnp.sign(table) * jnp.log2(jnp.abs(table) + 1.0) / 3.0
            h = jax.nn.relu(table @ cpb_w1.T + cpb_b1)
            bias_table = (h @ cpb_w2.T).reshape(-1, HEADS)
            coords = np.stack(np.meshgrid(np.arange(ws0), np.arange(ws1), indexing='ij'))
            coords = coords.reshape(2, -1)
            rel = (coords[:, :, None] - coords[:, None, :]).transpose(1, 2, 0)
            rel[..., 0] += ws0 - 1
            rel[..., 1] += ws1 - 1
            rel[..., 0] *= 2 * ws1 - 1
            idx = jnp.asarray(rel.sum(-1))
            bias = bias_table[idx]
            bias = jnp.transpose(bias, (2, 0, 1))
            return 16.0 * jax.nn.sigmoid(bias)

        def _shift_attn_mask(pad_H, pad_W):
            ws0, ws1 = WS
            s0, s1 = SHIFT
            m = np.zeros((pad_H, pad_W), dtype=np.float32)
            cnt = 0
            h_slices = ((0, pad_H - ws0), (pad_H - ws0, pad_H - s0), (pad_H - s0, pad_H))
            w_slices = ((0, pad_W - ws1), (pad_W - ws1, pad_W - s1), (pad_W - s1, pad_W))
            for h0, h1 in h_slices:
                for w0, w1 in w_slices:
                    m[h0:h1, w0:w1] = cnt
                    cnt += 1
            m = m.reshape(pad_H // ws0, ws0, pad_W // ws1, ws1)
            m = m.transpose(0, 2, 1, 3).reshape(-1, ws0 * ws1)
            diff = m[:, None, :] - m[:, :, None]
            mask = np.where(diff != 0, -100.0, 0.0).astype(np.float32)
            return jnp.asarray(mask)
        B, H, W, C = x.shape
        ws0, ws1 = WS
        s0, s1 = SHIFT
        L = ws0 * ws1
        hd = C // HEADS
        bias = _rel_position_bias(cpb_w1, cpb_b1, cpb_w2)
        xr = jnp.roll(x, (-s0, -s1), axis=(1, 2))
        nWh, nWw = (H // ws0, W // ws1)
        nW = nWh * nWw
        xw = xr.reshape(B, nWh, ws0, nWw, ws1, C).transpose(0, 1, 3, 2, 4, 5)
        xw = xw.reshape(B * nW, L, C)
        qb = qkv_b.at[C:2 * C].set(0.0)
        qkv = xw @ qkv_w.T + qb
        qkv = qkv.reshape(B * nW, L, 3, HEADS, hd).transpose(2, 0, 3, 1, 4)
        q, k, v = (qkv[0], qkv[1], qkv[2])
        qn = q / jnp.maximum(jnp.linalg.norm(q, axis=-1, keepdims=True), 1e-12)
        kn = k / jnp.maximum(jnp.linalg.norm(k, axis=-1, keepdims=True), 1e-12)
        scale = jnp.exp(jnp.minimum(logit_scale, math.log(100.0)))
        attn = jnp.einsum('whid,whjd->whij', qn, kn) * scale + bias
        mask = _shift_attn_mask(H, W)
        attn = attn.reshape(B, nW, HEADS, L, L) + mask[None, :, None]
        attn = jax.nn.softmax(attn.reshape(B * nW, HEADS, L, L), axis=-1)
        out = jnp.einsum('whij,whjd->whid', attn, v)
        out = out.transpose(0, 2, 1, 3).reshape(B * nW, L, C)
        out = out @ proj_w.T + proj_b
        out = out.reshape(B, nWh, nWw, ws0, ws1, C).transpose(0, 1, 3, 2, 4, 5)
        out = out.reshape(B, H, W, C)
        out = jnp.roll(out, (s0, s1), axis=(1, 2))
        return out

    def _L1_attn_ref(x, qkv_w, qkv_b, proj_w, proj_b, gate):
        import jax, jax.numpy as jnp
        import numpy as np
        B, T, C = (64, 64, 96)
        HEADS = 6
        HEAD_DIM = C // HEADS
        WINDOW = 16
        Bx, Tx, Cx = x.shape
        qkv = x @ qkv_w + qkv_b
        q, k, v = jnp.split(qkv, 3, axis=-1)
        q = q.reshape(Bx, Tx, HEADS, HEAD_DIM).transpose(0, 2, 1, 3)
        k = k.reshape(Bx, Tx, HEADS, HEAD_DIM).transpose(0, 2, 1, 3)
        v = v.reshape(Bx, Tx, HEADS, HEAD_DIM).transpose(0, 2, 1, 3)
        att = jnp.einsum('bhqd,bhkd->bhqk', q, k) * (1.0 / np.sqrt(HEAD_DIM).astype(np.float32))
        idx = jnp.arange(Tx)
        causal = idx[:, None] >= idx[None, :]
        local = jnp.abs(idx[:, None] - idx[None, :]) <= WINDOW
        mask = (causal & local)[None, None, :, :]
        att = jnp.where(mask, att, -jnp.inf)
        att = jax.nn.softmax(att, axis=-1)
        out = jnp.einsum('bhqk,bhkd->bhqd', att, v)
        out = out.transpose(0, 2, 1, 3).reshape(Bx, Tx, Cx)
        return out * gate @ proj_w + proj_b

    def _L1_ffn_ref(x, gate_w, gate_b, w1, b1, w2, b2):
        import jax, jax.numpy as jnp
        import numpy as np
        NUM_EXPERTS = 4
        TOP_K = 2
        DIM = 96
        HID = 4 * DIM
        scores = jnp.einsum('bsd,de->bse', x, gate_w) + gate_b
        probs = jax.nn.softmax(scores, axis=-1)
        topk_vals, topk_idx = jax.lax.top_k(probs, TOP_K)
        mask = jnp.sum(jax.nn.one_hot(topk_idx, NUM_EXPERTS, dtype=probs.dtype), axis=-2)
        masked = probs * mask
        masked = masked / (jnp.sum(masked, axis=-1, keepdims=True) + 1e-09)
        h = jax.nn.gelu(jnp.einsum('bsd,edh->ebsh', x, w1) + b1[:, None, None, :], approximate=False)
        y = jnp.einsum('ebsh,ehd->ebsd', h, w2) + b2[:, None, None, :]
        out = jnp.einsum('bse,ebsd->bsd', masked, y)
        return out

    def _gn(v, G=32, eps=1e-05):
        B_, H_, W_, C_ = v.shape
        g = v.reshape(B_, H_, W_, G, C_ // G)
        m = jnp.mean(g, axis=(1, 2, 4), keepdims=True)
        s = jnp.var(g, axis=(1, 2, 4), keepdims=True)
        return ((g - m) / jnp.sqrt(s + eps)).reshape(v.shape)

    def _ln_c(v, eps=1e-06):
        m = jnp.mean(v, axis=-1, keepdims=True)
        s = jnp.var(v, axis=-1, keepdims=True)
        return (v - m) / jnp.sqrt(s + eps)

    def _ln_t(v, eps=1e-05):
        m = jnp.mean(v, axis=-1, keepdims=True)
        s = jnp.var(v, axis=-1, keepdims=True)
        return (v - m) / jnp.sqrt(s + eps)

    def _to_tokens(v):
        B_, H_, W_, C_ = v.shape
        return v.reshape(B_, H_ * W_, C_)

    def _from_tokens(t, like):
        return t.reshape(like.shape)
    x = x + _L0_conv_ref(_gn(x), L0_conv_qkv_w, L0_conv_qkv_b, L0_conv_proj_w, L0_conv_proj_b, L0_conv_logit_scale, L0_conv_cpb_w1, L0_conv_cpb_b1, L0_conv_cpb_w2)
    t = _to_tokens(x)
    t = t + _L1_attn_ref(_ln_t(t), L1_attn_qkv_w, L1_attn_qkv_b, L1_attn_proj_w, L1_attn_proj_b, L1_attn_gate)
    t = t + _L1_ffn_ref(_ln_t(t), L1_ffn_gate_w, L1_ffn_gate_b, L1_ffn_w1, L1_ffn_b1, L1_ffn_w2, L1_ffn_b2)
    x = _from_tokens(t, x)
    return x

_drawn_inputs = setup_inputs


def setup_inputs(seed=0):
    import zlib

    import numpy as np

    out = dict(_drawn_inputs(seed))
    spreads = {'L0_conv_logit_scale': (2.3025851249694824, 0.6),
     'L0_conv_cpb_b1': (0.0, 2.0),
     'L1_attn_gate': (1.0, 0.6),
     'L1_ffn_gate_b': (0.0, 0.1),
     'L1_ffn_b1': (0.0, 0.1),
     'L1_ffn_b2': (0.0, 0.1)}
    factors = {'L0_conv_qkv_b': 3.126,
     'L0_conv_cpb_w1': 31.581,
     'L0_conv_cpb_w2': 39.108,
     'L1_attn_qkv_b': 3.889}
    for name, (base, spread) in spreads.items():
        noise = np.random.default_rng([zlib.crc32(name.encode()), seed]).standard_normal(out[name].shape)
        drawn = base * np.exp(spread * noise) if base else spread * noise
        out[name] = jnp.asarray(drawn.astype(out[name].dtype))
    for name, factor in factors.items():
        out[name] = (out[name] * factor).astype(out[name].dtype)
    return out
```

```python
from contextlib import ExitStack

import numpy as np

import concourse.bass as bass
from concourse import mybir

F32 = mybir.dt.float32
F16 = mybir.dt.float16
BF16 = mybir.dt.bfloat16
ALU = mybir.AluOpType
ACT = mybir.ActivationFunctionType
AX = mybir.AxisListType

B, HW, C = 16, 16, 96
T = HW * HW
P = 128
UNITS = B * T // P
PER_IMAGE = T // P
K1 = C + 1

WIN, SHIFT = 8, 4
KEYS = 64
BAND = 16
QBLOCK = 32
NQB = P // QBLOCK
GROUPS = 32
GN_EPS, LN_EPS = 1e-5, 1e-5

HEADS0, D0 = 12, C // 12
HEADS1, D1 = 6, C // 6
PAIRS0, PAIRS1 = HEADS0 // 2, HEADS1 // 2
SLOT0, SLOT1 = 32, 64
TILES3 = 3
QK_SCALE0 = 64.0
QK_RANGE1 = 1024.0
MASKED = -1e30

EXPERTS, TOP, HID = 4, 2, 384
CHUNK = 512
CHUNKS = B * T // CHUNK
CT = CHUNK // P
HC = HID // P
NH = EXPERTS * HC


def build(nc, a, out):
    ctx = ExitStack()
    with ctx:
        def sb(name, shape, dt=F32):
            return ctx.enter_context(nc.sbuf_tensor(name, shape, dt))

        def sem(name):
            return ctx.enter_context(nc.semaphore(name))

        perm = sb("perm", [P, 5, P])
        ident = perm[:, 0, :]
        ident_bf = sb("ident_bf", [P, P], BF16)
        ident_h = sb("ident_h", [P, P], F16)
        ident_scaled = sb("ident_scaled", [P, P], F16)
        group_avg = sb("group_avg", [C, C])
        w_qkv = [sb("w_qkv0", [P, 3 * C]), sb("w_qkv1", [P, 3 * C])]
        w_proj = [sb("w_proj0", [P, C]), sb("w_proj1", [P, C])]
        gate_vec = sb("gate_vec", [C, 1])
        w1 = sb("w1", [K1, EXPERTS * HID])
        w2 = sb("w2", [P, NH, C])
        w_gate = sb("w_gate", [K1, EXPERTS])
        bias_bf = sb("bias_bf", [P, 2, 768], F16)
        bias_lo = sb("bias_lo", [P, 2, 768], F16)
        band_f = sb("band_f", [P, 2, KEYS])
        band = sb("band", [P, 2, KEYS], BF16)
        head_scale = sb("head_scale", [P, 2 * HEADS0])
        minus_half = sb("minus_half", [P, 32])
        fac1 = sb("fac1", [P, 2])
        exp_scale1 = sb("exp_scale1", [P, 1])
        x_all = sb("x_all", [P, UNITS, C])
        xT_all = sb("xT_all", [C, B, T])
        gn_scale = sb("gn_scale", [C, B])
        gn_shift = sb("gn_shift", [C, B])
        ln_half = sb("ln_half", [P, UNITS, 6])
        ln_sum = sb("ln_sum", [P, UNITS])
        ln_dif = sb("ln_dif", [P, UNITS])
        ln_mean = sb("ln_mean", [P, UNITS])
        ln_var = sb("ln_var", [P, UNITS])
        ln_rstd = sb("ln_rstd", [P, UNITS])

        bank = [ctx.enter_context(nc.psum_tensor(f"bank{i}", [P, 512], F32)) for i in range(4)]
        score_banks = [ctx.enter_context(nc.psum_tensor(f"score_banks{i}", [P, 2, 512], F32)) for i in range(2)]

        loads_and_tables(nc, sb, sem, a, locals())
        s = locals()
        attention(nc, sb, sem, s, 0)
        attention_scales(nc, sb, sem, s)
        attention(nc, sb, sem, s, 1)
        experts(nc, sb, sem, s, out)


def loads_and_tables(nc, sb, sem, a, s):
    x_all, xT_all, perm, bank, score_banks = s["x_all"], s["xT_all"], s["perm"], s["bank"], s["score_banks"]
    group_avg, gn_scale, gn_shift = s["group_avg"], s["gn_scale"], s["gn_shift"]
    minus_half, head_scale = s["minus_half"], s["head_scale"]
    ident = perm[:, 0, :]
    NREL = (2 * WIN - 1) ** 2
    stats = sb("gn_stats", [C, B, 6])
    gn_sum = sb("gn_sum", [C, 2, B])
    gn_sq = sb("gn_sq", [C, B, 2])
    gn_e2 = sb("gn_e2", [C, B, 2])
    gn_mean = sb("gn_mean", [C, 2, B])
    gn_var = sb("gn_var", [C, B])
    rel_table = sb("rel_table", [3, NREL])
    cpb_w1 = sb("cpb_w1", [3, P])
    cpb_w2 = sb("cpb_w2", [P, HEADS0])
    cpb_h = sb("cpb_h", [P, NREL])
    cpb_e = sb("cpb_e", [HEADS0, NREL])
    cpb_t = sb("cpb_t", [HEADS0, NREL])
    bias_f = sb("bias_f", [P, HEADS0, KEYS])
    win_mask = sb("win_mask", [P, 2, KEYS])
    bias_sum = sb("bias_sum", [P, 2, HEADS0 * KEYS])
    logit = sb("logit", [P, HEADS0])

    rel_dram = nc.dram_tensor("rel_scratch", (HEADS0, NREL), F32)
    col_dram = nc.dram_tensor("col_scratch", (WIN, HEADS0, 2 * WIN - 1, WIN), F32)

    x_loaded = [sem(f"x_loaded{i}") for i in range(4)]
    perm_loaded = sem("perm_loaded")
    table_loaded = sem("table_loaded")
    weights_loaded = sem("weights_loaded")
    xT_ready, xT_copied, stats_ready = sem("xT_ready"), sem("xT_copied"), sem("gn_stats_ready")
    gn_step, gn_group, gn_sums, gn_pow, gn_done = (sem("gn_step"), sem("gn_group"), sem("gn_sums"), sem("gn_pow"),
                                                   sem("gn_done"))
    cpb_mm, cpb_relu, cpb_exp, cpb_table, table_step = (sem("cpb_mm"), sem("cpb_relu"), sem("cpb_exp"),
                                                        sem("cpb_table"), sem("table_step"))
    rel_stored, col_stored, bias_loaded, bias_step = (sem("rel_stored"), sem("col_stored"), sem("bias_loaded"),
                                                      sem("bias_step"))
    half_set, weights_padded = sem("half_set"), sem("weights_padded")
    scale_step = sem("scale_step")
    side = 2 * WIN - 1

    with nc.Block() as block:
        @block.sync
        def _(sp):
            sp.dma_start(perm[:], a["permutations"]).then_inc(perm_loaded, 16)
            xv = a["x"].rearrange("b h w c -> (b h w) c").rearrange("(u p) c -> p u c", p=P)
            for i in range(4):
                part = slice(i * UNITS // 4, (i + 1) * UNITS // 4)
                sp.dma_start(x_all[:, part, :], xv[:, part, :]).then_inc(x_loaded[i], 16)
            sp.wait_ge(weights_padded, 4)
            sp.dma_start(s["w_qkv"][0][0:K1, :], a["w_qkv0"]).then_inc(weights_loaded, 16)
            sp.dma_start(s["w_proj"][0][0:K1, :], a["w_proj0"]).then_inc(weights_loaded, 16)
            sp.dma_start(s["w_qkv"][1][0:K1, :], a["w_qkv1"]).then_inc(weights_loaded, 16)
            sp.dma_start(s["w_proj"][1][0:K1, :], a["w_proj1"]).then_inc(weights_loaded, 16)
            sp.dma_start(s["gate_vec"][:], a["gate_vec"]).then_inc(weights_loaded, 16)
            sp.dma_start(s["w1"][:], a["w1"]).then_inc(weights_loaded, 16)
            sp.dma_start(s["w2"][:], a["w2"]).then_inc(weights_loaded, 16)
            sp.dma_start(s["w_gate"][:], a["w_gate"]).then_inc(weights_loaded, 16)
            sp.wait_ge(weights_loaded, 16 * 8)

        @block.gpsimd
        def _(pool):
            nc.gpsimd.memset(minus_half[:], -0.5).then_inc(half_set, 1)
            pool.dma_start(cpb_w1[:], a["cpb_w1"]).then_inc(table_loaded, 16)
            pool.dma_start(cpb_w2[:], a["cpb_w2"]).then_inc(table_loaded, 16)
            pool.dma_start(rel_table[:], a["rel_table"]).then_inc(table_loaded, 16)
            pool.dma_start(logit[:], a["logit_scale"].partition_broadcast(P)).then_inc(table_loaded, 16)
            pool.dma_start(group_avg[:], a["group_avg"]).then_inc(table_loaded, 16)
            pool.dma_start(win_mask[:], a["win_mask"]).then_inc(table_loaded, 16)
            pool.dma_start(s["band_f"][:], a["band_mask"]).then_inc(table_loaded, 16)
            pool.wait_ge(half_set, 1)
            pool.wait_ge(gn_step, 6)
            nc.gpsimd.tensor_tensor(gn_scale[:], gn_var[:], minus_half[0:C, 0:B], ALU.pow).then_inc(gn_pow, 1)
            pool.wait_ge(table_loaded, 16 * 7)

        @block.scalar
        def _(act):
            act.preload_act_table_set("natural_log_exp_and_others")
            act.wait_ge(cpb_mm, 1)
            nc.scalar.activation(cpb_h[:], bank[3][:, 0:NREL], ACT.Relu).then_inc(cpb_relu, 1)
            act.wait_ge(cpb_mm, 2)
            nc.scalar.activation(cpb_e[:], bank[3][0:HEADS0, 256:256 + NREL], ACT.Exp, scale=-1.0).then_inc(cpb_exp, 1)
            act.wait_ge(cpb_table, 1)
            act.dma_start(rel_dram.ap(), cpb_t[:]).then_inc(rel_stored, 16)
            act.wait_ge(rel_stored, 16)
            rel = rel_dram.ap().rearrange("h (r c) -> h r c", r=side)
            for ci in range(WIN):
                act.dma_start(col_dram.ap()[ci], rel[:, :, WIN - 1 - ci:2 * WIN - 1 - ci]).then_inc(col_stored, 16)
            act.wait_ge(col_stored, 16 * WIN)
            cols = col_dram.ap().rearrange("i h r c -> i h (r c)")
            for half in range(2):
                for ri in range(WIN):
                    at = half * KEYS + ri * WIN
                    act.dma_start(bias_f[at:at + WIN, :, :],
                                  cols[:, :, (WIN - 1 - ri) * WIN:(2 * WIN - 1 - ri) * WIN]).then_inc(bias_loaded, 16)
            act.wait_ge(scale_step, 1)
            nc.scalar.activation(logit[:], logit[:], ACT.Exp).then_inc(scale_step, 1)

        @block.tensor
        def _(pe):
            pe.wait_ge(perm_loaded, 16)
            pe.wait_ge(table_loaded, 16 * 7)
            nc.tensor.matmul(bank[3][:, 0:NREL], cpb_w1[:], rel_table[:], start=True, stop=True).then_inc(cpb_mm, 1)
            pe.wait_ge(cpb_relu, 1)
            nc.tensor.matmul(bank[3][0:HEADS0, 256:256 + NREL], cpb_w2[:], cpb_h[:], start=True,
                             stop=True).then_inc(cpb_mm, 1)
            for b in range(B):
                pe.wait_ge(x_loaded[b // 4], 16)
                if b >= 2:
                    pe.wait_ge(xT_copied, b - 1)
                    pe.wait_ge(stats_ready, b - 1)
                h32 = KEYS // 2
                for tile, (start, width) in enumerate(((0, 5), (h32, 3))):
                    places = bank[b % 2][0:C, start:start + 2 * width * h32].rearrange(
                        "c (w a t) -> c w a t", a=width, t=h32)[:, :, 0:3:2, :]
                    last = pe.transpose(places, x_all[:, 2 * b + tile, :], perm[:, 1 + tile, :])
                last.then_inc(xT_ready, 1)
            pe.wait_ge(gn_sums, 1)
            nc.tensor.matmul(bank[2][0:C, 0:2 * B], group_avg[:], gn_sum[:].rearrange("c a b -> c (a b)"),
                             start=True, stop=True).then_inc(gn_group, 1)

        @block.vector
        def _(v):
            for w in (*s["w_qkv"], *s["w_proj"]):
                v.memset(w[C:P, :], 0.0).then_inc(weights_padded, 1)
            for b in range(B):
                v.wait_ge(xT_ready, b + 1)
                nc.vector.tensor_copy(xT_all[:, b, :], bank[b % 2][0:C, 0:T]).then_inc(xT_copied, 1)
                nc.vector.bn_stats(stats[:, b, :], bank[b % 2][0:C, 0:T]).then_inc(stats_ready, 1)
            v.wait_ge(stats_ready, B)
            st = stats[:].rearrange("c b (e k) -> c b e k", k=3)
            v.tensor_tensor(gn_sq[:], st[:, :, :, 1], st[:, :, :, 1], ALU.mult).then_inc(gn_step, 1)
            v.wait_ge(gn_step, 1)
            v.scalar_tensor_tensor(gn_e2[:], st[:, :, :, 2], 2.0 / T, gn_sq[:], ALU.mult, ALU.add).then_inc(gn_step, 1)
            v.wait_ge(gn_step, 2)
            v.tensor_tensor(gn_sum[:, 0, :], st[:, :, 0, 1], st[:, :, 1, 1], ALU.add)
            v.tensor_tensor(gn_sum[:, 1, :], gn_e2[:, :, 0], gn_e2[:, :, 1], ALU.add).then_inc(gn_sums, 1)
            v.wait_ge(gn_group, 1)
            v.tensor_copy(gn_mean[:].rearrange("c a b -> c (a b)"), bank[2][0:C, 0:2 * B]).then_inc(gn_step, 1)
            v.wait_ge(gn_step, 3)
            v.tensor_tensor(gn_var[:], gn_mean[:, 0, :], gn_mean[:, 0, :], ALU.mult).then_inc(gn_step, 1)
            v.wait_ge(gn_step, 4)
            v.tensor_tensor(gn_var[:], gn_mean[:, 1, :], gn_var[:], ALU.subtract).then_inc(gn_step, 1)
            v.wait_ge(gn_step, 5)
            v.tensor_scalar(gn_var[:], gn_var[:], GN_EPS, None, ALU.add).then_inc(gn_step, 1)
            v.wait_ge(gn_pow, 1)
            v.scalar_tensor_tensor(gn_shift[:], gn_mean[:, 0, :], -1.0, gn_scale[:], ALU.mult,
                                   ALU.mult).then_inc(gn_done, 1)
            v.wait_ge(cpb_exp, 1)
            v.tensor_scalar(cpb_e[:], cpb_e[:], 1.0, None, ALU.add).then_inc(table_step, 1)
            v.wait_ge(table_step, 1)
            v.reciprocal(cpb_t[:], cpb_e[:]).then_inc(table_step, 1)
            v.wait_ge(table_step, 2)
            v.tensor_scalar(cpb_t[:], cpb_t[:], 16.0, None, ALU.mult).then_inc(cpb_table, 1)
            v.wait_ge(perm_loaded, 16)
            v.tensor_copy(s["ident_bf"][:], ident)
            v.tensor_copy(s["ident_h"][:], ident)
            v.tensor_scalar(s["ident_scaled"][:], ident, QK_SCALE0 * QK_SCALE0, None, ALU.mult)
            v.wait_ge(table_loaded, 16 * 7)
            v.tensor_copy(s["band"][:], s["band_f"][:])
            v.tensor_scalar(logit[:], logit[:], float(np.log(100.0)), None, ALU.min).then_inc(scale_step, 1)
            v.wait_ge(scale_step, 2)
            v.memset(head_scale[:, HEADS0:], QK_SCALE0)
            v.tensor_scalar(head_scale[:, 0:HEADS0], logit[:], QK_SCALE0, None, ALU.mult)
            v.wait_ge(bias_loaded, 16 * 2 * WIN)
            for wh in range(2):
                total = bias_sum[:, wh, :]
                v.tensor_tensor(total.rearrange("p (h j) -> p h j", h=HEADS0), bias_f[:],
                                win_mask[:, wh, None, :].to_broadcast([P, HEADS0, KEYS]), ALU.add).then_inc(bias_step, 1)
                v.wait_ge(bias_step, 3 * wh + 1)
                v.tensor_copy(s["bias_bf"][:, wh, :], total).then_inc(bias_step, 1)
                v.wait_ge(bias_step, 3 * wh + 2)
                v.tensor_tensor(s["bias_lo"][:, wh, :], total, s["bias_bf"][:, wh, :],
                                ALU.subtract).then_inc(bias_step, 1)


def attention_scales(nc, sb, sem, s):
    wsq = sb("wsq", [K1, 2 * C])
    ones97 = sb("ones97", [K1, P])
    wmax = sb("wmax", [P, 2])
    sprod = sb("sprod", [P, 1])
    fac1, exp_scale1, w_qkv1, bank = s["fac1"], s["exp_scale1"], s["w_qkv"][1], s["bank"]
    sq_ready, sums_ready, step, powed, rstd_ready = (sem("wsq_ready"), sem("wsums_ready"), sem("wscale_step"),
                                                     sem("wscale_pow"), sem("ln1_rstd_ready"))
    with nc.Block() as block:
        @block.vector
        def _(v):
            v.tensor_scalar(s["w_proj"][1][0:C, :], s["w_proj"][1][0:C, :], s["gate_vec"][:, 0:1], None, ALU.mult)
            v.memset(ones97[:], 1.0)
            v.tensor_tensor(wsq[:], w_qkv1[0:K1, 0:2 * C], w_qkv1[0:K1, 0:2 * C], ALU.mult).then_inc(sq_ready, 1)
            v.wait_ge(sums_ready, 1)
            v.tensor_reduce(wmax[:], bank[0][:, 0:2 * C].rearrange("p (a c) -> p a c", a=2), AX.X,
                            ALU.max).then_inc(step, 1)
            v.wait_ge(step, 1)
            v.tensor_scalar(wmax[:], wmax[:], float(K1), 1e-30, ALU.mult, ALU.max).then_inc(step, 1)
            v.wait_ge(powed, 1)
            v.tensor_scalar(fac1[:], fac1[:], QK_RANGE1, None, ALU.mult).then_inc(step, 1)
            v.wait_ge(step, 3)
            v.tensor_tensor(sprod[:], fac1[:, 0:1], fac1[:, 1:2], ALU.mult).then_inc(step, 1)
            v.wait_ge(step, 4)
            v.reciprocal(exp_scale1[:], sprod[:]).then_inc(step, 1)
            v.wait_ge(step, 5)
            v.tensor_scalar(exp_scale1[:], exp_scale1[:], float(D1) ** -0.5, None, ALU.mult)

        @block.tensor
        def _(pe):
            pe.wait_ge(sq_ready, 1)
            nc.tensor.matmul(bank[0][:, 0:2 * C], ones97[:], wsq[:], start=True, stop=True).then_inc(sums_ready, 1)

        @block.gpsimd
        def _(pool):
            pool.wait_ge(step, 2)
            nc.gpsimd.tensor_tensor(fac1[:], wmax[:], s["minus_half"][:, 0:2], ALU.pow).then_inc(powed, 1)


def norm_statistics(v, s, step):
    half, total, dif = s["ln_half"], s["ln_sum"][:], s["ln_dif"][:]
    v.tensor_tensor(total, half[:, :, 1], half[:, :, 4], ALU.add)
    v.tensor_tensor(dif, half[:, :, 1], half[:, :, 4], ALU.subtract)
    v.tensor_tensor(s["ln_var"][:], half[:, :, 2], half[:, :, 5], ALU.add).then_inc(step, 1)
    v.wait_ge(step, 1)
    v.tensor_scalar(s["ln_mean"][:], total, 0.5, None, ALU.mult)
    v.scalar_tensor_tensor(dif, dif, 0.25, dif, ALU.mult, ALU.mult)
    v.tensor_scalar(s["ln_var"][:], s["ln_var"][:], 1.0 / C, LN_EPS, ALU.mult, ALU.add).then_inc(step, 1)
    v.wait_ge(step, 2)
    v.tensor_tensor(s["ln_var"][:], s["ln_var"][:], dif, ALU.add).then_inc(step, 1)


def at_least(eng, semaphore, count):
    if not (isinstance(count, int) and count <= 0):
        eng.wait_ge(semaphore, count)


def attention(nc, sb, sem, s, layer):
    first = layer == 0
    L = f"{layer}"
    heads, d, pairs, slot = (HEADS0, D0, PAIRS0, SLOT0) if first else (HEADS1, D1, PAIRS1, SLOT1)
    per_tile = heads // TILES3
    vwin = 2 if first else NQB
    vstep = KEYS if first else QBLOCK
    vd = d + 1
    cols = heads * KEYS
    half = cols // 2
    qrows = KEYS if first else QBLOCK
    halo = 0 if first else QBLOCK

    x_all, bank, score_banks = s["x_all"], s["bank"], s["score_banks"]
    w_qkv, w_proj = s["w_qkv"][layer], s["w_proj"][layer]
    perm, ident, ident_bf, ident_h = s["perm"], s["ident"], s["ident_bf"], s["ident_h"]

    xnT = sb("xnT" + L, [P, halo + T])
    sq = sb("sq" + L, [P, 2 * C])
    sumsq = sb("sumsq" + L, [P, 2 * heads])
    log_sum = sb("log_sum" + L, [P, 2 * heads])
    guess = sb("guess" + L, [P, 2 * heads])
    guess_scaled = sb("guess_scaled" + L, [P, 2 * heads])
    newton = sb("newton" + L, [P, 2 * heads])
    rnorm = sb("rnorm" + L, [P, 2 * heads])
    qk = sb("qk" + L, [P, 2 * heads, d])
    stack = sb("stack" + L, [P, 2 * heads, slot], F16)
    qT = sb("qT" + L, [P, TILES3, P], F16)
    kT = sb("kT" + L, [P, TILES3, halo + (P if first else T)], F16)
    negmax = sb("negmax" + L, [P, heads], BF16)
    probs = sb("probs" + L, [P, cols])
    probsT = sb("probsT" + L, [P, pairs, P])
    vals = [sb(f"vals{k}_{L}", [P, vwin, pairs, 2 * vd]) for k in range(2)]
    ones = sb("ones" + L, [P, 1])
    rsum = sb("rsum" + L, [P, heads])
    o_tm = sb("o_tm" + L, [P, PER_IMAGE, C])
    oT = sb("oT" + L, [P, T])
    x_new = sb("x_new" + L, [P, PER_IMAGE, C])
    stat6 = sb("stat6" + L, [P, PER_IMAGE, 6])
    xn_tm = sb("xn_tm" + L, [P, PER_IMAGE, C])

    qk_bank, v_bank, t_bank, o_bank = bank
    stackT_ps = t_bank[:].bitcast(F16)
    PV_COLS = heads * vd
    OT_AT = 128

    pair_of = [2 * (i % TILES3) + i // TILES3 for i in range(pairs)] if first else list(range(pairs))

    names = ("setup", "xn_ready", "xnT_ps", "xnT_ready", "qk_proj_ready", "v_proj_ready", "squares_ready", "squares_summed", "sumsq_ready", "log_ready", "guess_ready",
             "newton_step", "rnorm_ready", "qk_ready", "stack_hi", "stack_ready", "stackT_ready", "qkT_ready", "v_ready",
             "row_group_done", "scores_ready", "negmax_ready", "shifted_ready", "probs_ready", "probsT_ready", "probsT_copied_a",
             "probsT_copied_b", "pv_ready", "rsum_ready", "o_ready", "oT_ready", "oT_copied", "proj_out_ready",
             "x_ready", "bn_ready", "stat_ready", "ln_step", "rstd_ready")
    q = {n: sem(n + L) for n in names}
    SETUPS = 8 if first else 9

    def on(n):
        return not isinstance(n, int) or 0 <= n < UNITS

    def pe_step(pe, b, k):
        n = 2 * b + k
        S = score_banks[k]
        if on(n):
            if not first and k == 0 and on(n + 2):
                at_least(pe, q["xnT_ready"], b + 2)
            at_least(pe, q["qkT_ready"], n + 1)
            at_least(pe, q["probsT_copied_a"], n - 1)
            if first:
                at_least(pe, q["probsT_copied_b"], n - 1)
            for g2 in range(2):
                Sg = S[:, g2, 0:half]
                if first:
                    pe.matmul(Sg, s["ident_scaled"][:], s["bias_bf"][:, k, g2 * half:(g2 + 1) * half],
                              start=True, stop=False, skip_group_check=True)
                    pe.matmul(Sg, s["ident_scaled"][:], s["bias_lo"][:, k, g2 * half:(g2 + 1) * half],
                              start=False, stop=False, skip_group_check=True)
                else:
                    pe.matmul(Sg.rearrange("p (t j) -> p t j", t=TILES3), ident_bf[:],
                              s["band"][:, k, None, :].to_broadcast([P, TILES3, KEYS]),
                              start=True, stop=False, skip_group_check=True)
            for i, g in enumerate((0, 2, 1, 3) if first else (0, 1)):
                if i >= 2:
                    at_least(pe, q["row_group_done"], 2 * n + i - 1)
                for t in range(TILES3):
                    for w in range(P // qrows):
                        rows = slice(slot * g, slot * (g + 1))
                        at = (t * 2 + g % 2) * KEYS if first else t * KEYS
                        k0 = w * KEYS if first else k * P + w * QBLOCK
                        last = pe.matmul(S[w * qrows:(w + 1) * qrows, g // 2 if first else g, at:at + KEYS],
                                         qT[rows, t, w * qrows:(w + 1) * qrows], kT[rows, t, k0:k0 + KEYS],
                                         start=False, stop=True, skip_group_check=True)
                if first and i < 2:
                    last.then_inc(q["row_group_done"], 1)
            last.then_inc(q["scores_ready"], 1)
        if on(n - 1):
            at_least(pe, q["probsT_copied_a"], n)
            if first:
                at_least(pe, q["probsT_copied_b"], n)
            at_least(pe, q["v_ready"], n)
            at_least(pe, q["o_ready"], n - 1)
            if k == 0:
                at_least(pe, q["x_ready"], b - 1)
            else:
                at_least(pe, q["oT_copied"], b)
            for h2 in range(pairs):
                for w in range(P // qrows):
                    rows = slice(w * qrows, (w + 1) * qrows)
                    last = pe.matmul(o_bank[rows, pair_of[h2] * 2 * vd:(pair_of[h2] + 1) * 2 * vd],
                                     probsT[:, h2, rows], vals[(k + 1) % 2][:, w, pair_of[h2], :],
                                     start=True, stop=True)
            last.then_inc(q["pv_ready"], 1)
        if on(n + 2):
            mine = xnT[:, k * P:(k + 1) * P] if first else xnT[:, halo + k * P:halo + (k + 1) * P]
            at_least(pe, q["xnT_ready"], b + 2)
            at_least(pe, q["qk_ready"], n + 2)
            pe.matmul(qk_bank[:, 0:2 * C], mine, w_qkv[:, 0:2 * C], start=True, stop=True).then_inc(q["qk_proj_ready"], 1)
        if on(n):
            at_least(pe, q["negmax_ready"], n + 1)
            for g2 in range(2):
                Sg = S[:, g2, 0:half].rearrange("p (h j) -> p h j", j=KEYS)
                last = pe.matmul(Sg, ident_bf[:],
                                 negmax[:, g2 * heads // 2:(g2 + 1) * heads // 2, None].to_broadcast(
                                     [P, heads // 2, KEYS]), start=False, stop=True, skip_group_check=True)
            last.then_inc(q["shifted_ready"], 1)
        if on(n + 2):
            at_least(pe, q["v_ready"], n + 2)
            base = k * P
            for w in range(vwin // 2):
                at = base + w * vstep
                pe.matmul(v_bank[:, w * C:(w + 1) * C], xnT[:, at:at + P], w_qkv[:, 2 * C:3 * C],
                          start=True, stop=True)
                far = w + vwin // 2
                pe.matmul(v_bank[0:KEYS, far * C:(far + 1) * C], xnT[:, at + KEYS:at + 2 * KEYS],
                          w_qkv[:, 2 * C:3 * C], start=True, stop=True)
                last = pe.matmul(v_bank[KEYS:P, far * C:(far + 1) * C], xnT[:, at:at + KEYS],
                                 w_qkv[:, 2 * C:3 * C], start=True, stop=True)
            last.then_inc(q["v_proj_ready"], 1)
        if not first and k == 1 and on(n + 3):
            at_least(pe, q["xn_ready"], b + 3)
            for i in range(PER_IMAGE):
                last = pe.transpose(score_banks[0][0:C, i, half:half + P], xn_tm[:, i, :], ident)
            last.then_inc(q["xnT_ps"], 1)
        if on(n + 1):
            at_least(pe, q["stack_ready"], n + 2)
            at_least(pe, q["qkT_ready"], n + 1)
            st = stack[:].rearrange("p h e -> p (h e)")
            for t in range(2 * TILES3):
                last = pe.transpose(stackT_ps[:, t * P:(t + 1) * P], st[:, t * P:(t + 1) * P], ident_h[:])
            last.then_inc(q["stackT_ready"], 1)
        if k == 0 and on(n - 1):
            at_least(pe, q["o_ready"], n)
            to = o_bank[0:C, OT_AT:OT_AT + T]
            if first:
                pe.transpose(to[:, 64:192], o_tm[:, 0, :], perm[:, 3, :])
                wrap = to.rearrange("c (a t) -> c a t", a=4)[:, 0:4:3, :]
                last = pe.transpose(wrap, o_tm[:, 1, :], perm[:, 4, :])
            else:
                pe.transpose(to[:, 0:P], o_tm[:, 0, :], ident)
                last = pe.transpose(to[:, P:T], o_tm[:, 1, :], ident)
            last.then_inc(q["oT_ready"], 1)
        if k == 1 and on(n - 3):
            at_least(pe, q["oT_copied"], b)
            at_least(pe, q["o_ready"], n if not isinstance(n, int) or n <= UNITS else UNITS)
            for i in range(PER_IMAGE):
                last = pe.matmul(o_bank[:, OT_AT + i * C:OT_AT + (i + 1) * C], oT[:, i * P:(i + 1) * P], w_proj[:],
                                 start=True, stop=True)
            last.then_inc(q["proj_out_ready"], 1)
        if on(n):
            at_least(pe, q["probs_ready"], n + 1)
            for i in range(pairs):
                to = S[:, i // TILES3, (i % TILES3) * P:(i % TILES3 + 1) * P]
                last = pe.transpose(to, probs[:, i * P:(i + 1) * P], ident)
            last.then_inc(q["probsT_ready"], 1)

    def act_step(act, b, k):
        n = 2 * b + k
        if on(n + 1):
            at_least(act, q["v_proj_ready"], n + 2)
            at_least(act, q["setup"], SETUPS)
            at_least(act, q["pv_ready"], n)
            to = vals[(k + 1) % 2]
            src = v_bank[:, 0:vwin * C].rearrange("p (w t e) -> p w t e", w=vwin, e=2 * d)
            near, far = slice(0, vwin // 2), slice(vwin // 2, vwin)
            nc.scalar.activation(to[0:KEYS, :, :, 0:d], src[0:KEYS, :, :, 0:d], ACT.Copy)
            nc.scalar.activation(to[KEYS:P, near, :, vd:vd + d], src[KEYS:P, far, :, d:2 * d], ACT.Copy)
            last = nc.scalar.activation(to[KEYS:P, far, :, vd:vd + d], src[KEYS:P, near, :, d:2 * d], ACT.Copy)
            last.then_inc(q["v_ready"], 1)
        if on(n):
            at_least(act, q["shifted_ready"], n + 1)
            if first:
                nc.scalar.activation(probs[:].rearrange("p (g c) -> p g c", g=2), score_banks[k][:, :, 0:half],
                                     ACT.Exp, scale=1.0 / (QK_SCALE0 * QK_SCALE0)).then_inc(q["probs_ready"], 1)
            else:
                nc.scalar.activation(probs[:].rearrange("p (t g j) -> p g t j", g=2, j=KEYS),
                                     score_banks[k][:, :, 0:half].rearrange("p g (t j) -> p g t j", j=KEYS),
                                     ACT.Exp, scale=s["exp_scale1"][:, 0:1]).then_inc(q["probs_ready"], 1)
        if first and on(n + 2):
            at_least(act, q["qk_proj_ready"], n + 3)
            at_least(act, q["sumsq_ready"], n + 2)
            nc.scalar.activation(sq[:], qk_bank[:, 0:2 * C], ACT.Square).then_inc(q["squares_ready"], 1)
        if on(n + 1):
            at_least(act, q["stackT_ready"], n + 2)
            st = stackT_ps.rearrange("p (t e) -> p t e", e=P)
            kcol = 0 if first else halo + ((k + 1) % 2) * P
            nc.scalar.activation(qT[:], st[:, 0:TILES3, :], ACT.Copy)
            nc.scalar.activation(kT[:, :, kcol:kcol + P], st[:, TILES3:2 * TILES3, :],
                                 ACT.Copy).then_inc(q["qkT_ready"], 1)
        if first and on(n + 2):
            at_least(act, q["sumsq_ready"], n + 3)
            at_least(act, q["rnorm_ready"], n + 2)
            nc.scalar.activation(log_sum[:], sumsq[:], ACT.Ln).then_inc(q["log_ready"], 1)
            at_least(act, q["log_ready"], n + 3)
            nc.scalar.activation(guess[:], log_sum[:], ACT.Exp, scale=-0.5).then_inc(q["guess_ready"], 1)
        if on(n):
            at_least(act, q["probsT_ready"], n + 1)
            if first:
                nc.scalar.activation(probsT[:, 0:TILES3, :].rearrange("p t e -> p (t e)"),
                                     score_banks[k][:, 0, 0:TILES3 * P], ACT.Copy).then_inc(q["probsT_copied_a"], 1)
            else:
                nc.scalar.activation(probsT[:].rearrange("p t e -> p (t e)"),
                                     score_banks[k][:, 0, 0:TILES3 * P], ACT.Copy).then_inc(q["probsT_copied_a"], 1)

    def dve_step(v, b, k):
        n = 2 * b + k
        if on(n + 1):
            at_least(v, q["stack_ready"], n + 1)
            if first:
                at_least(v, q["rnorm_ready"], n + 2)
                v.tensor_tensor(qk[:], qk_bank[:, 0:2 * C].rearrange("p (h e) -> p h e", e=d),
                                rnorm[:, :, None].to_broadcast([P, 2 * heads, d]), ALU.mult).then_inc(q["qk_ready"], 1)
            else:
                at_least(v, q["qk_proj_ready"], n + 2)
                v.tensor_tensor(qk[:].rearrange("p (a h) e -> p a (h e)", a=2),
                                qk_bank[:, 0:2 * C].rearrange("p (a e) -> p a e", a=2),
                                s["fac1"][:, :, None].to_broadcast([P, 2, C]), ALU.mult).then_inc(q["qk_ready"], 1)
        if first and k == 0 and on(n + 2):
            at_least(v, q["v_proj_ready"], n + 2)
            v.tensor_scalar(xnT[0:C, :], s["xT_all"][:, b + 1, :], s["gn_scale"][:, bass.ds(b + 1, 1)],
                            s["gn_shift"][:, bass.ds(b + 1, 1)], ALU.mult, ALU.add).then_inc(q["xnT_ready"], 1)
        if on(n):
            at_least(v, q["scores_ready"], n + 1)
            v.tensor_reduce(negmax[:].rearrange("p (g h) -> p g h", g=2),
                            score_banks[k][:, :, 0:half].rearrange("p g (h j) -> p g h j", j=KEYS), AX.X, ALU.max,
                            negate=True).then_inc(q["negmax_ready"], 1)
        if on(n - 1):
            at_least(v, q["pv_ready"], n)
            pv = o_bank[:, 0:PV_COLS].rearrange("p (h e) -> p h e", e=vd)
            v.reciprocal(rsum[:], pv[:, :, d]).then_inc(q["rsum_ready"], 1)
            at_least(v, q["rsum_ready"], n)
            at_least(v, q["oT_ready"], b - 1 if k == 0 else b)
            v.tensor_tensor(o_tm[:, (k + 1) % 2, :].rearrange("p (h e) -> p h e", e=d), pv[:, :, 0:d],
                            rsum[:, :, None].to_broadcast([P, heads, d]), ALU.mult).then_inc(q["o_ready"], 1)
        if on(n + 2):
            if first:
                at_least(v, q["squares_ready"], n + 3)
                v.tensor_reduce(sumsq[:], sq[:].rearrange("p (h e) -> p h e", e=d), AX.X,
                                ALU.add).then_inc(q["squares_summed"], 1)
                at_least(v, q["squares_summed"], n + 3)
                v.tensor_scalar(sumsq[:], sumsq[:], 1e-24, None, ALU.max).then_inc(q["sumsq_ready"], 1)
        if not first and k == 1 and on(n + 3):
            at_least(v, q["v_proj_ready"], n + 3)
            at_least(v, q["xnT_ps"], b + 3)
            v.tensor_copy(xnT[0:C, halo:].rearrange("c (i t) -> c i t", i=PER_IMAGE),
                          score_banks[0][0:C, :, half:half + P]).then_inc(q["xnT_ready"], 1)
        if k == 1 and on(n - 3):
            at_least(v, q["proj_out_ready"], b)
            img = bass.ds(2 * (b - 1), PER_IMAGE)
            v.tensor_tensor(x_new[:], x_all[:, img, :],
                            o_bank[:, OT_AT:OT_AT + 2 * C].rearrange("p (i c) -> p i c", i=PER_IMAGE),
                            ALU.add).then_inc(q["x_ready"], 1)
            at_least(v, q["x_ready"], b)
            for i in range(PER_IMAGE):
                last = v.bn_stats(stat6[:, i, :], x_new[:, i, :])
            last.then_inc(q["bn_ready"], 1)
            v.tensor_scalar(x_all[:, img, :], x_new[:], 1.0, None, ALU.mult)
            at_least(v, q["bn_ready"], b)
            v.tensor_scalar(s["ln_half"][:, img, :], stat6[:], 1.0, None, ALU.mult).then_inc(q["stat_ready"], 1)
        if first and on(n + 2):
            at_least(v, q["guess_ready"], n + 3)
            v.scalar_tensor_tensor(newton[:], guess[:], -0.5, guess[:], ALU.mult,
                                   ALU.mult).then_inc(q["newton_step"], 1)
            v.tensor_tensor(guess_scaled[:], guess[:], s["head_scale"][:], ALU.mult)
            at_least(v, q["newton_step"], 2 * n + 5)
            v.tensor_tensor(newton[:], newton[:], sumsq[:], ALU.mult).then_inc(q["newton_step"], 1)
            at_least(v, q["newton_step"], 2 * n + 6)
            v.scalar_tensor_tensor(rnorm[:], newton[:], 1.5, guess_scaled[:], ALU.add,
                                   ALU.mult).then_inc(q["rnorm_ready"], 1)
        if first and on(n):
            at_least(v, q["probsT_ready"], n + 1)
            v.tensor_copy(probsT[:, TILES3:, :].rearrange("p t e -> p (t e)"),
                          score_banks[k][:, 1, 0:TILES3 * P]).then_inc(q["probsT_copied_b"], 1)
        if k == 0 and on(n - 1):
            at_least(v, q["oT_ready"], b)
            at_least(v, q["proj_out_ready"], b - 1)
            v.tensor_copy(oT[0:C, :], o_bank[0:C, OT_AT:OT_AT + T]).then_inc(q["oT_copied"], 1)
        if not first and k == 0 and on(n + 4):
            normalise(v, b + 2)

    def normalise(v, img):
        at_least(v, q["xnT_ps"], img)
        for i in range(PER_IMAGE):
            u = 2 * img + i
            last = v.tensor_scalar(xn_tm[:, i, :], x_all[:, u, :], s["ln_mean"][:, bass.ds(u, 1)], s["ln_rstd"][:, bass.ds(u, 1)],
                                   ALU.subtract, ALU.mult)
        last.then_inc(q["xn_ready"], 1)

    def pool_step(pool, b, k):
        n = 2 * b + k
        if on(n + 1):
            at_least(pool, q["qk_ready"], n + 2)
            at_least(pool, q["stackT_ready"], n + 1)
            nc.gpsimd.tensor_tensor(stack[:, 0:heads, 0:3 * d].rearrange("p h (e d) -> p h e d", d=d)[:, :, 0:3:2, :],
                                    qk[:, 0:heads, None, :].to_broadcast([P, heads, 2, d]),
                                    ones[:, 0:1, None, None].to_broadcast([P, heads, 2, d]), ALU.mult)
            nc.gpsimd.tensor_copy(stack[:, heads:, 0:2 * d].rearrange("p h (e d) -> p h e d", d=d),
                                  qk[:, heads:, None, :].to_broadcast([P, heads, 2, d])).then_inc(q["stack_hi"], 1)
            at_least(pool, q["stack_hi"], n + 2)
            nc.gpsimd.tensor_tensor(stack[:, 0:heads, d:2 * d], qk[:, 0:heads, :], stack[:, 0:heads, 0:d], ALU.subtract)
            nc.gpsimd.tensor_tensor(stack[:, heads:, 2 * d:3 * d], qk[:, heads:, :], stack[:, heads:, 0:d],
                                    ALU.subtract).then_inc(q["stack_ready"], 1)

    def run(eng, step):
        for n in range(-2 if first else -3, 4):
            step(eng, n // 2, n % 2)
        with eng.Fori(2, B - 2) as b:
            step(eng, b, 0)
            step(eng, b, 1)
        for n in range(UNITS - 4, UNITS + 2):
            step(eng, n // 2, n % 2)

    with nc.Block() as block:
        @block.gpsimd
        def _(pool):
            nc.gpsimd.memset(stack[:].rearrange("p h e -> p (h e)"), 0.0).then_inc(q["setup"], 1)
            for k in range(2):
                nc.gpsimd.memset(vals[k][:], 0.0).then_inc(q["setup"], 1)
            nc.gpsimd.memset(ones[:], 1.0).then_inc(q["setup"], 1)
            pool.wait_ge(q["setup"], 4)
            for k in range(2):
                for g in range(2):
                    rows = slice(g * KEYS, (g + 1) * KEYS)
                    nc.gpsimd.memset(vals[k][rows, :, :, g * vd + d:g * vd + d + 1], 1.0).then_inc(q["setup"], 1)
            pool.wait_ge(q["setup"], 8)
            if not first:
                nc.gpsimd.memset(kT[:, :, 0:halo], 0.0).then_inc(q["setup"], 1)
                pool.wait_ge(q["ln_step"], 3)
                nc.gpsimd.tensor_tensor(s["ln_rstd"][:], s["ln_var"][:], s["minus_half"][:, 0:UNITS],
                                        ALU.pow).then_inc(q["rstd_ready"], 1)
            run(pool, pool_step)

        @block.vector
        def _(v):
            if first:
                v.memset(xnT[C:P, :], 1.0)
            else:
                v.memset(xnT[:, 0:halo], 0.0)
                v.memset(xnT[C:P, halo:], 1.0)
                norm_statistics(v, s, q["ln_step"])
                v.wait_ge(q["rstd_ready"], 1)
                normalise(v, 0)
            v.memset(oT[C:P, :], 1.0)
            run(v, dve_step)

        @block.scalar
        def _(act):
            run(act, act_step)

        @block.tensor
        def _(pe):
            pe.wait_ge(q["setup"], SETUPS)
            run(pe, pe_step)


def experts(nc, sb, sem, s, out):
    HBUF = 3
    x_all, bank, score_banks = s["x_all"], s["bank"], s["score_banks"]
    ident = s["ident"]
    w1, w2, w_gate = s["w1"], s["w2"], s["w_gate"]
    xT = [sb(f"moe_xT{k}", [K1, CHUNK]) for k in range(2)]
    xn = sb("moe_xn", [P, CT, C])
    hidden = [sb(f"hidden{i}", [P, CHUNK]) for i in range(HBUF)]
    acc = [sb(f"acc{k}", [P, CT, C]) for k in range(2)]
    gates = [sb(f"gates{k}", [P, CT, EXPERTS]) for k in range(2)]
    pe_ = sb("gate_exp", [P, CT, EXPERTS])
    shifted = sb("gate_shifted", [P, CT, EXPERTS])
    gmax = sb("gate_max", [P, CT])
    above = sb("gate_above", [P, CT, EXPERTS, EXPERTS])
    tied = sb("gate_tied", [P, CT, EXPERTS, EXPERTS])
    rank = sb("gate_rank", [P, CT, EXPERTS])
    gsum = sb("gate_sum", [P, CT])
    earlier = sb("earlier", [P, EXPERTS, EXPERTS])
    b2_f = sb("b2_f", [3, EXPERTS * C])
    b2_rest = sb("b2_rest", [3, EXPERTS * C])
    b2_part = [sb(f"b2_part{i}", [3, EXPERTS * C], BF16) for i in range(3)]
    b2_sel = sb("b2_sel", [3, EXPERTS * C])
    b2_rows = sb("b2_rows", [3, EXPERTS, C], BF16)
    ones3 = sb("ones3", [3, P], BF16)
    h_bank = [score_banks[0][:, 0, :], score_banks[0][:, 1, :]]
    y_bank = [score_banks[1][:, 0, :], score_banks[1][:, 1, :]]
    x_bank, g_bank = bank[0], bank[1]
    out_v = out.rearrange("b h w c -> (b h w) c").rearrange("(u p) c -> p u c", p=P)
    a = s["a"]

    names = ("tables", "ln_step", "rstd", "ones", "b2", "xn_ready", "xT_ps", "xT_ready", "scores", "gate_step", "gate_exp",
             "gates_ready", "hidden_ps", "hidden_ready", "hidden_used", "y_ready", "y_used", "acc_ready")
    q = {n: sem("moe_" + n) for n in names}
    stored = [sem(f"moe_stored{k}") for k in range(2)]
    GSTEPS = 12

    def on(c):
        return not isinstance(c, int) or 0 <= c < CHUNKS

    def pe_inputs(pe, c, k):
        at_least(pe, q["xn_ready"], c + 1)
        for j in range(CT):
            last = pe.transpose(x_bank[0:C, j * P:(j + 1) * P], xn[:, j, :], ident)
        last.then_inc(q["xT_ps"], 1)

    def pe_gates(pe, c, k):
        at_least(pe, q["xT_ready"], c + 1)
        at_least(pe, q["gate_step"], GSTEPS * c)
        for j in range(CT):
            last = pe.matmul(g_bank[:, j * EXPERTS:(j + 1) * EXPERTS], xT[k][:, j * P:(j + 1) * P], w_gate[:],
                             start=True, stop=True)
        last.then_inc(q["scores"], 1)

    def pe_chunk(pe, c, k):
        for m in range(NH + 1):
            if m < NH:
                at_least(pe, q["hidden_ready"], NH * c + m - 1)
                pe.matmul(h_bank[m % 2], w1[:, m * P:(m + 1) * P], xT[k][:], start=True,
                          stop=True).then_inc(q["hidden_ps"], 1)
            if m == 3 and on(c + 1):
                pe_inputs(pe, c + 1, 1 - k)
            if m == 6 and on(c + 1):
                pe_gates(pe, c + 1, 1 - k)
            if m > 0:
                e, i = divmod(m - 1, HC)
                y = y_bank[e % 2][:, 0:CT * C]
                if i == 0:
                    at_least(pe, q["y_used"], EXPERTS * c + e - 1)
                    pe.matmul(y.rearrange("p (j c) -> p j c", j=CT), ones3[:],
                              b2_rows[:, e, None, :].to_broadcast([3, CT, C]), start=True, stop=False,
                              skip_group_check=True)
                at_least(pe, q["hidden_ready"], NH * c + m)
                for j in range(CT):
                    last = pe.matmul(y[:, j * C:(j + 1) * C], hidden[(m - 1) % HBUF][:, j * P:(j + 1) * P],
                                     w2[:, m - 1, :], start=False, stop=(i == HC - 1), skip_group_check=True)
                last.then_inc(q["hidden_used"], 1)

    def act_chunk(act, c, k):
        for m in range(NH):
            at_least(act, q["hidden_ps"], NH * c + m + 1)
            at_least(act, q["hidden_used"], NH * c + m + 1 - HBUF)
            nc.scalar.activation(hidden[m % HBUF][:], h_bank[m % 2], ACT.Gelu).then_inc(q["hidden_ready"], 1)
            if m == 9 and on(c + 1):
                act_gate(act, c + 1)

    def act_gate(act, c):
        at_least(act, q["gate_step"], GSTEPS * c + 2)
        nc.scalar.activation(pe_[:], shifted[:], ACT.Exp).then_inc(q["gate_exp"], 1)

    def dve_normalise(v, c):
        at_least(v, q["xT_ps"], c)
        for j in range(CT):
            u = CT * c + j
            last = v.tensor_scalar(xn[:, j, :], x_all[:, u, :], s["ln_mean"][:, bass.ds(u, 1)], s["ln_rstd"][:, bass.ds(u, 1)],
                                   ALU.subtract, ALU.mult)
        last.then_inc(q["xn_ready"], 1)

    def dve_inputs(v, c, k):
        at_least(v, q["xT_ps"], c + 1)
        at_least(v, q["hidden_ps"], NH * (c - 1))
        v.tensor_copy(xT[k][0:C, :], x_bank[0:C, :]).then_inc(q["xT_ready"], 1)

    def dve_gates(v, c, k):
        G = GSTEPS * c
        sc = g_bank[:, 0:CT * EXPERTS].rearrange("p (j e) -> p j e", e=EXPERTS)
        at_least(v, q["scores"], c + 1)
        v.tensor_reduce(gmax[:], sc, AX.X, ALU.max).then_inc(q["gate_step"], 1)
        at_least(v, q["gate_step"], G + 1)
        v.tensor_tensor(shifted[:], sc, gmax[:, :, None].to_broadcast([P, CT, EXPERTS]),
                        ALU.subtract).then_inc(q["gate_step"], 1)

    def dve_topk(v, c, k):
        G = GSTEPS * c
        at_least(v, q["gate_exp"], c + 1)
        v.tensor_reduce(gsum[:], pe_[:], AX.X, ALU.add).then_inc(q["gate_step"], 1)
        at_least(v, q["gate_step"], G + 3)
        v.reciprocal(gsum[:], gsum[:]).then_inc(q["gate_step"], 1)
        at_least(v, q["gate_step"], G + 4)
        v.tensor_tensor(pe_[:], pe_[:], gsum[:, :, None].to_broadcast([P, CT, EXPERTS]),
                        ALU.mult).then_inc(q["gate_step"], 1)
        at_least(v, q["gate_step"], G + 5)
        for j in range(CT):
            mine = pe_[:, j, :, None].to_broadcast([P, EXPERTS, EXPERTS])
            other = pe_[:, j, None, :].to_broadcast([P, EXPERTS, EXPERTS])
            v.tensor_tensor(above[:, j], other, mine, ALU.is_gt)
            last = v.tensor_tensor(tied[:, j], other, mine, ALU.is_equal)
        last.then_inc(q["gate_step"], 1)
        at_least(v, q["gate_step"], G + 6)
        v.tensor_tensor(tied[:], tied[:], earlier[:, None].to_broadcast([P, CT, EXPERTS, EXPERTS]),
                        ALU.mult).then_inc(q["gate_step"], 1)
        at_least(v, q["gate_step"], G + 7)
        v.tensor_tensor(above[:], above[:], tied[:], ALU.add).then_inc(q["gate_step"], 1)
        at_least(v, q["gate_step"], G + 8)
        v.tensor_reduce(rank[:], above[:], AX.X, ALU.add).then_inc(q["gate_step"], 1)
        at_least(v, q["gate_step"], G + 9)
        v.scalar_tensor_tensor(pe_[:], rank[:], float(TOP), pe_[:], ALU.is_lt, ALU.mult).then_inc(q["gate_step"], 1)
        at_least(v, q["gate_step"], G + 10)
        v.tensor_reduce(gsum[:], pe_[:], AX.X, ALU.add).then_inc(q["gate_step"], 1)
        at_least(v, q["gate_step"], G + 11)
        v.tensor_scalar(gsum[:], gsum[:], 1e-9, None, ALU.add).then_inc(q["gate_step"], 1)
        at_least(v, q["gate_step"], G + 12)
        v.reciprocal(gmax[:], gsum[:]).then_inc(q["gates_ready"], 1)
        at_least(v, q["gates_ready"], 2 * c + 1)
        v.tensor_tensor(gates[k][:], pe_[:], gmax[:, :, None].to_broadcast([P, CT, EXPERTS]),
                        ALU.mult).then_inc(q["gates_ready"], 1)

    def dve_chunk(v, c, k):
        for e in range(EXPERTS):
            if e == 1 and on(c + 1):
                dve_inputs(v, c + 1, 1 - k)
            if e == 2 and on(c + 1):
                dve_gates(v, c + 1, 1 - k)
                if on(c + 2):
                    dve_normalise(v, c + 2)
            at_least(v, q["hidden_used"], NH * c + HC * (e + 1))
            at_least(v, q["gates_ready"], 2 * (c + 1))
            if e == 0:
                at_least(v, stored[k], 16 * ((c - k) // 2))
            for j in range(CT):
                onto = x_all[:, CT * c + j, :] if e == 0 else acc[k][:, j, :]
                if e > 0 and j == 0:
                    at_least(v, q["y_used"], EXPERTS * c + e)
                last = v.scalar_tensor_tensor(acc[k][:, j, :], y_bank[e % 2][:, j * C:(j + 1) * C],
                                              gates[k][:, j, e:e + 1], onto, ALU.mult, ALU.add)
            last.then_inc(q["y_used"], 1)
        if on(c + 1):
            dve_topk(v, c + 1, 1 - k)

    with nc.Block() as block:
        @block.gpsimd
        def _(pool):
            pool.wait_ge(q["ln_step"], 3)
            nc.gpsimd.tensor_tensor(s["ln_rstd"][:], s["ln_var"][:], s["minus_half"][:, 0:UNITS],
                                    ALU.pow).then_inc(q["rstd"], 1)

        @block.sync
        def _(sp):
            sp.dma_start(earlier[:], a["earlier"].partition_broadcast(P)).then_inc(q["tables"], 16)
            sp.dma_start(b2_f[:], a["b2"].partition_broadcast(3)).then_inc(q["tables"], 16)
            with sp.Fori(0, CHUNKS // 2) as cc:
                for k in range(2):
                    c = 2 * cc + k
                    sp.wait_ge(q["y_used"], EXPERTS * (c + 1))
                    sp.dma_start(out_v[:, bass.ds(CT * c, CT), :], acc[k][:]).then_inc(stored[k], 16)
            for k in range(2):
                sp.wait_ge(stored[k], 16 * (CHUNKS // 2))

        @block.vector
        def _(v):
            for k in range(2):
                v.memset(xT[k][C:K1, :], 1.0)
            v.memset(ones3[:], 1.0)
            norm_statistics(v, s, q["ln_step"])
            v.wait_ge(q["rstd"], 1)
            dve_normalise(v, 0)
            v.wait_ge(q["tables"], 32)
            v.tensor_copy(b2_part[0][:], b2_f[:]).then_inc(q["b2"], 1)
            for i in range(2):
                v.wait_ge(q["b2"], 2 * i + 1)
                v.tensor_tensor(b2_rest[:], b2_f[:] if i == 0 else b2_rest[:], b2_part[i][:],
                                ALU.subtract).then_inc(q["b2"], 1)
                v.wait_ge(q["b2"], 2 * i + 2)
                v.tensor_copy(b2_part[i + 1][:], b2_rest[:]).then_inc(q["b2"], 1)
            v.wait_ge(q["b2"], 5)
            v.tensor_scalar(b2_sel[:], b2_part[0][:], ident[0:3, 0:1], None, ALU.mult).then_inc(q["b2"], 1)
            v.wait_ge(q["b2"], 6)
            v.scalar_tensor_tensor(b2_sel[:], b2_part[1][:], ident[0:3, 1:2], b2_sel[:], ALU.mult,
                                   ALU.add).then_inc(q["b2"], 1)
            v.wait_ge(q["b2"], 7)
            v.scalar_tensor_tensor(b2_rows[:].rearrange("p e c -> p (e c)"), b2_part[2][:], ident[0:3, 2:3], b2_sel[:],
                                   ALU.mult, ALU.add).then_inc(q["b2"], 1)
            dve_inputs(v, 0, 0)
            dve_gates(v, 0, 0)
            dve_normalise(v, 1)
            dve_topk(v, 0, 0)
            dve_chunk(v, 0, 0)
            dve_chunk(v, 1, 1)
            with v.Fori(1, CHUNKS // 2 - 1) as cc:
                dve_chunk(v, 2 * cc, 0)
                dve_chunk(v, 2 * cc + 1, 1)
            dve_chunk(v, CHUNKS - 2, 0)
            dve_chunk(v, CHUNKS - 1, 1)

        @block.scalar
        def _(act):
            act_gate(act, 0)
            act_chunk(act, 0, 0)
            act_chunk(act, 1, 1)
            with act.Fori(1, CHUNKS // 2 - 1) as cc:
                act_chunk(act, 2 * cc, 0)
                act_chunk(act, 2 * cc + 1, 1)
            act_chunk(act, CHUNKS - 2, 0)
            act_chunk(act, CHUNKS - 1, 1)

        @block.tensor
        def _(pe):
            pe_inputs(pe, 0, 0)
            pe_gates(pe, 0, 0)
            pe.wait_ge(q["b2"], 8)
            pe_chunk(pe, 0, 0)
            pe_chunk(pe, 1, 1)
            with pe.Fori(1, CHUNKS // 2 - 1) as cc:
                pe_chunk(pe, 2 * cc, 0)
                pe_chunk(pe, 2 * cc + 1, 1)
            pe_chunk(pe, CHUNKS - 2, 0)
            pe_chunk(pe, CHUNKS - 1, 1)


def shape_constants():
    i = np.arange(P)
    perms = np.zeros((P, 5, P), np.float32)
    perms[i, 0, i] = 1
    row, col = i // HW, i % HW
    for tile in range(PER_IMAGE):
        r, c = (tile * WIN + row - SHIFT) % HW, (col - SHIFT) % HW
        perms[i, 1 + tile, r // WIN * KEYS + c // WIN * (KEYS // 2) + r % SHIFT * WIN + c % WIN] = 1
    w, r, c = i // KEYS, i % KEYS // WIN, i % WIN
    wcol = (w * WIN + c + SHIFT) % HW
    perms[i, 3, r * HW + wcol] = 1
    perms[i, 4, (r + SHIFT) % WIN * HW + wcol] = 1
    ch = np.arange(-(WIN - 1), WIN, dtype=np.float32)
    tab = np.stack(np.meshgrid(ch, ch, indexing="ij"), -1) / np.float32(WIN - 1) * np.float32(8)
    tab = np.sign(tab) * np.log2(np.abs(tab) + np.float32(1)) / np.float32(3)
    tab = tab[::-1, ::-1].reshape(-1, 2).astype(np.float32)
    rel = np.concatenate([tab.T, np.ones((1, tab.shape[0]), np.float32)])
    region = np.zeros((HW, HW), np.int64)
    cuts = (slice(0, HW - WIN), slice(HW - WIN, HW - SHIFT), slice(HW - SHIFT, HW))
    for m, hs in enumerate(cuts):
        for n, ws in enumerate(cuts):
            region[hs, ws] = 3 * m + n
    win = region.reshape(2, WIN, 2, WIN).transpose(0, 2, 1, 3).reshape(2, 2, KEYS)
    wmask = np.where(win[:, :, :, None] != win[:, :, None, :], -100.0, 0.0).astype(np.float32)
    wmask = wmask.reshape(2, P, KEYS).transpose(1, 0, 2)
    back = (QBLOCK + i % QBLOCK)[:, None] - np.arange(KEYS)[None]
    seen = (back >= 0) & (back <= BAND)
    seen = np.stack([seen & ~((i < QBLOCK)[:, None] & (np.arange(KEYS) < QBLOCK)[None]), seen], 1)
    bmask = np.where(seen, 0.0, MASKED).astype(np.float32)
    group = np.arange(C) // (C // GROUPS)
    gavg = (group[:, None] == group[None]).astype(np.float32) / np.float32(2 * C // GROUPS)
    earlier = (np.arange(EXPERTS)[None] < np.arange(EXPERTS)[:, None]).astype(np.float32)
    return {"permutations": perms, "rel_table": rel, "win_mask": wmask, "band_mask": bmask, "group_avg": gavg,
            "earlier": earlier}


def kernel(x, L0_conv_qkv_w, L0_conv_qkv_b, L0_conv_proj_w, L0_conv_proj_b, L0_conv_logit_scale, L0_conv_cpb_w1,
           L0_conv_cpb_b1, L0_conv_cpb_w2, L1_attn_qkv_w, L1_attn_qkv_b, L1_attn_proj_w, L1_attn_proj_b, L1_attn_gate,
           L1_ffn_gate_w, L1_ffn_gate_b, L1_ffn_w1, L1_ffn_b1, L1_ffn_w2, L1_ffn_b2):
    import concourse.bacc as bacc
    from concourse.bass_utils import run_bass_kernel_spmd

    cat = np.concatenate
    order = [4 * t + 2 * g + r for g in range(2) for t in range(TILES3) for r in range(2)]
    b0 = np.array(L0_conv_qkv_b)
    b0 = cat([b0[:C], np.zeros(C, np.float32), b0[2 * C:]])
    arrays = {
        "x": np.array(x),
        "w_qkv0": cat([np.array(L0_conv_qkv_w).T, b0[None]]),
        "w_proj0": cat([np.array(L0_conv_proj_w).T, np.array(L0_conv_proj_b)[None]]),
        "w_qkv1": cat([np.array(L1_attn_qkv_w), np.array(L1_attn_qkv_b)[None]]),
        "w_proj1": cat([np.array(L1_attn_proj_w), np.array(L1_attn_proj_b)[None]]),
        "gate_vec": np.array(L1_attn_gate)[:, None],
        "logit_scale": np.array(L0_conv_logit_scale).reshape(HEADS0),
        "cpb_w1": cat([np.array(L0_conv_cpb_w1).T, np.array(L0_conv_cpb_b1)[None]]),
        "cpb_w2": np.array(L0_conv_cpb_w2).T[:, order],
        "w1": cat([np.array(L1_ffn_w1).transpose(1, 0, 2).reshape(C, EXPERTS * HID),
                   np.array(L1_ffn_b1).reshape(1, EXPERTS * HID)]),
        "w2": np.array(L1_ffn_w2).reshape(NH, P, C).transpose(1, 0, 2),
        "b2": np.array(L1_ffn_b2).reshape(EXPERTS * C),
        "w_gate": cat([np.array(L1_ffn_gate_w), np.array(L1_ffn_gate_b)[None]]),
    }
    arrays.update(shape_constants())
    nc = bacc.Bacc("TRN2", target_bir_lowering=False, num_devices=1)
    feed, dram = {}, {}
    for name, value in arrays.items():
        feed["in_" + name] = np.ascontiguousarray(value)
        dram[name] = nc.dram_tensor("in_" + name, value.shape, mybir.dt.from_np(value.dtype), kind="ExternalInput").ap()
    out = nc.dram_tensor("out_0", (B, HW, HW, C), F32, kind="ExternalOutput").ap()
    build(nc, dram, out)
    result = run_bass_kernel_spmd(nc, [feed], core_ids=[0])
    return result.results[0]["out_0"]
```

```python
from contextlib import ExitStack

import numpy as np

import concourse.bass as bass
from concourse import mybir

F32 = mybir.dt.float32
F16 = mybir.dt.float16
BF16 = mybir.dt.bfloat16
F32R = mybir.dt.float32r
ALU = mybir.AluOpType
ACT = mybir.ActivationFunctionType
AX = mybir.AxisListType

B, HW, C = 16, 16, 96
T = HW * HW
P = 128
UNITS = B * T // P
PER_IMAGE = T // P
K1 = C + 1

WIN, SHIFT = 8, 4
KEYS = 64
BAND = 16
QBLOCK = 32
NQB = P // QBLOCK
GROUPS = 32
GN_EPS, LN_EPS = 1e-5, 1e-5

HEADS0, D0 = 12, C // 12
HEADS1, D1 = 6, C // 6
PAIRS0, PAIRS1 = HEADS0 // 2, HEADS1 // 2
SLOT0, SLOT1 = 32, 64
TILES3 = 3
QK_SCALE0 = 64.0
QK_RANGE1 = 1024.0
MASKED = -1e30

EXPERTS, TOP, HID = 4, 2, 384
CHUNK = 512
CHUNKS = B * T // CHUNK
CT = CHUNK // P
HC = HID // P
NH = EXPERTS * HC


def build(nc, a, out):
    ctx = ExitStack()
    with ctx:
        def sb(name, shape, dt=F32):
            return ctx.enter_context(nc.sbuf_tensor(name, shape, dt))

        def sem(name):
            return ctx.enter_context(nc.semaphore(name))

        perm = sb("perm", [P, 5, P])
        ident = perm[:, 0, :]
        ident_bf = sb("ident_bf", [P, P], BF16)
        ident_h = sb("ident_h", [P, P], F16)
        ident_scaled = sb("ident_scaled", [P, P], F16)
        group_avg = sb("group_avg", [C, C])
        w_qkv = [sb("w_qkv0", [P, 3 * C]), sb("w_qkv1", [P, 3 * C])]
        w_proj = [sb("w_proj0", [P, C]), sb("w_proj1", [P, C])]
        gate_vec = sb("gate_vec", [C, 1])
        w1 = sb("w1", [K1, EXPERTS * HID])
        w2 = sb("w2", [P, NH, C])
        w_gate = sb("w_gate", [K1, EXPERTS])
        b2_f = sb("b2_f", [2, EXPERTS * C])
        w1_hi, w1_lo = (sb("w1_" + n, [K1, EXPERTS * HID], F32R) for n in ("hi", "lo"))
        b2_hi, b2_lo = (sb("b2_" + n, [2, EXPERTS * C], F32R) for n in ("hi", "lo"))
        b2_rows = sb("b2_rows", [2, EXPERTS, C], F32R)
        ones2 = sb("ones2", [2, P], F32R)
        moe_hi, moe_lo = (sb("moe_" + n, [K1, CHUNKS, CHUNK], F32R) for n in ("hi", "lo"))
        earlier = sb("earlier", [P, EXPERTS, EXPERTS])
        bias_bf = sb("bias_bf", [P, 2, 768], F16)
        bias_lo = sb("bias_lo", [P, 2, 768], F16)
        band_f = sb("band_f", [P, 2, KEYS])
        band = sb("band", [P, 2, KEYS], BF16)
        head_scale = sb("head_scale", [P, 2 * HEADS0])
        minus_half = sb("minus_half", [P, 32])
        fac1 = sb("fac1", [P, 2])
        exp_scale1 = sb("exp_scale1", [P, 1])
        x_all = sb("x_all", [P, UNITS, C])
        xT_all = sb("xT_all", [C, B, T])
        gn_scale = sb("gn_scale", [C, B])
        gn_shift = sb("gn_shift", [C, B])
        ln_half = sb("ln_half", [P, UNITS, 6])
        ln_sum = sb("ln_sum", [P, UNITS])
        ln_dif = sb("ln_dif", [P, UNITS])
        ln_mean = sb("ln_mean", [P, UNITS])
        ln_var = sb("ln_var", [P, UNITS])
        ln_rstd = sb("ln_rstd", [P, UNITS])
        ln_log = sb("ln_log", [P, UNITS])
        ln_guess = sb("ln_guess", [P, UNITS])
        ln_newton = sb("ln_newton", [P, UNITS])

        bank = [ctx.enter_context(nc.psum_tensor(f"bank{i}", [P, 512], F32)) for i in range(4)]
        score_banks = [ctx.enter_context(nc.psum_tensor(f"score_banks{i}", [P, 2, 512], F32)) for i in range(2)]

        w1_loaded, experts_loaded = sem("w1_loaded"), sem("experts_loaded")
        buffers = [attention_buffers(sb, layer) for layer in range(2)]
        s = locals()
        loads_and_tables(nc, sb, sem, a, s)
        attention(nc, sb, sem, s, 0)
        attention(nc, sb, sem, s, 1)
        experts(nc, sb, sem, s, out)


def attention_shape(layer):
    if layer == 0:
        return HEADS0, D0, PAIRS0, SLOT0, P // KEYS, 0
    return HEADS1, D1, PAIRS1, SLOT1, NQB, QBLOCK


def attention_buffers(sb, layer):
    heads, d, pairs, slot, vwin, halo = attention_shape(layer)
    L = f"{layer}"
    return {
        "xnT": sb("xnT" + L, [P, halo + T]),
        "stack": sb("stack" + L, [P, 2 * heads, slot], F16),
        "kT": sb("kT" + L, [P, TILES3, halo + (P if layer == 0 else T)], F16),
        "vals": [sb(f"vals{k}_{L}", [P, vwin, pairs, 2 * (d + 1)]) for k in range(2)],
        "ones": sb("ones" + L, [P, 1]),
        "oT": sb("oT" + L, [P, T]),
    }


def set_once_pool(pool, nc, bufs, layer, done):
    heads, d, pairs, slot, vwin, halo = attention_shape(layer)
    vd = d + 1
    stack, vals = bufs["stack"], bufs["vals"]
    start = 8 * layer
    nc.gpsimd.memset(stack[:].rearrange("p h e -> p (h e)"), 0.0).then_inc(done, 1)
    for k in range(2):
        nc.gpsimd.memset(vals[k][:], 0.0).then_inc(done, 1)
    nc.gpsimd.memset(bufs["ones"][:], 1.0).then_inc(done, 1)
    pool.wait_ge(done, start + 4)
    for k in range(2):
        for g in range(2):
            rows = slice(g * KEYS, (g + 1) * KEYS)
            nc.gpsimd.memset(vals[k][rows, :, :, g * vd + d:g * vd + d + 1], 1.0).then_inc(done, 1)
    pool.wait_ge(done, start + 8)
    if halo:
        nc.gpsimd.memset(bufs["kT"][:, :, 0:halo], 0.0).then_inc(done, 1)


def set_once_vector(v, bufs, layer):
    halo = attention_shape(layer)[-1]
    if halo:
        v.memset(bufs["xnT"][:, 0:halo], 0.0)
    v.memset(bufs["xnT"][C:P, halo:], 1.0)
    v.memset(bufs["oT"][C:P, :], 1.0)


def first_guess(act, nc, value, log, guess, ready, logged, guessed):
    act.wait_ge(*ready)
    nc.scalar.activation(log, value, ACT.Ln).then_inc(logged, 1)
    act.wait_ge(logged, 1)
    nc.scalar.activation(guess, log, ACT.Exp, scale=-0.5).then_inc(guessed, 1)


def newton_root(v, out, value, guess, tmp, guessed, step):
    v.wait_ge(guessed, 1)
    v.scalar_tensor_tensor(tmp, guess, -0.5, guess, ALU.mult, ALU.mult).then_inc(step, 1)
    v.wait_ge(step, 1)
    v.tensor_tensor(tmp, tmp, value, ALU.mult).then_inc(step, 1)
    v.wait_ge(step, 2)
    v.scalar_tensor_tensor(out, tmp, 1.5, guess, ALU.add, ALU.mult).then_inc(step, 1)
    v.wait_ge(step, 3)


def loads_and_tables(nc, sb, sem, a, s):
    x_all, xT_all, perm, bank, score_banks = s["x_all"], s["xT_all"], s["perm"], s["bank"], s["score_banks"]
    group_avg, gn_scale, gn_shift = s["group_avg"], s["gn_scale"], s["gn_shift"]
    minus_half, head_scale = s["minus_half"], s["head_scale"]
    ident = perm[:, 0, :]
    NREL = (2 * WIN - 1) ** 2
    stats = sb("gn_stats", [C, B, 6])
    gn_sum = sb("gn_sum", [C, 2, B])
    gn_sq = sb("gn_sq", [C, B, 2])
    gn_e2 = sb("gn_e2", [C, B, 2])
    gn_mean = sb("gn_mean", [C, 2, B])
    gn_var = sb("gn_var", [C, B])
    rel_table = sb("rel_table", [3, NREL])
    cpb_w1 = sb("cpb_w1", [3, P])
    cpb_w2 = sb("cpb_w2", [P, HEADS0])
    cpb_h = sb("cpb_h", [P, NREL])
    cpb_e = sb("cpb_e", [HEADS0, NREL])
    cpb_t = sb("cpb_t", [HEADS0, NREL])
    bias_f = sb("bias_f", [P, HEADS0, KEYS])
    win_mask = sb("win_mask", [P, 2, KEYS])
    bias_sum = sb("bias_sum", [P, 2, HEADS0 * KEYS])
    logit = sb("logit", [P, HEADS0])

    rel_dram = nc.dram_tensor("rel_scratch", (HEADS0, NREL), F32)
    col_dram = nc.dram_tensor("col_scratch", (WIN, HEADS0, 2 * WIN - 1, WIN), F32)

    x_loaded = [sem(f"x_loaded{i}") for i in range(4)]
    perm_loaded = sem("perm_loaded")
    table_loaded, mask_loaded = sem("table_loaded"), sem("mask_loaded")
    weights_loaded = sem("weights_loaded")
    xT_ready, xT_copied, stats_ready = sem("xT_ready"), sem("xT_copied"), sem("gn_stats_ready")
    gn_step, gn_group, gn_sums = sem("gn_step"), sem("gn_group"), sem("gn_sums")
    cpb_mm, cpb_relu, cpb_exp, cpb_table, table_step = (sem("cpb_mm"), sem("cpb_relu"), sem("cpb_exp"),
                                                        sem("cpb_table"), sem("table_step"))
    rel_stored, col_stored, bias_loaded = sem("rel_stored"), sem("col_stored"), sem("bias_loaded")
    half_set, weights_padded = sem("half_set"), sem("weights_padded")
    set_once, group_loaded, w_qkv1_loaded, w_proj1_loaded = (sem("set_once"), sem("group_loaded"),
                                                             sem("w_qkv1_loaded"), sem("w_proj1_loaded"))
    bias_summed, bias_rounded = sem("bias_summed"), sem("bias_rounded")
    gn_logged, gn_guessed, gn_newton_step = sem("gn_logged"), sem("gn_guessed"), sem("gn_newton_step")
    wsq = sb("wsq", [K1, 2 * C])
    ones97 = sb("ones97", [K1, P])
    wmax = sb("wmax", [P, 2])
    sprod = sb("sprod", [P, 1])
    gn_log = sb("gn_log", [C, B])
    gn_guess = sb("gn_guess", [C, B])
    gn_tmp = sb("gn_tmp", [C, B])
    fac1, exp_scale1, w_qkv1 = s["fac1"], s["exp_scale1"], s["w_qkv"][1]
    wsq_ready, wsums_ready, wscale_step, wscale_pow = (sem("wsq_ready"), sem("wsums_ready"), sem("wscale_step"),
                                                       sem("wscale_pow"))
    scale_step = sem("scale_step")
    side = 2 * WIN - 1

    def store_columns(eng, which):
        eng.wait_ge(rel_stored, 16)
        rel = rel_dram.ap().rearrange("h (r c) -> h r c", r=side)
        for ci in which:
            eng.dma_start(col_dram.ap()[ci], rel[:, :, WIN - 1 - ci:2 * WIN - 1 - ci]).then_inc(col_stored, 16)

    def load_bias(eng, half):
        eng.wait_ge(col_stored, 16 * WIN)
        cols = col_dram.ap().rearrange("i h r c -> i h (r c)")
        for ri in range(WIN):
            at = half * KEYS + ri * WIN
            eng.dma_start(bias_f[at:at + WIN, :, :],
                          cols[:, :, (WIN - 1 - ri) * WIN:(2 * WIN - 1 - ri) * WIN]).then_inc(bias_loaded, 16)

    with nc.Block() as block:
        @block.sync
        def _(sp):
            sp.dma_start(perm[:], a["permutations"]).then_inc(perm_loaded, 16)
            xv = a["x"].rearrange("b h w c -> (b h w) c").rearrange("(u p) c -> p u c", p=P)
            for i in range(4):
                part = slice(i * UNITS // 4, (i + 1) * UNITS // 4)
                sp.dma_start(x_all[:, part, :], xv[:, part, :]).then_inc(x_loaded[i], 16)
            sp.wait_ge(weights_padded, 4)
            sp.dma_start(s["w_qkv"][1][0:K1, :], a["w_qkv1"]).then_inc(w_qkv1_loaded, 16)
            sp.dma_start(s["w_qkv"][0][0:K1, :], a["w_qkv0"]).then_inc(weights_loaded, 16)
            sp.dma_start(s["w_proj"][0][0:K1, :], a["w_proj0"]).then_inc(weights_loaded, 16)
            sp.dma_start(s["w_proj"][1][0:K1, :], a["w_proj1"]).then_inc(w_proj1_loaded, 16)
            sp.dma_start(s["gate_vec"][:], a["gate_vec"]).then_inc(w_proj1_loaded, 16)
            store_columns(sp, range(0, WIN // 2))
            load_bias(sp, 0)
            sp.dma_start(s["w1"][:], a["w1"]).then_inc(s["w1_loaded"], 16)
            sp.dma_start(s["w2"][:], a["w2"]).then_inc(s["experts_loaded"], 16)
            sp.dma_start(s["w_gate"][:], a["w_gate"]).then_inc(s["experts_loaded"], 16)
            sp.dma_start(s["b2_f"][:], a["b2"].partition_broadcast(2)).then_inc(s["experts_loaded"], 16)
            sp.dma_start(s["earlier"][:], a["earlier"].partition_broadcast(P)).then_inc(s["experts_loaded"], 16)
            sp.wait_ge(weights_loaded, 16 * 2)

        @block.gpsimd
        def _(pool):
            nc.gpsimd.memset(minus_half[:], -0.5).then_inc(half_set, 1)
            pool.dma_start(logit[:], a["logit_scale"].partition_broadcast(P)).then_inc(mask_loaded, 16)
            pool.dma_start(win_mask[:], a["win_mask"]).then_inc(mask_loaded, 16)
            pool.dma_start(s["band_f"][:], a["band_mask"]).then_inc(mask_loaded, 16)
            pool.wait_ge(half_set, 1)
            for layer in range(2):
                set_once_pool(pool, nc, s["buffers"][layer], layer, set_once)
            pool.wait_ge(set_once, 17)
            nc.gpsimd.memset(s["moe_hi"][C:K1, :, :].bitcast(F32), 1.0).then_inc(set_once, 1)
            nc.gpsimd.memset(s["moe_lo"][C:K1, :, :].bitcast(F32), 0.0).then_inc(set_once, 1)
            pool.wait_ge(set_once, 19)
            pool.wait_ge(wscale_step, 2)
            nc.gpsimd.tensor_tensor(fac1[:], wmax[:], minus_half[:, 0:2], ALU.pow).then_inc(wscale_pow, 1)
            pool.wait_ge(mask_loaded, 16 * 3)

        @block.scalar
        def _(act):
            act.dma_start(cpb_w1[:], a["cpb_w1"]).then_inc(table_loaded, 16)
            act.dma_start(rel_table[:], a["rel_table"]).then_inc(table_loaded, 16)
            act.dma_start(cpb_w2[:], a["cpb_w2"]).then_inc(table_loaded, 16)
            act.dma_start(group_avg[:], a["group_avg"]).then_inc(group_loaded, 16)
            act.preload_act_table_set("natural_log_exp_and_others")
            act.wait_ge(cpb_mm, 1)
            nc.scalar.activation(cpb_h[:], bank[3][:, 0:NREL], ACT.Relu).then_inc(cpb_relu, 1)
            act.wait_ge(cpb_mm, 2)
            nc.scalar.activation(cpb_e[:], bank[3][0:HEADS0, 256:256 + NREL], ACT.Exp, scale=-1.0).then_inc(cpb_exp, 1)
            act.wait_ge(cpb_table, 1)
            act.dma_start(rel_dram.ap(), cpb_t[:]).then_inc(rel_stored, 16)
            store_columns(act, range(WIN // 2, WIN))
            load_bias(act, 1)
            act.wait_ge(scale_step, 1)
            nc.scalar.activation(logit[:], logit[:], ACT.Exp).then_inc(scale_step, 1)
            first_guess(act, nc, gn_var[:], gn_log[:], gn_guess[:], (gn_step, 6), gn_logged, gn_guessed)
            for wh in range(2):
                act.wait_ge(bias_summed, wh + 1)
                nc.scalar.activation(s["bias_bf"][:, wh, :], bias_sum[:, wh, :], ACT.Copy).then_inc(bias_rounded, 1)

        @block.tensor
        def _(pe):
            pe.wait_ge(table_loaded, 16 * 3)
            nc.tensor.matmul(bank[3][:, 0:NREL], cpb_w1[:], rel_table[:], start=True, stop=True).then_inc(cpb_mm, 1)
            pe.wait_ge(cpb_relu, 1)
            nc.tensor.matmul(bank[3][0:HEADS0, 256:256 + NREL], cpb_w2[:], cpb_h[:], start=True,
                             stop=True).then_inc(cpb_mm, 1)
            pe.wait_ge(perm_loaded, 16)
            for b in range(B):
                pe.wait_ge(x_loaded[b // 4], 16)
                if b >= 2:
                    pe.wait_ge(xT_copied, b - 1)
                    pe.wait_ge(stats_ready, b - 1)
                h32 = KEYS // 2
                for tile, (start, width) in enumerate(((0, 5), (h32, 3))):
                    places = bank[b % 2][0:C, start:start + 2 * width * h32].rearrange(
                        "c (w a t) -> c w a t", a=width, t=h32)[:, :, 0:3:2, :]
                    last = pe.transpose(places, x_all[:, 2 * b + tile, :], perm[:, 1 + tile, :])
                last.then_inc(xT_ready, 1)
            pe.wait_ge(gn_sums, 1)
            pe.wait_ge(group_loaded, 16)
            nc.tensor.matmul(bank[2][0:C, 0:2 * B], group_avg[:], gn_sum[:].rearrange("c a b -> c (a b)"),
                             start=True, stop=True).then_inc(gn_group, 1)
            pe.wait_ge(wsq_ready, 1)
            nc.tensor.matmul(score_banks[0][:, 0, 0:2 * C], ones97[:], wsq[:], start=True, stop=True).then_inc(wsums_ready, 1)

        @block.vector
        def _(v):
            for w in (*s["w_qkv"], *s["w_proj"]):
                v.memset(w[C:P, :], 0.0).then_inc(weights_padded, 1)
            v.memset(ones97[:], 1.0)
            v.memset(s["ones2"][:].bitcast(F32), 1.0)
            for layer in range(2):
                set_once_vector(v, s["buffers"][layer], layer)
            v.wait_ge(cpb_exp, 1)
            v.tensor_scalar(cpb_e[:], cpb_e[:], 1.0, None, ALU.add).then_inc(table_step, 1)
            v.wait_ge(table_step, 1)
            v.reciprocal(cpb_t[:], cpb_e[:]).then_inc(table_step, 1)
            v.wait_ge(table_step, 2)
            v.tensor_scalar(cpb_t[:], cpb_t[:], 16.0, None, ALU.mult).then_inc(cpb_table, 1)
            for b in range(B):
                v.wait_ge(xT_ready, b + 1)
                nc.vector.tensor_copy(xT_all[:, b, :], bank[b % 2][0:C, 0:T]).then_inc(xT_copied, 1)
                nc.vector.bn_stats(stats[:, b, :], bank[b % 2][0:C, 0:T]).then_inc(stats_ready, 1)
            v.wait_ge(stats_ready, B)
            st = stats[:].rearrange("c b (e k) -> c b e k", k=3)
            v.tensor_tensor(gn_sq[:], st[:, :, :, 1], st[:, :, :, 1], ALU.mult).then_inc(gn_step, 1)
            v.wait_ge(gn_step, 1)
            v.scalar_tensor_tensor(gn_e2[:], st[:, :, :, 2], 2.0 / T, gn_sq[:], ALU.mult, ALU.add).then_inc(gn_step, 1)
            v.wait_ge(gn_step, 2)
            v.tensor_tensor(gn_sum[:, 0, :], st[:, :, 0, 1], st[:, :, 1, 1], ALU.add)
            v.tensor_tensor(gn_sum[:, 1, :], gn_e2[:, :, 0], gn_e2[:, :, 1], ALU.add).then_inc(gn_sums, 1)
            v.wait_ge(gn_group, 1)
            v.tensor_copy(gn_mean[:].rearrange("c a b -> c (a b)"), bank[2][0:C, 0:2 * B]).then_inc(gn_step, 1)
            v.wait_ge(gn_step, 3)
            v.tensor_tensor(gn_var[:], gn_mean[:, 0, :], gn_mean[:, 0, :], ALU.mult).then_inc(gn_step, 1)
            v.wait_ge(gn_step, 4)
            v.tensor_tensor(gn_var[:], gn_mean[:, 1, :], gn_var[:], ALU.subtract).then_inc(gn_step, 1)
            v.wait_ge(gn_step, 5)
            v.tensor_scalar(gn_var[:], gn_var[:], GN_EPS, None, ALU.add).then_inc(gn_step, 1)
            v.tensor_copy(s["ident_bf"][:], ident)
            v.tensor_copy(s["ident_h"][:], ident)
            v.tensor_scalar(s["ident_scaled"][:], ident, QK_SCALE0 * QK_SCALE0, None, ALU.mult)
            v.wait_ge(mask_loaded, 16 * 3)
            v.tensor_copy(s["band"][:], s["band_f"][:])
            v.tensor_scalar(logit[:], logit[:], float(np.log(100.0)), None, ALU.min).then_inc(scale_step, 1)
            v.wait_ge(w_qkv1_loaded, 16)
            v.tensor_tensor(wsq[:], w_qkv1[0:K1, 0:2 * C], w_qkv1[0:K1, 0:2 * C], ALU.mult).then_inc(wsq_ready, 1)
            v.wait_ge(w_proj1_loaded, 32)
            v.tensor_scalar(s["w_proj"][1][0:C, :], s["w_proj"][1][0:C, :], s["gate_vec"][:, 0:1], None, ALU.mult)
            v.wait_ge(wsums_ready, 1)
            v.tensor_reduce(wmax[:], score_banks[0][:, 0, 0:2 * C].rearrange("p (a c) -> p a c", a=2), AX.X,
                            ALU.max).then_inc(wscale_step, 1)
            v.wait_ge(wscale_step, 1)
            v.tensor_scalar(wmax[:], wmax[:], float(K1), 1e-30, ALU.mult, ALU.max).then_inc(wscale_step, 1)
            v.wait_ge(bias_loaded, 16 * 2 * WIN)
            for wh in range(2):
                v.tensor_tensor(bias_sum[:, wh, :].rearrange("p (h j) -> p h j", h=HEADS0), bias_f[:],
                                win_mask[:, wh, None, :].to_broadcast([P, HEADS0, KEYS]), ALU.add).then_inc(bias_summed, 1)
            v.wait_ge(scale_step, 2)
            v.memset(head_scale[:, HEADS0:], QK_SCALE0)
            v.tensor_scalar(head_scale[:, 0:HEADS0], logit[:], QK_SCALE0, None, ALU.mult)
            newton_root(v, gn_scale[:], gn_var[:], gn_guess[:], gn_tmp[:], gn_guessed, gn_newton_step)
            v.scalar_tensor_tensor(gn_shift[:], gn_mean[:, 0, :], -1.0, gn_scale[:], ALU.mult, ALU.mult)
            for wh in range(2):
                v.wait_ge(bias_rounded, wh + 1)
                v.tensor_tensor(s["bias_lo"][:, wh, :], bias_sum[:, wh, :], s["bias_bf"][:, wh, :], ALU.subtract)
            v.wait_ge(wscale_pow, 1)
            v.tensor_scalar(fac1[:], fac1[:], QK_RANGE1, None, ALU.mult).then_inc(wscale_step, 1)
            v.wait_ge(wscale_step, 3)
            v.tensor_tensor(sprod[:], fac1[:, 0:1], fac1[:, 1:2], ALU.mult).then_inc(wscale_step, 1)
            v.wait_ge(wscale_step, 4)
            v.reciprocal(exp_scale1[:], sprod[:]).then_inc(wscale_step, 1)
            v.wait_ge(wscale_step, 5)
            v.tensor_scalar(exp_scale1[:], exp_scale1[:], float(D1) ** -0.5, None, ALU.mult)


def norm_statistics(v, s, step):
    half, total, dif = s["ln_half"], s["ln_sum"][:], s["ln_dif"][:]
    v.tensor_tensor(total, half[:, :, 1], half[:, :, 4], ALU.add)
    v.tensor_tensor(dif, half[:, :, 1], half[:, :, 4], ALU.subtract)
    v.tensor_tensor(s["ln_var"][:], half[:, :, 2], half[:, :, 5], ALU.add).then_inc(step, 1)
    v.wait_ge(step, 1)
    v.tensor_scalar(s["ln_mean"][:], total, 0.5, None, ALU.mult)
    v.scalar_tensor_tensor(dif, dif, 0.25, dif, ALU.mult, ALU.mult)
    v.tensor_scalar(s["ln_var"][:], s["ln_var"][:], 1.0 / C, LN_EPS, ALU.mult, ALU.add).then_inc(step, 1)
    v.wait_ge(step, 2)
    v.tensor_tensor(s["ln_var"][:], s["ln_var"][:], dif, ALU.add).then_inc(step, 1)


def at_least(eng, semaphore, count):
    if not (isinstance(count, int) and count <= 0):
        eng.wait_ge(semaphore, count)


def attention(nc, sb, sem, s, layer):
    first = layer == 0
    L = f"{layer}"
    heads, d, pairs, slot = (HEADS0, D0, PAIRS0, SLOT0) if first else (HEADS1, D1, PAIRS1, SLOT1)
    per_tile = heads // TILES3
    vwin = 2 if first else NQB
    vstep = KEYS if first else QBLOCK
    vd = d + 1
    cols = heads * KEYS
    half = cols // 2
    qrows = KEYS if first else QBLOCK
    halo = 0 if first else QBLOCK

    x_all, bank, score_banks = s["x_all"], s["bank"], s["score_banks"]
    w_qkv, w_proj = s["w_qkv"][layer], s["w_proj"][layer]
    perm, ident, ident_bf, ident_h = s["perm"], s["ident"], s["ident_bf"], s["ident_h"]

    bufs = s["buffers"][layer]
    xnT, stack, kT, vals, ones, oT = (bufs[n] for n in ("xnT", "stack", "kT", "vals", "ones", "oT"))
    sq = sb("sq" + L, [P, 2 * C])
    sumsq = sb("sumsq" + L, [P, 2 * heads])
    log_sum = sb("log_sum" + L, [P, 2 * heads])
    guess = sb("guess" + L, [P, 2 * heads])
    guess_scaled = sb("guess_scaled" + L, [P, 2 * heads])
    newton = sb("newton" + L, [P, 2 * heads])
    rnorm = sb("rnorm" + L, [P, 2 * heads])
    qk = sb("qk" + L, [P, 2 * heads, d])
    qT = sb("qT" + L, [P, TILES3, P], F16)
    negmax = sb("negmax" + L, [P, heads], BF16)
    probs = sb("probs" + L, [P, cols])
    probsT = sb("probsT" + L, [P, pairs, P])
    rsum = sb("rsum" + L, [P, heads])
    o_tm = sb("o_tm" + L, [P, PER_IMAGE, C])
    x_new = sb("x_new" + L, [P, PER_IMAGE, C])
    stat6 = sb("stat6" + L, [P, PER_IMAGE, 6])
    xn_tm = sb("xn_tm" + L, [P, PER_IMAGE, C])

    qk_bank, v_bank, t_bank, o_bank = bank
    stackT_ps = t_bank[:].bitcast(F16)
    PV_COLS = heads * vd
    OT_AT = 128

    pair_of = [2 * (i % TILES3) + i // TILES3 for i in range(pairs)] if first else list(range(pairs))

    names = ("xn_ready", "xnT_ps", "xnT_ready", "qk_proj_ready", "v_proj_ready", "squares_ready", "squares_summed", "sumsq_ready", "log_ready", "guess_ready",
             "newton_step", "rnorm_ready", "qk_ready", "q_hi", "k_hi", "stack_ready", "stackT_ready", "qkT_ready", "v_ready",
             "row_group_done", "scores_ready", "negmax_ready", "shifted_ready", "probs_ready", "probsT_ready", "probsT_copied_a",
             "probsT_copied_b", "pv_ready", "rsum_ready", "o_ready", "oT_ready", "oT_copied", "proj_out_ready",
             "x_ready", "bn_ready", "stat_ready", "ln_step", "ln_logged", "ln_guessed", "ln_newton_step", "split_step")
    q = {n: sem(n + L) for n in names}

    def on(n):
        return not isinstance(n, int) or 0 <= n < UNITS

    def pe_stacks(pe, n):
        if on(n + 1):
            at_least(pe, q["stack_ready"], n + 2)
            at_least(pe, q["qkT_ready"], n + 1)
            st = stack[:].rearrange("p h e -> p (h e)")
            for t in range(2 * TILES3):
                last = pe.transpose(stackT_ps[:, t * P:(t + 1) * P], st[:, t * P:(t + 1) * P], ident_h[:])
            last.then_inc(q["stackT_ready"], 1)

    def pe_step(pe, b, k):
        n = 2 * b + k
        S = score_banks[k]
        if on(n):
            if not first and k == 0 and on(n + 2):
                at_least(pe, q["xnT_ready"], b + 2)
            at_least(pe, q["qkT_ready"], n + 1)
            at_least(pe, q["probsT_copied_a"], n - 1)
            if first:
                at_least(pe, q["probsT_copied_b"], n - 1)
            for i, g in enumerate((0, 2, 1, 3) if first else (0, 1)):
                g2 = g // 2 if first else g
                Sg = S[:, g2, 0:half]
                if first and i < 2:
                    pe.matmul(Sg, s["ident_scaled"][:], s["bias_bf"][:, k, g2 * half:(g2 + 1) * half],
                              start=True, stop=False, skip_group_check=True)
                    pe.matmul(Sg, s["ident_scaled"][:], s["bias_lo"][:, k, g2 * half:(g2 + 1) * half],
                              start=False, stop=False, skip_group_check=True)
                if not first:
                    pe.matmul(Sg.rearrange("p (t j) -> p t j", t=TILES3), ident_bf[:],
                              s["band"][:, k, None, :].to_broadcast([P, TILES3, KEYS]),
                              start=True, stop=False, skip_group_check=True)
                if i >= 2:
                    at_least(pe, q["row_group_done"], 2 * n + i - 1)
                for t in range(TILES3):
                    for w in range(P // qrows):
                        rows = slice(slot * g, slot * (g + 1))
                        at = (t * 2 + g % 2) * KEYS if first else t * KEYS
                        k0 = w * KEYS if first else k * P + w * QBLOCK
                        last = pe.matmul(S[w * qrows:(w + 1) * qrows, g2, at:at + KEYS],
                                         qT[rows, t, w * qrows:(w + 1) * qrows], kT[rows, t, k0:k0 + KEYS],
                                         start=False, stop=True, skip_group_check=True)
                if first and i < 2:
                    last.then_inc(q["row_group_done"], 1)
            last.then_inc(q["scores_ready"], 1)
        if on(n - 1):
            at_least(pe, q["probsT_copied_a"], n)
            if first:
                at_least(pe, q["probsT_copied_b"], n)
            at_least(pe, q["v_ready"], n)
            at_least(pe, q["o_ready"], n - 1)
            if k == 0:
                at_least(pe, q["x_ready"], b - 1)
            else:
                at_least(pe, q["oT_copied"], b)
            for h2 in range(pairs):
                for w in range(P // qrows):
                    rows = slice(w * qrows, (w + 1) * qrows)
                    last = pe.matmul(o_bank[rows, pair_of[h2] * 2 * vd:(pair_of[h2] + 1) * 2 * vd],
                                     probsT[:, h2, rows], vals[(k + 1) % 2][:, w, pair_of[h2], :],
                                     start=True, stop=True)
            last.then_inc(q["pv_ready"], 1)
        if on(n + 2):
            mine = xnT[:, k * P:(k + 1) * P] if first else xnT[:, halo + k * P:halo + (k + 1) * P]
            at_least(pe, q["xnT_ready"], b + 2)
            at_least(pe, q["qk_ready"], n + 2)
            pe.matmul(qk_bank[:, 0:2 * C], mine, w_qkv[:, 0:2 * C], start=True, stop=True).then_inc(q["qk_proj_ready"], 1)
        if on(n):
            at_least(pe, q["negmax_ready"], n + 1)
            for g2 in range(2):
                Sg = S[:, g2, 0:half].rearrange("p (h j) -> p h j", j=KEYS)
                last = pe.matmul(Sg, ident_bf[:],
                                 negmax[:, g2 * heads // 2:(g2 + 1) * heads // 2, None].to_broadcast(
                                     [P, heads // 2, KEYS]), start=False, stop=True, skip_group_check=True)
            last.then_inc(q["shifted_ready"], 1)
        if not first:
            pe_stacks(pe, n)
        if on(n + 2):
            at_least(pe, q["v_ready"], n + 2)
            base = k * P
            for w in range(vwin // 2):
                at = base + w * vstep
                pe.matmul(v_bank[:, w * C:(w + 1) * C], xnT[:, at:at + P], w_qkv[:, 2 * C:3 * C],
                          start=True, stop=True)
                far = w + vwin // 2
                pe.matmul(v_bank[0:KEYS, far * C:(far + 1) * C], xnT[:, at + KEYS:at + 2 * KEYS],
                          w_qkv[:, 2 * C:3 * C], start=True, stop=True)
                last = pe.matmul(v_bank[KEYS:P, far * C:(far + 1) * C], xnT[:, at:at + KEYS],
                                 w_qkv[:, 2 * C:3 * C], start=True, stop=True)
            last.then_inc(q["v_proj_ready"], 1)
        if not first and k == 1 and on(n + 3):
            at_least(pe, q["xn_ready"], b + 3)
            for i in range(PER_IMAGE):
                last = pe.transpose(score_banks[0][0:C, i, half:half + P], xn_tm[:, i, :], ident)
            last.then_inc(q["xnT_ps"], 1)
        if first:
            pe_stacks(pe, n)
        if k == 0 and on(n - 1):
            at_least(pe, q["o_ready"], n)
            to = o_bank[0:C, OT_AT:OT_AT + T]
            if first:
                pe.transpose(to[:, 64:192], o_tm[:, 0, :], perm[:, 3, :])
                wrap = to.rearrange("c (a t) -> c a t", a=4)[:, 0:4:3, :]
                last = pe.transpose(wrap, o_tm[:, 1, :], perm[:, 4, :])
            else:
                pe.transpose(to[:, 0:P], o_tm[:, 0, :], ident)
                last = pe.transpose(to[:, P:T], o_tm[:, 1, :], ident)
            last.then_inc(q["oT_ready"], 1)
        if k == 1 and on(n - 3):
            at_least(pe, q["oT_copied"], b)
            at_least(pe, q["o_ready"], n if not isinstance(n, int) or n <= UNITS else UNITS)
            for i in range(PER_IMAGE):
                last = pe.matmul(o_bank[:, OT_AT + i * C:OT_AT + (i + 1) * C], oT[:, i * P:(i + 1) * P], w_proj[:],
                                 start=True, stop=True)
            last.then_inc(q["proj_out_ready"], 1)
        if on(n):
            at_least(pe, q["probs_ready"], n + 1)
            for i in range(pairs):
                to = S[:, i // TILES3, (i % TILES3) * P:(i % TILES3 + 1) * P]
                last = pe.transpose(to, probs[:, i * P:(i + 1) * P], ident)
            last.then_inc(q["probsT_ready"], 1)

    def act_step(act, b, k):
        n = 2 * b + k
        if first:
            act_stacks(act, n)
        if on(n + 1):
            at_least(act, q["v_proj_ready"], n + 2)
            at_least(act, q["pv_ready"], n)
            to = vals[(k + 1) % 2]
            src = v_bank[:, 0:vwin * C].rearrange("p (w t e) -> p w t e", w=vwin, e=2 * d)
            near, far = slice(0, vwin // 2), slice(vwin // 2, vwin)
            nc.scalar.activation(to[0:KEYS, :, :, 0:d], src[0:KEYS, :, :, 0:d], ACT.Copy)
            nc.scalar.activation(to[KEYS:P, near, :, vd:vd + d], src[KEYS:P, far, :, d:2 * d], ACT.Copy)
            last = nc.scalar.activation(to[KEYS:P, far, :, vd:vd + d], src[KEYS:P, near, :, d:2 * d], ACT.Copy)
            last.then_inc(q["v_ready"], 1)
        if first and on(n + 2):
            at_least(act, q["qk_proj_ready"], n + 3)
            at_least(act, q["sumsq_ready"], n + 2)
            nc.scalar.activation(sq[:], qk_bank[:, 0:2 * C], ACT.Square).then_inc(q["squares_ready"], 1)
        if on(n):
            at_least(act, q["shifted_ready"], n + 1)
            if first:
                nc.scalar.activation(probs[:].rearrange("p (g c) -> p g c", g=2), score_banks[k][:, :, 0:half],
                                     ACT.Exp, scale=1.0 / (QK_SCALE0 * QK_SCALE0)).then_inc(q["probs_ready"], 1)
            else:
                nc.scalar.activation(probs[:].rearrange("p (t g j) -> p g t j", g=2, j=KEYS),
                                     score_banks[k][:, :, 0:half].rearrange("p g (t j) -> p g t j", j=KEYS),
                                     ACT.Exp, scale=s["exp_scale1"][:, 0:1]).then_inc(q["probs_ready"], 1)
        if on(n + 1):
            at_least(act, q["stackT_ready"], n + 2)
            st = stackT_ps.rearrange("p (t e) -> p t e", e=P)
            kcol = 0 if first else halo + ((k + 1) % 2) * P
            nc.scalar.activation(qT[:], st[:, 0:TILES3, :], ACT.Copy)
            nc.scalar.activation(kT[:, :, kcol:kcol + P], st[:, TILES3:2 * TILES3, :],
                                 ACT.Copy).then_inc(q["qkT_ready"], 1)
        if not first:
            act_stacks(act, n)
        if first and on(n + 2):
            at_least(act, q["sumsq_ready"], n + 3)
            at_least(act, q["rnorm_ready"], n + 2)
            nc.scalar.activation(log_sum[:], sumsq[:], ACT.Ln).then_inc(q["log_ready"], 1)
            at_least(act, q["log_ready"], n + 3)
            nc.scalar.activation(guess[:], log_sum[:], ACT.Exp, scale=-0.5).then_inc(q["guess_ready"], 1)
        if on(n):
            at_least(act, q["probsT_ready"], n + 1)
            if first:
                nc.scalar.activation(probsT[:, 0:TILES3, :].rearrange("p t e -> p (t e)"),
                                     score_banks[k][:, 0, 0:TILES3 * P], ACT.Copy).then_inc(q["probsT_copied_a"], 1)
            else:
                nc.scalar.activation(probsT[:].rearrange("p t e -> p (t e)"),
                                     score_banks[k][:, 0, 0:TILES3 * P], ACT.Copy).then_inc(q["probsT_copied_a"], 1)

    def dve_step(v, b, k):
        n = 2 * b + k
        if first and on(n + 1):
            at_least(v, q["stack_ready"], n + 1)
            at_least(v, q["rnorm_ready"], n + 2)
            v.tensor_tensor(qk[:], qk_bank[:, 0:2 * C].rearrange("p (h e) -> p h e", e=d),
                            rnorm[:, :, None].to_broadcast([P, 2 * heads, d]), ALU.mult).then_inc(q["qk_ready"], 1)
        if first and k == 0 and on(n + 2):
            at_least(v, q["v_proj_ready"], n + 2)
            v.tensor_scalar(xnT[0:C, :], s["xT_all"][:, b + 1, :], s["gn_scale"][:, bass.ds(b + 1, 1)],
                            s["gn_shift"][:, bass.ds(b + 1, 1)], ALU.mult, ALU.add).then_inc(q["xnT_ready"], 1)
        if on(n):
            at_least(v, q["scores_ready"], n + 1)
            v.tensor_reduce(negmax[:].rearrange("p (g h) -> p g h", g=2),
                            score_banks[k][:, :, 0:half].rearrange("p g (h j) -> p g h j", j=KEYS), AX.X, ALU.max,
                            negate=True).then_inc(q["negmax_ready"], 1)
        if not first and on(n + 2):
            at_least(v, q["stack_ready"], n + 2)
            at_least(v, q["qk_proj_ready"], n + 3)
            v.tensor_tensor(qk[:].rearrange("p (a h) e -> p a (h e)", a=2),
                            qk_bank[:, 0:2 * C].rearrange("p (a e) -> p a e", a=2),
                            s["fac1"][:, :, None].to_broadcast([P, 2, C]), ALU.mult).then_inc(q["qk_ready"], 1)
        if on(n - 1):
            at_least(v, q["pv_ready"], n)
            pv = o_bank[:, 0:PV_COLS].rearrange("p (h e) -> p h e", e=vd)
            v.reciprocal(rsum[:], pv[:, :, d]).then_inc(q["rsum_ready"], 1)
            at_least(v, q["rsum_ready"], n)
            at_least(v, q["oT_ready"], b - 1 if k == 0 else b)
            v.tensor_tensor(o_tm[:, (k + 1) % 2, :].rearrange("p (h e) -> p h e", e=d), pv[:, :, 0:d],
                            rsum[:, :, None].to_broadcast([P, heads, d]), ALU.mult).then_inc(q["o_ready"], 1)
        if k == 0 and on(n - 4):
            at_least(v, q["x_ready"], b - 1)
            for i in range(PER_IMAGE):
                last = v.bn_stats(stat6[:, i, :], x_new[:, i, :])
            last.then_inc(q["bn_ready"], 1)
            img = bass.ds(2 * (b - 2), PER_IMAGE)
            v.tensor_scalar(x_all[:, img, :], x_new[:], 1.0, None, ALU.mult)
            at_least(v, q["bn_ready"], b - 1)
            v.tensor_scalar(s["ln_half"][:, img, :], stat6[:], 1.0, None, ALU.mult).then_inc(q["stat_ready"], 1)
        if on(n + 2):
            if first:
                at_least(v, q["squares_ready"], n + 3)
                v.tensor_reduce(sumsq[:], sq[:].rearrange("p (h e) -> p h e", e=d), AX.X,
                                ALU.add).then_inc(q["squares_summed"], 1)
                at_least(v, q["squares_summed"], n + 3)
                v.tensor_scalar(sumsq[:], sumsq[:], 1e-24, None, ALU.max).then_inc(q["sumsq_ready"], 1)
        if not first and k == 1 and on(n + 3):
            at_least(v, q["v_proj_ready"], n + 3)
            at_least(v, q["xnT_ps"], b + 3)
            v.tensor_copy(xnT[0:C, halo:].rearrange("c (i t) -> c i t", i=PER_IMAGE),
                          score_banks[0][0:C, :, half:half + P]).then_inc(q["xnT_ready"], 1)
        if k == 1 and on(n - 3):
            at_least(v, q["proj_out_ready"], b)
            img = bass.ds(2 * (b - 1), PER_IMAGE)
            v.tensor_tensor(x_new[:], x_all[:, img, :],
                            o_bank[:, OT_AT:OT_AT + 2 * C].rearrange("p (i c) -> p i c", i=PER_IMAGE),
                            ALU.add).then_inc(q["x_ready"], 1)
        if first and on(n):
            at_least(v, q["probsT_ready"], n + 1)
            v.tensor_copy(probsT[:, TILES3:, :].rearrange("p t e -> p (t e)"),
                          score_banks[k][:, 1, 0:TILES3 * P]).then_inc(q["probsT_copied_b"], 1)
        if first and on(n + 2):
            at_least(v, q["guess_ready"], n + 3)
            v.scalar_tensor_tensor(newton[:], guess[:], -0.5, guess[:], ALU.mult,
                                   ALU.mult).then_inc(q["newton_step"], 1)
            v.tensor_tensor(guess_scaled[:], guess[:], s["head_scale"][:], ALU.mult)
            at_least(v, q["newton_step"], 2 * n + 5)
            v.tensor_tensor(newton[:], newton[:], sumsq[:], ALU.mult).then_inc(q["newton_step"], 1)
            at_least(v, q["newton_step"], 2 * n + 6)
            v.scalar_tensor_tensor(rnorm[:], newton[:], 1.5, guess_scaled[:], ALU.add,
                                   ALU.mult).then_inc(q["rnorm_ready"], 1)
        if k == 0 and on(n - 1):
            at_least(v, q["oT_ready"], b)
            at_least(v, q["proj_out_ready"], b - 1)
            v.tensor_copy(oT[0:C, :], o_bank[0:C, OT_AT:OT_AT + T]).then_inc(q["oT_copied"], 1)
        if not first and k == 0 and on(n + 4):
            normalise(v, b + 2)

    def normalise(v, img):
        at_least(v, q["xnT_ps"], img)
        for i in range(PER_IMAGE):
            u = 2 * img + i
            last = v.tensor_scalar(xn_tm[:, i, :], x_all[:, u, :], s["ln_mean"][:, bass.ds(u, 1)], s["ln_rstd"][:, bass.ds(u, 1)],
                                   ALU.subtract, ALU.mult)
        last.then_inc(q["xn_ready"], 1)

    ahead = 1 if first else 2

    def act_stacks(act, n):
        if on(n + ahead):
            at_least(act, q["qk_ready"], n + ahead + 1)
            at_least(act, q["stackT_ready"], n + ahead)
            nc.scalar.activation(stack[:, heads:, 0:2 * d].rearrange("p h (e d) -> p h e d", d=d),
                                 qk[:, heads:, None, :].to_broadcast([P, heads, 2, d]), ACT.Copy).then_inc(q["k_hi"], 1)

    def pool_step(pool, b, k):
        n = 2 * b + k
        if on(n + ahead):
            at_least(pool, q["qk_ready"], n + ahead + 1)
            at_least(pool, q["stackT_ready"], n + ahead)
            nc.gpsimd.tensor_tensor(stack[:, 0:heads, 0:3 * d].rearrange("p h (e d) -> p h e d", d=d)[:, :, 0:3:2, :],
                                    qk[:, 0:heads, None, :].to_broadcast([P, heads, 2, d]),
                                    ones[:, 0:1, None, None].to_broadcast([P, heads, 2, d]),
                                    ALU.mult).then_inc(q["q_hi"], 1)
            at_least(pool, q["q_hi"], n + ahead + 1)
            nc.gpsimd.tensor_tensor(stack[:, 0:heads, d:2 * d], qk[:, 0:heads, :], stack[:, 0:heads, 0:d], ALU.subtract)
            at_least(pool, q["k_hi"], n + ahead + 1)
            nc.gpsimd.tensor_tensor(stack[:, heads:, 2 * d:3 * d], qk[:, heads:, :], stack[:, heads:, 0:d],
                                    ALU.subtract).then_inc(q["stack_ready"], 1)

    def run(eng, step):
        for n in range(-2 if first else -3, 4):
            step(eng, n // 2, n % 2)
        with eng.Fori(1, (B - 2) // 2) as i:
            for b in (2 * i, 2 * i + 1):
                step(eng, b, 0)
                step(eng, b, 1)
        for n in range(UNITS - 4, UNITS + 3):
            step(eng, n // 2, n % 2)

    with nc.Block() as block:
        @block.gpsimd
        def _(pool):
            run(pool, pool_step)
            if first:
                pool.wait_ge(s["w1_loaded"], 16)
                split_parts(pool, nc, s["w1"][:], s["w1_hi"][:], s["w1_lo"][:], q["split_step"])
            else:
                pool.wait_ge(s["experts_loaded"], 16 * 4)
                split_expert_bias(pool, nc, s, q["split_step"])

        @block.vector
        def _(v):
            if not first:
                norm_statistics(v, s, q["ln_step"])
                newton_root(v, s["ln_rstd"][:], s["ln_var"][:], s["ln_guess"][:], s["ln_newton"][:], q["ln_guessed"],
                       q["ln_newton_step"])
                normalise(v, 0)
            run(v, dve_step)

        @block.scalar
        def _(act):
            if not first:
                first_guess(act, nc, s["ln_var"][:], s["ln_log"][:], s["ln_guess"][:], (q["ln_step"], 3), q["ln_logged"],
                            q["ln_guessed"])
            run(act, act_step)

        @block.tensor
        def _(pe):
            run(pe, pe_step)


def split_parts(pool, nc, whole, hi, lo, step):
    nc.gpsimd.tensor_copy(hi, whole).then_inc(step, 1)
    pool.wait_ge(step, 1)
    nc.gpsimd.tensor_tensor(lo, whole, hi, ALU.subtract).then_inc(step, 1)
    pool.wait_ge(step, 2)


def split_expert_bias(pool, nc, s, step):
    ident, hi, lo = s["ident"], s["b2_hi"][:], s["b2_lo"][:]
    split_parts(pool, nc, s["b2_f"][:], hi, lo, step)
    nc.gpsimd.tensor_scalar(hi, hi, ident[0:2, 0:1], None, ALU.mult).then_inc(step, 1)
    nc.gpsimd.tensor_scalar(lo, lo, ident[0:2, 1:2], None, ALU.mult).then_inc(step, 1)
    pool.wait_ge(step, 4)
    nc.gpsimd.tensor_tensor(s["b2_rows"][:].rearrange("p e c -> p (e c)"), hi, lo, ALU.add)


def experts(nc, sb, sem, s, out):
    HBUF = 3
    LAG = 2
    x_all, bank, score_banks = s["x_all"], s["bank"], s["score_banks"]
    ident = s["ident"]
    w1_hi, w1_lo, w2, w_gate = (s[n] for n in ("w1_hi", "w1_lo", "w2", "w_gate"))
    b2_rows, ones2, xT_hi, xT_lo = (s[n] for n in ("b2_rows", "ones2", "moe_hi", "moe_lo"))
    earlier = s["earlier"]
    xn = [sb(f"moe_xn{k}", [P, CT, C]) for k in range(2)]
    hidden = [sb(f"hidden{i}", [P, CHUNK]) for i in range(HBUF)]
    xT = [sb(f"moe_xT{k}", [K1, CHUNK]) for k in range(2)]
    acc = [sb(f"acc{k}", [P, CT, C]) for k in range(2)]
    gates = sb("gates", [P, UNITS, EXPERTS])
    pe_ = sb("gate_exp", [P, UNITS, EXPERTS])
    shifted = sb("gate_shifted", [P, UNITS, EXPERTS])
    gmax = sb("gate_max", [P, UNITS])
    above = sb("gate_above", [P, UNITS, EXPERTS, EXPERTS])
    tied = sb("gate_tied", [P, UNITS, EXPERTS, EXPERTS])
    rank = sb("gate_rank", [P, UNITS, EXPERTS])
    gsum = sb("gate_sum", [P, UNITS])
    h_bank = [score_banks[0][:, 0, :], score_banks[0][:, 1, :], bank[3][:]]
    y_bank = [score_banks[1][:, 0, :], score_banks[1][:, 1, :]]
    x_bank, g_bank = [bank[0], bank[2]], bank[1]
    out_v = out.rearrange("b h w c -> (b h w) c").rearrange("(u p) c -> p u c", p=P)
    BATCHES = ((0, 2), (2, CHUNKS))

    names = ("ln_step", "ln_logged", "ln_guessed", "ln_newton_step", "xn_ready", "xn_pool_ready", "xT_ps", "xhi_ready", "xlo_ready",
             "scores", "gate_step", "gate_exp", "gates_ready", "hidden_ps", "hidden_ready", "hidden_used",
             "y_used")
    q = {n: sem("moe_" + n) for n in names}
    stored = [sem(f"moe_stored{k}") for k in range(2)]
    GSTEPS = 12

    def inputs_at(c, m):
        return 2 + 3 * c + (m - 2) // 3 if isinstance(c, int) and c < 2 and m in (2, 5, 8) else None

    def gates_at(c, m):
        return inputs_at(c, m - 2)

    def pe_inputs(pe, c):
        if c < 2:
            pe.wait_ge(q["xn_ready"], c + 1)
        else:
            pe.wait_ge(q["xn_pool_ready"], c - 1)
            pe.wait_ge(q["xlo_ready"], c - 1)
        for j in range(CT):
            last = pe.transpose(x_bank[c % 2][0:C, j * P:(j + 1) * P], xn[c % 2][:, j, :], ident)
        last.then_inc(q["xT_ps"], 1)

    def pe_gates(pe, c):
        pe.wait_ge(q["xlo_ready"], c + 1)
        if c == BATCHES[1][0]:
            pe.wait_ge(q["gate_step"], 2)
        for j in range(CT):
            u = CT * c + j
            to = g_bank[:, u * EXPERTS:(u + 1) * EXPERTS]
            last = pe.matmul(to, xT[c % 2][:, j * P:(j + 1) * P], w_gate[:], start=True, stop=True)
        last.then_inc(q["scores"], 1)

    def pe_first(pe, c, m):
        G = NH * c + m
        at_least(pe, q["hidden_ready"], G + 1 - HBUF)
        w = slice(m * P, (m + 1) * P)
        pe.matmul(h_bank[m % HBUF], w1_hi[:, w], xT_hi[:, c, :], start=True, stop=False)
        pe.matmul(h_bank[m % HBUF], w1_hi[:, w], xT_lo[:, c, :], start=False, stop=False)
        pe.matmul(h_bank[m % HBUF], w1_lo[:, w], xT_hi[:, c, :], start=False, stop=True).then_inc(q["hidden_ps"], 1)

    def pe_second(pe, c, m):
        e, i = divmod(m, HC)
        y = y_bank[e % 2][:, 0:CT * C]
        if i == 0:
            at_least(pe, q["y_used"], EXPERTS * c + e - 1)
            pe.matmul(y.rearrange("p (j c) -> p j c", j=CT), ones2[:], b2_rows[:, e, None, :].to_broadcast([2, CT, C]),
                      start=True, stop=False, skip_group_check=True)
        at_least(pe, q["hidden_ready"], NH * c + m + 1)
        for j in range(CT):
            yj, t = y[:, j * C:(j + 1) * C], slice(j * P, (j + 1) * P)
            last = pe.matmul(yj, hidden[m % HBUF][:, t], w2[:, m, :], start=False, stop=(i == HC - 1),
                             skip_group_check=True)
        last.then_inc(q["hidden_used"], 1)

    def pe_chunk(pe, c):
        for m in range(NH):
            pe_first(pe, c, m)
            if inputs_at(c, m) is not None:
                pe_inputs(pe, inputs_at(c, m))
            if gates_at(c, m) is not None:
                pe_gates(pe, gates_at(c, m))
            if m >= LAG:
                pe_second(pe, c, m - LAG)
            elif not isinstance(c, int) or c > 0:
                pe_second(pe, c - 1, NH + m - LAG)

    def act_inputs(act, c):
        act.wait_ge(q["xT_ps"], c + 1)
        nc.scalar.activation(xT_hi[0:C, c, :], x_bank[c % 2][0:C, :], ACT.Copy)
        if c >= 2:
            act.wait_ge(q["scores"], c - 1)
        nc.scalar.activation(xT[c % 2][0:C, :], x_bank[c % 2][0:C, :], ACT.Copy).then_inc(q["xhi_ready"], 1)

    def act_gate(act, batch):
        first, end = (CT * c for c in BATCHES[batch])
        act.wait_ge(q["gate_step"], GSTEPS * batch + 2)
        nc.scalar.activation(pe_[:, first:end, :], shifted[:, first:end, :], ACT.Exp).then_inc(q["gate_exp"], 1)

    def act_chunk(act, c):
        for m in range(NH):
            G = NH * c + m
            at_least(act, q["hidden_ps"], G + 1)
            at_least(act, q["hidden_used"], G + 1 - HBUF)
            nc.scalar.activation(hidden[m % HBUF][:], h_bank[m % HBUF], ACT.Gelu).then_inc(q["hidden_ready"], 1)
            if inputs_at(c, m) is not None:
                act_inputs(act, inputs_at(c, m))

    def normalise(eng, vector, c, done):
        for j in range(CT):
            u = CT * c + j
            last = vector.tensor_scalar(xn[c % 2][:, j, :], x_all[:, u, :], s["ln_mean"][:, u:u + 1],
                                        s["ln_rstd"][:, u:u + 1], ALU.subtract, ALU.mult)
        last.then_inc(done, 1)

    def dve_inputs(v, c):
        v.wait_ge(q["xhi_ready"], c + 1)
        v.tensor_tensor(xT_lo[0:C, c, :], x_bank[c % 2][0:C, :], xT_hi[0:C, c, :], ALU.subtract).then_inc(q["xlo_ready"], 1)

    def dve_gates(v, batch):
        first, end = (CT * c for c in BATCHES[batch])
        u, G, n = slice(first, end), GSTEPS * batch, end - first
        sc = g_bank[:, first * EXPERTS:end * EXPERTS].rearrange("p (j e) -> p j e", e=EXPERTS)
        v.wait_ge(q["scores"], BATCHES[batch][1])
        v.tensor_reduce(gmax[:, u], sc, AX.X, ALU.max).then_inc(q["gate_step"], 1)
        v.wait_ge(q["gate_step"], G + 1)
        v.tensor_tensor(shifted[:, u, :], sc, gmax[:, u, None].to_broadcast([P, n, EXPERTS]),
                        ALU.subtract).then_inc(q["gate_step"], 1)

    def dve_topk(v, batch):
        first, end = (CT * c for c in BATCHES[batch])
        u, G, n = slice(first, end), GSTEPS * batch, end - first
        p, ab, ti, gs = pe_[:, u, :], above[:, u], tied[:, u], gsum[:, u]
        v.wait_ge(q["gate_exp"], batch + 1)
        v.tensor_reduce(gs, p, AX.X, ALU.add).then_inc(q["gate_step"], 1)
        v.wait_ge(q["gate_step"], G + 3)
        v.reciprocal(gs, gs).then_inc(q["gate_step"], 1)
        v.wait_ge(q["gate_step"], G + 4)
        v.tensor_tensor(p, p, gsum[:, u, None].to_broadcast([P, n, EXPERTS]), ALU.mult).then_inc(q["gate_step"], 1)
        v.wait_ge(q["gate_step"], G + 5)
        for e in range(EXPERTS):
            mine = pe_[:, u, e:e + 1].to_broadcast([P, n, EXPERTS])
            v.tensor_tensor(above[:, u, e, :], p, mine, ALU.is_gt)
            last = v.tensor_tensor(tied[:, u, e, :], p, mine, ALU.is_equal)
        last.then_inc(q["gate_step"], 1)
        v.wait_ge(q["gate_step"], G + 6)
        v.tensor_tensor(ti, ti, earlier[:, None].to_broadcast([P, n, EXPERTS, EXPERTS]),
                        ALU.mult).then_inc(q["gate_step"], 1)
        v.wait_ge(q["gate_step"], G + 7)
        v.tensor_tensor(ab, ab, ti, ALU.add).then_inc(q["gate_step"], 1)
        v.wait_ge(q["gate_step"], G + 8)
        v.tensor_reduce(rank[:, u, :], ab, AX.X, ALU.add).then_inc(q["gate_step"], 1)
        v.wait_ge(q["gate_step"], G + 9)
        v.scalar_tensor_tensor(p, rank[:, u, :], float(TOP), p, ALU.is_lt, ALU.mult).then_inc(q["gate_step"], 1)
        v.wait_ge(q["gate_step"], G + 10)
        v.tensor_reduce(gs, p, AX.X, ALU.add).then_inc(q["gate_step"], 1)
        v.wait_ge(q["gate_step"], G + 11)
        v.tensor_scalar(gs, gs, 1e-9, None, ALU.add).then_inc(q["gate_step"], 1)
        v.wait_ge(q["gate_step"], G + 12)
        v.reciprocal(gmax[:, u], gs).then_inc(q["gates_ready"], 1)
        v.wait_ge(q["gates_ready"], 2 * batch + 1)
        v.tensor_tensor(gates[:, u, :], p, gmax[:, u, None].to_broadcast([P, n, EXPERTS]),
                        ALU.mult).then_inc(q["gates_ready"], 1)

    def dve_add(v, c, k, e):
        at_least(v, q["hidden_used"], NH * c + HC * (e + 1))
        if isinstance(c, int) and c < BATCHES[0][1]:
            v.wait_ge(q["gates_ready"], 2)
        if e == 0:
            at_least(v, stored[k], 16 * ((c - k) // 2))
        else:
            at_least(v, q["y_used"], EXPERTS * c + e)
        for j in range(CT):
            u = CT * c + j
            onto = x_all[:, u, :] if e == 0 else acc[k][:, j, :]
            last = v.scalar_tensor_tensor(acc[k][:, j, :], y_bank[e % 2][:, j * C:(j + 1) * C],
                                          gates[:, u, e:e + 1], onto, ALU.mult, ALU.add)
        last.then_inc(q["y_used"], 1)

    def dve_chunk(v, c, k):
        for m in range(NH):
            if inputs_at(c, m) is not None:
                dve_inputs(v, inputs_at(c, m))
            if m % HC == 2:
                e = m // HC - 1
                if e >= 0:
                    dve_add(v, c, k, e)
                elif not isinstance(c, int) or c > 0:
                    dve_add(v, c - 1, 1 - k, EXPERTS - 1)
            if isinstance(c, int) and c == 0 and m == 0:
                dve_topk(v, 0)
        if isinstance(c, int) and c == 1:
            dve_gates(v, 1)
            dve_topk(v, 1)
            v.wait_ge(q["gates_ready"], 4)

    def chunks(eng, step):
        step(eng, 0, 0)
        step(eng, 1, 1)
        with eng.Fori(1, CHUNKS // 2) as cc:
            step(eng, 2 * cc, 0)
            step(eng, 2 * cc + 1, 1)

    with nc.Block() as block:
        @block.gpsimd
        def _(pool):
            pool.wait_ge(q["ln_newton_step"], 3)
            for c in range(2, CHUNKS):
                pool.wait_ge(q["xT_ps"], c - 1)
                normalise(pool, nc.gpsimd, c, q["xn_pool_ready"])
                pool.wait_ge(q["xn_pool_ready"], c - 1)

        @block.sync
        def _(sp):
            with sp.Fori(0, CHUNKS // 2) as cc:
                for k in range(2):
                    c = 2 * cc + k
                    sp.wait_ge(q["y_used"], EXPERTS * (c + 1))
                    sp.dma_start(out_v[:, bass.ds(CT * c, CT), :], acc[k][:]).then_inc(stored[k], 16)
            for k in range(2):
                sp.wait_ge(stored[k], 16 * (CHUNKS // 2))

        @block.vector
        def _(v):
            norm_statistics(v, s, q["ln_step"])
            for k in range(2):
                v.memset(xT[k][C:K1, :], 1.0)
            newton_root(v, s["ln_rstd"][:], s["ln_var"][:], s["ln_guess"][:], s["ln_newton"][:], q["ln_guessed"],
                        q["ln_newton_step"])
            for c in range(2):
                normalise(v, nc.vector, c, q["xn_ready"])
            for c in range(2):
                dve_inputs(v, c)
            dve_gates(v, 0)
            chunks(v, dve_chunk)
            dve_add(v, CHUNKS - 1, 1, EXPERTS - 1)

        @block.scalar
        def _(act):
            first_guess(act, nc, s["ln_var"][:], s["ln_log"][:], s["ln_guess"][:], (q["ln_step"], 3), q["ln_logged"],
                        q["ln_guessed"])
            for c in range(2):
                act_inputs(act, c)
            act_gate(act, 0)
            act_chunk(act, 0)
            act_chunk(act, 1)
            act_gate(act, 1)
            with act.Fori(1, CHUNKS // 2) as cc:
                act_chunk(act, 2 * cc)
                act_chunk(act, 2 * cc + 1)

        @block.tensor
        def _(pe):
            for c in range(2):
                pe_inputs(pe, c)
            for c in range(2):
                pe_gates(pe, c)
            pe_chunk(pe, 0)
            pe_chunk(pe, 1)
            with pe.Fori(1, CHUNKS // 2) as cc:
                pe_chunk(pe, 2 * cc)
                pe_chunk(pe, 2 * cc + 1)
            for m in range(NH - LAG, NH):
                pe_second(pe, CHUNKS - 1, m)


def shape_constants():
    i = np.arange(P)
    perms = np.zeros((P, 5, P), np.float32)
    perms[i, 0, i] = 1
    row, col = i // HW, i % HW
    for tile in range(PER_IMAGE):
        r, c = (tile * WIN + row - SHIFT) % HW, (col - SHIFT) % HW
        perms[i, 1 + tile, r // WIN * KEYS + c // WIN * (KEYS // 2) + r % SHIFT * WIN + c % WIN] = 1
    w, r, c = i // KEYS, i % KEYS // WIN, i % WIN
    wcol = (w * WIN + c + SHIFT) % HW
    perms[i, 3, r * HW + wcol] = 1
    perms[i, 4, (r + SHIFT) % WIN * HW + wcol] = 1
    ch = np.arange(-(WIN - 1), WIN, dtype=np.float32)
    tab = np.stack(np.meshgrid(ch, ch, indexing="ij"), -1) / np.float32(WIN - 1) * np.float32(8)
    tab = np.sign(tab) * np.log2(np.abs(tab) + np.float32(1)) / np.float32(3)
    tab = tab[::-1, ::-1].reshape(-1, 2).astype(np.float32)
    rel = np.concatenate([tab.T, np.ones((1, tab.shape[0]), np.float32)])
    region = np.zeros((HW, HW), np.int64)
    cuts = (slice(0, HW - WIN), slice(HW - WIN, HW - SHIFT), slice(HW - SHIFT, HW))
    for m, hs in enumerate(cuts):
        for n, ws in enumerate(cuts):
            region[hs, ws] = 3 * m + n
    win = region.reshape(2, WIN, 2, WIN).transpose(0, 2, 1, 3).reshape(2, 2, KEYS)
    wmask = np.where(win[:, :, :, None] != win[:, :, None, :], -100.0, 0.0).astype(np.float32)
    wmask = wmask.reshape(2, P, KEYS).transpose(1, 0, 2)
    back = (QBLOCK + i % QBLOCK)[:, None] - np.arange(KEYS)[None]
    seen = (back >= 0) & (back <= BAND)
    seen = np.stack([seen & ~((i < QBLOCK)[:, None] & (np.arange(KEYS) < QBLOCK)[None]), seen], 1)
    bmask = np.where(seen, 0.0, MASKED).astype(np.float32)
    group = np.arange(C) // (C // GROUPS)
    gavg = (group[:, None] == group[None]).astype(np.float32) / np.float32(2 * C // GROUPS)
    earlier = (np.arange(EXPERTS)[None] < np.arange(EXPERTS)[:, None]).astype(np.float32)
    return {"permutations": perms, "rel_table": rel, "win_mask": wmask, "band_mask": bmask, "group_avg": gavg,
            "earlier": earlier}


def kernel(x, L0_conv_qkv_w, L0_conv_qkv_b, L0_conv_proj_w, L0_conv_proj_b, L0_conv_logit_scale, L0_conv_cpb_w1,
           L0_conv_cpb_b1, L0_conv_cpb_w2, L1_attn_qkv_w, L1_attn_qkv_b, L1_attn_proj_w, L1_attn_proj_b, L1_attn_gate,
           L1_ffn_gate_w, L1_ffn_gate_b, L1_ffn_w1, L1_ffn_b1, L1_ffn_w2, L1_ffn_b2):
    import concourse.bacc as bacc
    from concourse.bass_utils import run_bass_kernel_spmd

    cat = np.concatenate
    order = [4 * t + 2 * g + r for g in range(2) for t in range(TILES3) for r in range(2)]
    b0 = np.array(L0_conv_qkv_b)
    b0 = cat([b0[:C], np.zeros(C, np.float32), b0[2 * C:]])
    arrays = {
        "x": np.array(x),
        "w_qkv0": cat([np.array(L0_conv_qkv_w).T, b0[None]]),
        "w_proj0": cat([np.array(L0_conv_proj_w).T, np.array(L0_conv_proj_b)[None]]),
        "w_qkv1": cat([np.array(L1_attn_qkv_w), np.array(L1_attn_qkv_b)[None]]),
        "w_proj1": cat([np.array(L1_attn_proj_w), np.array(L1_attn_proj_b)[None]]),
        "gate_vec": np.array(L1_attn_gate)[:, None],
        "logit_scale": np.array(L0_conv_logit_scale).reshape(HEADS0),
        "cpb_w1": cat([np.array(L0_conv_cpb_w1).T, np.array(L0_conv_cpb_b1)[None]]),
        "cpb_w2": np.array(L0_conv_cpb_w2).T[:, order],
        "w1": cat([np.array(L1_ffn_w1).transpose(1, 0, 2).reshape(C, EXPERTS * HID),
                   np.array(L1_ffn_b1).reshape(1, EXPERTS * HID)]),
        "w2": np.array(L1_ffn_w2).reshape(NH, P, C).transpose(1, 0, 2),
        "b2": np.array(L1_ffn_b2).reshape(EXPERTS * C),
        "w_gate": cat([np.array(L1_ffn_gate_w), np.array(L1_ffn_gate_b)[None]]),
    }
    arrays.update(shape_constants())
    nc = bacc.Bacc("TRN2", target_bir_lowering=False, num_devices=1)
    feed, dram = {}, {}
    for name, value in arrays.items():
        feed["in_" + name] = np.ascontiguousarray(value)
        dram[name] = nc.dram_tensor("in_" + name, value.shape, mybir.dt.from_np(value.dtype), kind="ExternalInput").ap()
    out = nc.dram_tensor("out_0", (B, HW, HW, C), F32, kind="ExternalOutput").ap()
    build(nc, dram, out)
    result = run_bass_kernel_spmd(nc, [feed], core_ids=[0])
    return result.results[0]["out_0"]
```

```python
from contextlib import ExitStack

import numpy as np

import concourse.bass as bass
from concourse import mybir

F32 = mybir.dt.float32
F16 = mybir.dt.float16
BF16 = mybir.dt.bfloat16
F32R = mybir.dt.float32r
ALU = mybir.AluOpType
ACT = mybir.ActivationFunctionType
AX = mybir.AxisListType

B, HW, C = 16, 16, 96
T = HW * HW
P = 128
UNITS = B * T // P
PER_IMAGE = T // P
K1 = C + 1

WIN, SHIFT = 8, 4
KEYS = 64
BAND = 16
QBLOCK = 32
NQB = P // QBLOCK
GROUPS = 32
GN_EPS, LN_EPS = 1e-5, 1e-5

HEADS0, D0 = 12, C // 12
HEADS1, D1 = 6, C // 6
PAIRS0, PAIRS1 = HEADS0 // 2, HEADS1 // 2
SLOT0, SLOT1 = 32, 64
TILES3 = 3
QK_SCALE0 = 64.0
QK_RANGE1 = 1024.0
MASKED = -1e30

EXPERTS, TOP, HID = 4, 2, 384
CHUNK = 512
CHUNKS = B * T // CHUNK
CT = CHUNK // P
HC = HID // P
NH = EXPERTS * HC


def build(nc, a, out):
    ctx = ExitStack()
    with ctx:
        def sb(name, shape, dt=F32):
            return ctx.enter_context(nc.sbuf_tensor(name, shape, dt))

        def sem(name):
            return ctx.enter_context(nc.semaphore(name))

        perm = sb("perm", [P, 5, P])
        ident = perm[:, 0, :]
        ident_bf = sb("ident_bf", [P, P], BF16)
        ident_h = sb("ident_h", [P, P], F16)
        ident_scaled = sb("ident_scaled", [P, P], F16)
        group_avg = sb("group_avg", [C, C])
        w_qkv = [sb("w_qkv0", [P, 3 * C]), sb("w_qkv1", [P, 3 * C])]
        w_proj = [sb("w_proj0", [P, C]), sb("w_proj1", [P, C])]
        gate_vec = sb("gate_vec", [C, 1])
        w1 = sb("w1", [K1, EXPERTS * HID])
        w2 = sb("w2", [P, NH, C])
        w_gate = sb("w_gate", [K1, EXPERTS])
        b2_f = sb("b2_f", [2, EXPERTS * C])
        w1_hi, w1_lo = (sb("w1_" + n, [K1, EXPERTS * HID], F32R) for n in ("hi", "lo"))
        b2_hi, b2_lo = (sb("b2_" + n, [2, EXPERTS * C], F32R) for n in ("hi", "lo"))
        b2_rows = sb("b2_rows", [2, EXPERTS, C], F32R)
        ones2 = sb("ones2", [2, P], F32R)
        moe_hi, moe_lo = (sb("moe_" + n, [K1, CHUNKS, CHUNK], F32R) for n in ("hi", "lo"))
        moe_xT = [sb(f"moe_xT{k}", [K1, CHUNK]) for k in range(2)]
        earlier = sb("earlier", [P, EXPERTS, EXPERTS])
        bias_bf = sb("bias_bf", [P, 2, 768], F16)
        bias_lo = sb("bias_lo", [P, 2, 768], F16)
        band_f = sb("band_f", [P, 2, KEYS])
        band = sb("band", [P, 2, KEYS], BF16)
        head_scale = sb("head_scale", [P, 2 * HEADS0])
        minus_half = sb("minus_half", [P, 32])
        fac1 = sb("fac1", [P, 2])
        exp_scale1 = sb("exp_scale1", [P, 1])
        x_all = sb("x_all", [P, UNITS, C])
        xT_all = sb("xT_all", [C, B, T])
        gn_scale = sb("gn_scale", [C, B])
        gn_shift = sb("gn_shift", [C, B])
        ln_half = sb("ln_half", [P, UNITS, 6])
        ln_sum = sb("ln_sum", [P, UNITS])
        ln_dif = sb("ln_dif", [P, UNITS])
        ln_mean = sb("ln_mean", [P, UNITS])
        ln_var = sb("ln_var", [P, UNITS])
        ln_rstd = sb("ln_rstd", [P, UNITS])
        ln_log = sb("ln_log", [P, UNITS])
        ln_guess = sb("ln_guess", [P, UNITS])
        ln_newton = sb("ln_newton", [P, UNITS])

        bank = [ctx.enter_context(nc.psum_tensor(f"bank{i}", [P, 512], F32)) for i in range(4)]
        score_banks = [ctx.enter_context(nc.psum_tensor(f"score_banks{i}", [P, 2, 512], F32)) for i in range(2)]

        w1_loaded, experts_loaded = sem("w1_loaded"), sem("experts_loaded")
        tables_set, bias_split = sem("tables_set"), sem("bias_split")
        buffers = [attention_buffers(sb, layer) for layer in range(2)]
        s = locals()
        setup = loads_and_tables(nc, sb, sem, a, s)
        layers = [attention(nc, sb, sem, s, layer) for layer in range(2)]
        whole_program(nc, s, setup, layers, experts(nc, sb, sem, s, out))


def attention_shape(layer):
    if layer == 0:
        return HEADS0, D0, PAIRS0, SLOT0, P // KEYS, 0
    return HEADS1, D1, PAIRS1, SLOT1, NQB, QBLOCK


def attention_buffers(sb, layer):
    heads, d, pairs, slot, vwin, halo = attention_shape(layer)
    L = f"{layer}"
    return {
        "xnT": sb("xnT" + L, [P, 2 * T if layer == 0 else halo + T]),
        "stack": sb("stack" + L, [P, 2 * heads, slot], F16),
        "kT": sb("kT" + L, [P, TILES3, halo + (P if layer == 0 else T)], F16),
        "vals": [sb(f"vals{k}_{L}", [P, vwin, pairs, 2 * (d + 1)]) for k in range(2)],
        "ones": sb("ones" + L, [P, 1]),
        "oT": sb("oT" + L, [P, T]),
    }


def set_once_pool(pool, nc, bufs, layer, done):
    heads, d, pairs, slot, vwin, halo = attention_shape(layer)
    vd = d + 1
    stack, vals = bufs["stack"], bufs["vals"]
    start = 8 * layer
    nc.gpsimd.memset(stack[:].rearrange("p h e -> p (h e)"), 0.0).then_inc(done, 1)
    for k in range(2):
        nc.gpsimd.memset(vals[k][:], 0.0).then_inc(done, 1)
    nc.gpsimd.memset(bufs["ones"][:], 1.0).then_inc(done, 1)
    pool.wait_ge(done, start + 4)
    for k in range(2):
        for g in range(2):
            rows = slice(g * KEYS, (g + 1) * KEYS)
            nc.gpsimd.memset(vals[k][rows, :, :, g * vd + d:g * vd + d + 1], 1.0).then_inc(done, 1)
    pool.wait_ge(done, start + 8)
    if halo:
        nc.gpsimd.memset(bufs["kT"][:, :, 0:halo], 0.0).then_inc(done, 1)


def set_once_vector(v, bufs, layer):
    halo = attention_shape(layer)[-1]
    if halo:
        v.memset(bufs["xnT"][:, 0:halo], 0.0)
    v.memset(bufs["xnT"][C:P, halo:], 1.0)
    v.memset(bufs["oT"][C:P, :], 1.0)


def first_guess(act, nc, value, log, guess, ready, logged, guessed, part=0):
    act.wait_ge(*ready)
    nc.scalar.activation(log, value, ACT.Ln).then_inc(logged, 1)
    act.wait_ge(logged, part + 1)
    nc.scalar.activation(guess, log, ACT.Exp, scale=-0.5).then_inc(guessed, 1)


def newton_root(v, out, value, guess, tmp, guessed, step, part=0):
    v.wait_ge(guessed, part + 1)
    v.scalar_tensor_tensor(tmp, guess, -0.5, guess, ALU.mult, ALU.mult).then_inc(step, 1)
    v.wait_ge(step, 3 * part + 1)
    v.tensor_tensor(tmp, tmp, value, ALU.mult).then_inc(step, 1)
    v.wait_ge(step, 3 * part + 2)
    v.scalar_tensor_tensor(out, tmp, 1.5, guess, ALU.add, ALU.mult).then_inc(step, 1)
    v.wait_ge(step, 3 * part + 3)


def loads_and_tables(nc, sb, sem, a, s):
    x_all, xT_all, perm, bank, score_banks = s["x_all"], s["xT_all"], s["perm"], s["bank"], s["score_banks"]
    group_avg, gn_scale, gn_shift = s["group_avg"], s["gn_scale"], s["gn_shift"]
    minus_half, head_scale = s["minus_half"], s["head_scale"]
    ident = perm[:, 0, :]
    NREL = (2 * WIN - 1) ** 2
    stats = sb("gn_stats", [C, B, 6])
    gn_sum = sb("gn_sum", [C, 2, B])
    gn_sq = sb("gn_sq", [C, B, 2])
    gn_e2 = sb("gn_e2", [C, B, 2])
    gn_mean = sb("gn_mean", [C, 2, B])
    gn_var = sb("gn_var", [C, B])
    rel_table = sb("rel_table", [3, NREL])
    cpb_w1 = sb("cpb_w1", [3, P])
    cpb_w2 = sb("cpb_w2", [P, HEADS0])
    cpb_h = sb("cpb_h", [P, NREL])
    cpb_e = sb("cpb_e", [HEADS0, NREL])
    cpb_t = sb("cpb_t", [HEADS0, NREL])
    bias_f = sb("bias_f", [P, HEADS0, KEYS])
    win_mask = sb("win_mask", [P, 2, KEYS])
    bias_sum = sb("bias_sum", [P, 2, HEADS0 * KEYS])
    logit = sb("logit", [P, HEADS0])

    rel_dram = nc.dram_tensor("rel_scratch", (HEADS0, NREL), F32)
    col_dram = nc.dram_tensor("col_scratch", (WIN, HEADS0, 2 * WIN - 1, WIN), F32)

    x_loaded = [sem(f"x_loaded{i}") for i in range(4)]
    perm_loaded = sem("perm_loaded")
    table_loaded, mask_loaded = sem("table_loaded"), sem("mask_loaded")
    weights_loaded = sem("weights_loaded")
    xT_ready, xT_copied, stats_ready = sem("xT_ready"), sem("xT_copied"), sem("gn_stats_ready")
    gn_step, gn_group, gn_sums = sem("gn_step"), sem("gn_group"), sem("gn_sums")
    cpb_mm, cpb_relu, cpb_exp, cpb_table, table_step = (sem("cpb_mm"), sem("cpb_relu"), sem("cpb_exp"),
                                                        sem("cpb_table"), sem("table_step"))
    rel_stored, col_stored, bias_loaded = sem("rel_stored"), sem("col_stored"), sem("bias_loaded")
    half_set, weights_padded = sem("half_set"), sem("weights_padded")
    set_once, group_loaded, w_qkv1_loaded, w_proj1_loaded = (sem("set_once"), sem("group_loaded"),
                                                             sem("w_qkv1_loaded"), sem("w_proj1_loaded"))
    bias_summed, bias_rounded = sem("bias_summed"), sem("bias_rounded")
    gn_logged, gn_guessed, gn_newton_step = sem("gn_logged"), sem("gn_guessed"), sem("gn_newton_step")
    wsq = sb("wsq", [K1, 2 * C])
    ones97 = sb("ones97", [K1, P])
    wmax = sb("wmax", [P, 2])
    sprod = sb("sprod", [P, 1])
    gn_log = sb("gn_log", [C, B])
    gn_guess = sb("gn_guess", [C, B])
    gn_tmp = sb("gn_tmp", [C, B])
    fac1, exp_scale1, w_qkv1 = s["fac1"], s["exp_scale1"], s["w_qkv"][1]
    wsq_ready, wsums_ready, wscale_step, wscale_pow = (sem("wsq_ready"), sem("wsums_ready"), sem("wscale_step"),
                                                       sem("wscale_pow"))
    scale_step = sem("scale_step")
    side = 2 * WIN - 1

    def store_columns(eng, which):
        eng.wait_ge(rel_stored, 16)
        rel = rel_dram.ap().rearrange("h (r c) -> h r c", r=side)
        for ci in which:
            eng.dma_start(col_dram.ap()[ci], rel[:, :, WIN - 1 - ci:2 * WIN - 1 - ci]).then_inc(col_stored, 16)

    def load_bias(eng, which):
        eng.wait_ge(col_stored, 16 * WIN)
        cols = col_dram.ap().rearrange("i h r c -> i h (r c)")
        for row in which:
            ri, at = row % WIN, row * WIN
            eng.dma_start(bias_f[at:at + WIN, :, :],
                          cols[:, :, (WIN - 1 - ri) * WIN:(2 * WIN - 1 - ri) * WIN]).then_inc(bias_loaded, 16)

    def sync_program(sp):
        sp.dma_start(perm[:], a["permutations"]).then_inc(perm_loaded, 16)
        xv = a["x"].rearrange("b h w c -> (b h w) c").rearrange("(u p) c -> p u c", p=P)
        for i in range(4):
            part = slice(i * UNITS // 4, (i + 1) * UNITS // 4)
            sp.dma_start(x_all[:, part, :], xv[:, part, :]).then_inc(x_loaded[i], 16)
        sp.wait_ge(weights_padded, 4)
        sp.dma_start(s["w_qkv"][1][0:K1, :], a["w_qkv1"]).then_inc(w_qkv1_loaded, 16)
        sp.dma_start(s["w_qkv"][0][0:K1, :], a["w_qkv0"]).then_inc(weights_loaded, 16)
        sp.dma_start(s["w_proj"][0][0:K1, :], a["w_proj0"]).then_inc(weights_loaded, 16)
        sp.dma_start(s["w_proj"][1][0:K1, :], a["w_proj1"]).then_inc(w_proj1_loaded, 16)
        sp.dma_start(s["gate_vec"][:], a["gate_vec"]).then_inc(w_proj1_loaded, 16)
        store_columns(sp, range(0, WIN // 2))
        load_bias(sp, range(0, 16))
        sp.dma_start(s["w1"][:], a["w1"]).then_inc(s["w1_loaded"], 16)
        sp.dma_start(s["w2"][:], a["w2"]).then_inc(s["experts_loaded"], 16)
        sp.dma_start(s["w_gate"][:], a["w_gate"]).then_inc(s["experts_loaded"], 16)
        sp.dma_start(s["b2_f"][:], a["b2"].partition_broadcast(2)).then_inc(s["experts_loaded"], 16)
        sp.dma_start(s["earlier"][:], a["earlier"].partition_broadcast(P)).then_inc(s["experts_loaded"], 16)

    def gpsimd_program(pool):
        nc.gpsimd.memset(minus_half[:], -0.5).then_inc(half_set, 1)
        pool.dma_start(logit[:], a["logit_scale"].partition_broadcast(P)).then_inc(mask_loaded, 16)
        pool.dma_start(win_mask[:], a["win_mask"]).then_inc(mask_loaded, 16)
        pool.dma_start(s["band_f"][:], a["band_mask"]).then_inc(mask_loaded, 16)
        pool.wait_ge(half_set, 1)
        for layer in range(2):
            set_once_pool(pool, nc, s["buffers"][layer], layer, set_once)
        pool.wait_ge(set_once, 17)
        nc.gpsimd.memset(s["moe_hi"][C:K1, :, :].bitcast(F32), 1.0).then_inc(set_once, 1)
        nc.gpsimd.memset(s["moe_lo"][C:K1, :, :].bitcast(F32), 0.0).then_inc(set_once, 1)
        pool.wait_ge(set_once, 19)
        pool.wait_ge(wscale_step, 2)
        nc.gpsimd.tensor_tensor(fac1[:], wmax[:], minus_half[:, 0:2], ALU.pow).then_inc(wscale_pow, 1)

    def scalar_program(act):
        act.dma_start(cpb_w1[:], a["cpb_w1"]).then_inc(table_loaded, 16)
        act.dma_start(rel_table[:], a["rel_table"]).then_inc(table_loaded, 16)
        act.dma_start(cpb_w2[:], a["cpb_w2"]).then_inc(table_loaded, 16)
        act.dma_start(group_avg[:], a["group_avg"]).then_inc(group_loaded, 16)
        act.preload_act_table_set("natural_log_exp_and_others")
        act.wait_ge(cpb_mm, 1)
        nc.scalar.activation(cpb_h[:], bank[3][:, 0:NREL], ACT.Relu).then_inc(cpb_relu, 1)
        act.wait_ge(cpb_mm, 2)
        nc.scalar.activation(cpb_e[:], bank[3][0:HEADS0, 256:256 + NREL], ACT.Exp, scale=-1.0).then_inc(cpb_exp, 1)
        act.wait_ge(cpb_table, 1)
        act.dma_start(rel_dram.ap(), cpb_t[:]).then_inc(rel_stored, 16)
        store_columns(act, range(WIN // 2, WIN))
        act.wait_ge(scale_step, 1)
        nc.scalar.activation(logit[:], logit[:], ACT.Exp).then_inc(scale_step, 1)
        first_guess(act, nc, gn_var[:], gn_log[:], gn_guess[:], (gn_step, 6), gn_logged, gn_guessed)

    def scalar_bias(act, wh):
        act.wait_ge(bias_summed, wh + 1)
        nc.scalar.activation(s["bias_bf"][:, wh, :], bias_sum[:, wh, :], ACT.Copy).then_inc(bias_rounded, 1)

    def tensor_program(pe):
        pe.wait_ge(table_loaded, 16 * 3)
        nc.tensor.matmul(bank[3][:, 0:NREL], cpb_w1[:], rel_table[:], start=True, stop=True).then_inc(cpb_mm, 1)
        pe.wait_ge(cpb_relu, 1)
        nc.tensor.matmul(bank[3][0:HEADS0, 256:256 + NREL], cpb_w2[:], cpb_h[:], start=True,
                         stop=True).then_inc(cpb_mm, 1)
        pe.wait_ge(perm_loaded, 16)
        for b in range(B):
            pe.wait_ge(x_loaded[b // 4], 16)
            if b >= 2:
                pe.wait_ge(xT_copied, b - 1)
                pe.wait_ge(stats_ready, b - 1)
            h32 = KEYS // 2
            for tile, (start, width) in enumerate(((0, 5), (h32, 3))):
                places = bank[b % 2][0:C, start:start + 2 * width * h32].rearrange(
                    "c (w a t) -> c w a t", a=width, t=h32)[:, :, 0:3:2, :]
                last = pe.transpose(places, x_all[:, 2 * b + tile, :], perm[:, 1 + tile, :])
            last.then_inc(xT_ready, 1)
        pe.wait_ge(gn_sums, 1)
        pe.wait_ge(group_loaded, 16)
        nc.tensor.matmul(bank[2][0:C, 0:2 * B], group_avg[:], gn_sum[:].rearrange("c a b -> c (a b)"),
                         start=True, stop=True).then_inc(gn_group, 1)
        pe.wait_ge(wsq_ready, 1)
        nc.tensor.matmul(score_banks[0][:, 0, 0:2 * C], ones97[:], wsq[:], start=True,
                         stop=True).then_inc(wsums_ready, 1)

    def vector_program(v):
        for w in (*s["w_qkv"], *s["w_proj"]):
            v.memset(w[C:P, :], 0.0).then_inc(weights_padded, 1)
        v.memset(ones97[:], 1.0)
        for k in range(2):
            v.memset(s["moe_xT"][k][C:K1, :], 1.0)
        v.memset(s["ones2"][:].bitcast(F32), 1.0)
        for layer in range(2):
            set_once_vector(v, s["buffers"][layer], layer)
        v.wait_ge(cpb_exp, 1)
        v.tensor_scalar(cpb_e[:], cpb_e[:], 1.0, None, ALU.add).then_inc(table_step, 1)
        v.wait_ge(table_step, 1)
        v.reciprocal(cpb_t[:], cpb_e[:]).then_inc(table_step, 1)
        v.wait_ge(table_step, 2)
        v.tensor_scalar(cpb_t[:], cpb_t[:], 16.0, None, ALU.mult).then_inc(cpb_table, 1)
        for b in range(B):
            v.wait_ge(xT_ready, b + 1)
            nc.vector.tensor_copy(xT_all[:, b, :], bank[b % 2][0:C, 0:T]).then_inc(xT_copied, 1)
            nc.vector.bn_stats(stats[:, b, :], bank[b % 2][0:C, 0:T]).then_inc(stats_ready, 1)
        v.wait_ge(stats_ready, B)
        st = stats[:].rearrange("c b (e k) -> c b e k", k=3)
        v.tensor_tensor(gn_sq[:], st[:, :, :, 1], st[:, :, :, 1], ALU.mult).then_inc(gn_step, 1)
        v.wait_ge(gn_step, 1)
        v.scalar_tensor_tensor(gn_e2[:], st[:, :, :, 2], 2.0 / T, gn_sq[:], ALU.mult, ALU.add).then_inc(gn_step, 1)
        v.wait_ge(gn_step, 2)
        v.tensor_tensor(gn_sum[:, 0, :], st[:, :, 0, 1], st[:, :, 1, 1], ALU.add)
        v.tensor_tensor(gn_sum[:, 1, :], gn_e2[:, :, 0], gn_e2[:, :, 1], ALU.add).then_inc(gn_sums, 1)
        v.wait_ge(gn_group, 1)
        v.tensor_copy(gn_mean[:].rearrange("c a b -> c (a b)"), bank[2][0:C, 0:2 * B]).then_inc(gn_step, 1)
        v.wait_ge(gn_step, 3)
        v.tensor_tensor(gn_var[:], gn_mean[:, 0, :], gn_mean[:, 0, :], ALU.mult).then_inc(gn_step, 1)
        v.wait_ge(gn_step, 4)
        v.tensor_tensor(gn_var[:], gn_mean[:, 1, :], gn_var[:], ALU.subtract).then_inc(gn_step, 1)
        v.wait_ge(gn_step, 5)
        v.tensor_scalar(gn_var[:], gn_var[:], GN_EPS, None, ALU.add).then_inc(gn_step, 1)
        v.tensor_copy(s["ident_bf"][:], ident)
        v.tensor_copy(s["ident_h"][:], ident)
        v.tensor_scalar(s["ident_scaled"][:], ident, QK_SCALE0 * QK_SCALE0, None, ALU.mult)
        v.wait_ge(mask_loaded, 16 * 3)
        v.tensor_scalar(logit[:], logit[:], float(np.log(100.0)), None, ALU.min).then_inc(scale_step, 1)
        v.wait_ge(w_qkv1_loaded, 16)
        v.tensor_tensor(wsq[:], w_qkv1[0:K1, 0:2 * C], w_qkv1[0:K1, 0:2 * C], ALU.mult).then_inc(wsq_ready, 1)
        v.wait_ge(scale_step, 2)
        v.memset(head_scale[:, HEADS0:], QK_SCALE0)
        v.tensor_scalar(head_scale[:, 0:HEADS0], logit[:], QK_SCALE0, None, ALU.mult)
        newton_root(v, gn_scale[:], gn_var[:], gn_guess[:], gn_tmp[:], gn_guessed, gn_newton_step)
        v.scalar_tensor_tensor(gn_shift[:], gn_mean[:, 0, :], -1.0, gn_scale[:], ALU.mult,
                               ALU.mult).then_inc(s["tables_set"], 1)

    def vector_second_attention(v):
        v.wait_ge(wsums_ready, 1)
        v.tensor_reduce(wmax[:], score_banks[0][:, 0, 0:2 * C].rearrange("p (a c) -> p a c", a=2), AX.X,
                        ALU.max).then_inc(wscale_step, 1)
        v.tensor_copy(s["band"][:], s["band_f"][:])
        v.wait_ge(w_proj1_loaded, 32)
        v.tensor_scalar(s["w_proj"][1][0:C, :], s["w_proj"][1][0:C, :], s["gate_vec"][:, 0:1], None, ALU.mult)
        v.wait_ge(wscale_step, 1)
        v.tensor_scalar(wmax[:], wmax[:], float(K1), 1e-30, ALU.mult, ALU.max).then_inc(wscale_step, 1)

    def vector_bias_sum(v):
        v.wait_ge(bias_loaded, 16 * 2 * WIN)
        for wh in range(2):
            v.tensor_tensor(bias_sum[:, wh, :].rearrange("p (h j) -> p h j", h=HEADS0), bias_f[:],
                            win_mask[:, wh, None, :].to_broadcast([P, HEADS0, KEYS]), ALU.add).then_inc(
                                bias_summed, 1)

    def vector_bias_split(v, wh):
        v.wait_ge(bias_rounded, wh + 1)
        v.tensor_tensor(s["bias_lo"][:, wh, :], bias_sum[:, wh, :], s["bias_bf"][:, wh, :], ALU.subtract).then_inc(
            s["bias_split"], 1)

    def vector_scales(v):
        v.wait_ge(wscale_pow, 1)
        v.tensor_scalar(fac1[:], fac1[:], QK_RANGE1, None, ALU.mult).then_inc(wscale_step, 1)
        v.wait_ge(wscale_step, 3)
        v.tensor_tensor(sprod[:], fac1[:, 0:1], fac1[:, 1:2], ALU.mult).then_inc(wscale_step, 1)
        v.wait_ge(wscale_step, 4)
        v.reciprocal(exp_scale1[:], sprod[:]).then_inc(wscale_step, 1)
        v.wait_ge(wscale_step, 5)
        v.tensor_scalar(exp_scale1[:], exp_scale1[:], float(D1) ** -0.5, None, ALU.mult)

    def tables_ready(eng):
        eng.wait_ge(s["tables_set"], 1)
        eng.wait_ge(set_once, 19)

    def weights_ready(pe):
        pe.wait_ge(weights_loaded, 16 * 2)

    return {"sync": sync_program, "pool": gpsimd_program, "act": scalar_program, "pe": tensor_program,
            "dve": vector_program, "act_bias": scalar_bias, "bias_sum": vector_bias_sum,
            "bias_split": vector_bias_split, "scales": vector_scales,
            "second_attention": vector_second_attention, "tables_ready": tables_ready, "weights_ready": weights_ready}


NORM_PARTS = ((0, UNITS - 4 * PER_IMAGE), (UNITS - 4 * PER_IMAGE, UNITS))


def norm_statistics(v, s, q, part, image_done):
    u, step, P3 = slice(*NORM_PARTS[part]), q["ln_step"], 3 * part
    half, total, dif, var = s["ln_half"][:, u, :], s["ln_sum"][:, u], s["ln_dif"][:, u], s["ln_var"][:, u]
    v.wait_ge(image_done, NORM_PARTS[part][1] // PER_IMAGE)
    v.tensor_tensor(total, half[:, :, 1], half[:, :, 4], ALU.add)
    v.tensor_tensor(dif, half[:, :, 1], half[:, :, 4], ALU.subtract)
    v.tensor_tensor(var, half[:, :, 2], half[:, :, 5], ALU.add).then_inc(step, 1)
    v.wait_ge(step, P3 + 1)
    v.tensor_scalar(s["ln_mean"][:, u], total, 0.5, None, ALU.mult)
    v.scalar_tensor_tensor(dif, dif, 0.25, dif, ALU.mult, ALU.mult)
    v.tensor_scalar(var, var, 1.0 / C, LN_EPS, ALU.mult, ALU.add).then_inc(step, 1)
    v.wait_ge(step, P3 + 2)
    v.tensor_tensor(var, var, dif, ALU.add).then_inc(step, 1)


def norm_guess(act, nc, s, q, part):
    u = slice(*NORM_PARTS[part])
    first_guess(act, nc, s["ln_var"][:, u], s["ln_log"][:, u], s["ln_guess"][:, u], (q["ln_step"], 3 * part + 3),
                q["ln_logged"], q["ln_guessed"], part)


def norm_root(v, s, q, part):
    u = slice(*NORM_PARTS[part])
    newton_root(v, s["ln_rstd"][:, u], s["ln_var"][:, u], s["ln_guess"][:, u], s["ln_newton"][:, u], q["ln_guessed"],
                q["ln_newton_step"], part)


def at_least(eng, semaphore, count):
    if not (isinstance(count, int) and count <= 0):
        eng.wait_ge(semaphore, count)


def attention(nc, sb, sem, s, layer):
    first = layer == 0
    L = f"{layer}"
    heads, d, pairs, slot = (HEADS0, D0, PAIRS0, SLOT0) if first else (HEADS1, D1, PAIRS1, SLOT1)
    vwin = 2 if first else NQB
    vstep = KEYS if first else QBLOCK
    vd = d + 1
    cols = heads * KEYS
    half = cols // 2
    qrows = KEYS if first else QBLOCK
    halo = 0 if first else QBLOCK

    x_all, bank, score_banks = s["x_all"], s["bank"], s["score_banks"]
    w_qkv, w_proj = s["w_qkv"][layer], s["w_proj"][layer]
    perm, ident, ident_bf, ident_h = s["perm"], s["ident"], s["ident_bf"], s["ident_h"]

    bufs = s["buffers"][layer]
    xnT, stack, kT, vals, ones, oT = (bufs[n] for n in ("xnT", "stack", "kT", "vals", "ones", "oT"))
    sq = sb("sq" + L, [P, 2 * C])
    sumsq = sb("sumsq" + L, [P, 2 * heads])
    log_sum = sb("log_sum" + L, [P, 2 * heads])
    guess = sb("guess" + L, [P, 2 * heads])
    guess_scaled = sb("guess_scaled" + L, [P, 2 * heads])
    newton = sb("newton" + L, [P, 2 * heads])
    rnorm = sb("rnorm" + L, [P, 2 * heads])
    qk = sb("qk" + L, [P, 2 * heads, d])
    qT = sb("qT" + L, [P, TILES3, P], F16)
    negmax = sb("negmax" + L, [P, heads], BF16)
    probs = sb("probs" + L, [P, cols])
    probsT = sb("probsT" + L, [P, pairs, P])
    rsum = sb("rsum" + L, [P, heads])
    o_tm = sb("o_tm" + L, [P, PER_IMAGE, C])
    x_new = sb("x_new" + L, [P, PER_IMAGE, C])
    stat6 = sb("stat6" + L, [P, PER_IMAGE, 6])
    xn_tm = sb("xn_tm" + L, [P, PER_IMAGE, C])

    qk_bank, v_bank, t_bank, o_bank = bank
    stackT_ps = t_bank[:].bitcast(F16)
    OT_AT = 128

    pair_of = [2 * (i % TILES3) + i // TILES3 for i in range(pairs)] if first else list(range(pairs))

    names = ("xn_ready", "xnT_ps", "xnT_ready", "qk_proj_ready", "v_proj_ready", "squares_ready", "squares_summed",
             "sumsq_ready", "log_ready", "guess_ready", "newton_step", "rnorm_ready", "qk_ready", "q_hi", "k_hi",
             "stack_ready", "stackT_ready", "qkT_ready", "v_ready", "row_group_done", "scores_ready",
             "negmax_ready", "shifted_ready", "probs_ready", "probsT_ready", "probsT_copied_a", "probsT_copied_b",
             "pv_ready", "rsum_ready", "o_ready", "oT_ready", "oT_copied", "proj_out_ready", "x_ready", "bn_ready",
             "stat_ready", "ln_step", "ln_logged", "ln_guessed", "ln_newton_step", "w1_split", "b2_split")
    q = {n: sem(n + L) for n in names}

    def on(n):
        return not isinstance(n, int) or 0 <= n < UNITS

    def pe_stacks(pe, n):
        if on(n + 1):
            at_least(pe, q["stack_ready"], n + 2)
            st = stack[:].rearrange("p h e -> p (h e)")
            for t in range(2 * TILES3):
                last = pe.transpose(stackT_ps[:, t * P:(t + 1) * P], st[:, t * P:(t + 1) * P], ident_h[:])
            last.then_inc(q["stackT_ready"], 1)

    def pe_scores(pe, n, b, k):
        S = score_banks[k]
        if on(n):
            if not first and k == 0 and on(n + 2):
                at_least(pe, q["xnT_ready"], b + 2)
            at_least(pe, q["qkT_ready"], n + 1)
            for i, g in enumerate((0, 2, 1, 3) if first else (0, 1)):
                g2 = g // 2 if first else g
                Sg = S[:, g2, 0:half]
                if first and i < 2:
                    pe.matmul(Sg, s["ident_scaled"][:], s["bias_bf"][:, k, g2 * half:(g2 + 1) * half],
                              start=True, stop=False, skip_group_check=True)
                    pe.matmul(Sg, s["ident_scaled"][:], s["bias_lo"][:, k, g2 * half:(g2 + 1) * half],
                              start=False, stop=False, skip_group_check=True)
                if not first:
                    pe.matmul(Sg.rearrange("p (t j) -> p t j", t=TILES3), ident_bf[:],
                              s["band"][:, k, None, :].to_broadcast([P, TILES3, KEYS]),
                              start=True, stop=False, skip_group_check=True)
                if i >= 2:
                    at_least(pe, q["row_group_done"], 2 * n + i - 1)
                for t in range(TILES3):
                    for w in range(P // qrows):
                        rows = slice(slot * g, slot * (g + 1))
                        at = (t * 2 + g % 2) * KEYS if first else t * KEYS
                        k0 = w * KEYS if first else k * P + w * QBLOCK
                        last = pe.matmul(S[w * qrows:(w + 1) * qrows, g2, at:at + KEYS],
                                         qT[rows, t, w * qrows:(w + 1) * qrows], kT[rows, t, k0:k0 + KEYS],
                                         start=False, stop=True, skip_group_check=True)
                if first and i < 2:
                    last.then_inc(q["row_group_done"], 1)
            last.then_inc(q["scores_ready"], 1)

    def pe_values(pe, n, b, k):
        if on(n - 1):
            at_least(pe, q["probsT_copied_a"], n)
            if first:
                at_least(pe, q["probsT_copied_b"], n)
            at_least(pe, q["v_ready"], n)
            at_least(pe, q["o_ready"], n - 1)
            if k == 0:
                at_least(pe, q["x_ready"], b - 1)
            else:
                at_least(pe, q["oT_copied"], b)
            for h2 in range(pairs):
                for w in range(P // qrows):
                    rows = slice(w * qrows, (w + 1) * qrows)
                    last = pe.matmul(o_bank[rows, pair_of[h2] * 2 * vd:(pair_of[h2] + 1) * 2 * vd],
                                     probsT[:, h2, rows], vals[(k + 1) % 2][:, w, pair_of[h2], :],
                                     start=True, stop=True)
            last.then_inc(q["pv_ready"], 1)

    def pe_project_qk(pe, n, b, k, x):
        if on(n + 2):
            at = halo + k * P
            if k == 0 and (first or not on(n)):
                at_least(pe, q["xnT_ready"], b + 2)
            at_least(pe, q["qk_ready"], n + 2)
            pe.matmul(qk_bank[:, 0:2 * C], x[:, at:at + P], w_qkv[:, 0:2 * C], start=True,
                      stop=True).then_inc(q["qk_proj_ready"], 1)

    def pe_shift(pe, n, k):
        if on(n):
            at_least(pe, q["negmax_ready"], n + 1)
            for g2 in range(2):
                Sg = score_banks[k][:, g2, 0:half].rearrange("p (h j) -> p h j", j=KEYS)
                last = pe.matmul(Sg, ident_bf[:],
                                 negmax[:, g2 * heads // 2:(g2 + 1) * heads // 2, None].to_broadcast(
                                     [P, heads // 2, KEYS]), start=False, stop=True, skip_group_check=True)
            last.then_inc(q["shifted_ready"], 1)

    def pe_project_v(pe, u, k, x):
        if on(u):
            at_least(pe, q["v_ready"], u)
            base = k * P
            for w in range(vwin // 2):
                at = base + w * vstep
                pe.matmul(v_bank[:, w * C:(w + 1) * C], x[:, at:at + P], w_qkv[:, 2 * C:3 * C],
                          start=True, stop=True)
                far = w + vwin // 2
                pe.matmul(v_bank[0:KEYS, far * C:(far + 1) * C], x[:, at + KEYS:at + 2 * KEYS],
                          w_qkv[:, 2 * C:3 * C], start=True, stop=True)
                last = pe.matmul(v_bank[KEYS:P, far * C:(far + 1) * C], x[:, at:at + KEYS],
                                 w_qkv[:, 2 * C:3 * C], start=True, stop=True)
            last.then_inc(q["v_proj_ready"], 1)

    def pe_output_transpose(pe, u, b):
        if on(u - 1):
            at_least(pe, q["o_ready"], u)
            to = o_bank[0:C, OT_AT:OT_AT + T]
            if first:
                pe.transpose(to[:, 64:192], o_tm[:, 0, :], perm[:, 3, :])
                wrap = to.rearrange("c (a t) -> c a t", a=4)[:, 0:4:3, :]
                last = pe.transpose(wrap, o_tm[:, 1, :], perm[:, 4, :])
            else:
                pe.transpose(to[:, 0:P], o_tm[:, 0, :], ident)
                last = pe.transpose(to[:, P:T], o_tm[:, 1, :], ident)
            last.then_inc(q["oT_ready"], 1)

    def pe_output_project(pe, u, b):
        if on(u - 3):
            at_least(pe, q["oT_copied"], b)
            at_least(pe, q["o_ready"], u if not isinstance(u, int) or u <= UNITS else UNITS)
            for i in range(PER_IMAGE):
                last = pe.matmul(o_bank[:, OT_AT + i * C:OT_AT + (i + 1) * C], oT[:, i * P:(i + 1) * P], w_proj[:],
                                 start=True, stop=True)
            last.then_inc(q["proj_out_ready"], 1)

    def pe_probs_transpose(pe, u, k):
        if on(u):
            at_least(pe, q["probs_ready"], u + 1)
            for i in range(pairs):
                to = score_banks[k][:, i // TILES3, (i % TILES3) * P:(i % TILES3 + 1) * P]
                last = pe.transpose(to, probs[:, i * P:(i + 1) * P], ident)
            last.then_inc(q["probsT_ready"], 1)

    def pe_step(pe, b, k, odd):
        n = 2 * b + k
        pe_scores(pe, n, b, k)
        if first:
            pe_project_qk(pe, n, b, k, xnT[:, (1 - odd) * T:(2 - odd) * T])
            if k == 0:
                pe_output_project(pe, n - 1, b - 1)
            else:
                pe_output_transpose(pe, n - 1, b)
            pe_probs_transpose(pe, n - 1, 1 - k)
            pe_stacks(pe, n)
            slot_v = odd if k == 0 else 1 - odd
            pe_project_v(pe, n + 1, 1 - k, xnT[:, slot_v * T:(slot_v + 1) * T])
            pe_shift(pe, n, k)
            pe_values(pe, n, b, k)
            return
        pe_values(pe, n, b, k)
        pe_project_qk(pe, n, b, k, xnT)
        pe_shift(pe, n, k)
        pe_stacks(pe, n)
        pe_project_v(pe, n + 2, k, xnT)
        if k == 1 and on(n + 3):
            at_least(pe, q["xn_ready"], b + 3)
            for i in range(PER_IMAGE):
                last = pe.transpose(score_banks[0][0:C, i, half:half + P], xn_tm[:, i, :], ident)
            last.then_inc(q["xnT_ps"], 1)
        if k == 0:
            pe_output_transpose(pe, n, b)
        else:
            pe_output_project(pe, n, b)
        pe_probs_transpose(pe, n, k)

    def act_values(act, n, k):
        if on(n + 1):
            at_least(act, q["v_proj_ready"], n + 2)
            at_least(act, q["pv_ready"], n)
            to = vals[(k + 1) % 2]
            src = v_bank[:, 0:vwin * C].rearrange("p (w t e) -> p w t e", w=vwin, e=2 * d)
            near, far = slice(0, vwin // 2), slice(vwin // 2, vwin)
            nc.scalar.activation(to[0:KEYS, :, :, 0:d], src[0:KEYS, :, :, 0:d], ACT.Copy)
            nc.scalar.activation(to[KEYS:P, near, :, vd:vd + d], src[KEYS:P, far, :, d:2 * d], ACT.Copy)
            last = nc.scalar.activation(to[KEYS:P, far, :, vd:vd + d], src[KEYS:P, near, :, d:2 * d], ACT.Copy)
            last.then_inc(q["v_ready"], 1)

    def act_squares(act, n):
        if on(n + 2):
            at_least(act, q["qk_proj_ready"], n + 3)
            at_least(act, q["sumsq_ready"], n + 2)
            nc.scalar.activation(sq[:], qk_bank[:, 0:2 * C], ACT.Square).then_inc(q["squares_ready"], 1)

    def act_exp(act, n, k):
        if on(n):
            at_least(act, q["shifted_ready"], n + 1)
            if first:
                nc.scalar.activation(probs[:].rearrange("p (g c) -> p g c", g=2), score_banks[k][:, :, 0:half],
                                     ACT.Exp, scale=1.0 / (QK_SCALE0 * QK_SCALE0)).then_inc(q["probs_ready"], 1)
            else:
                nc.scalar.activation(probs[:].rearrange("p (t g j) -> p g t j", g=2, j=KEYS),
                                     score_banks[k][:, :, 0:half].rearrange("p g (t j) -> p g t j", j=KEYS),
                                     ACT.Exp, scale=s["exp_scale1"][:, 0:1]).then_inc(q["probs_ready"], 1)

    def act_transposed_stacks(act, n, k):
        if on(n + 1):
            at_least(act, q["stackT_ready"], n + 2)
            st = stackT_ps.rearrange("p (t e) -> p t e", e=P)
            kcol = 0 if first else halo + ((k + 1) % 2) * P
            nc.scalar.activation(qT[:], st[:, 0:TILES3, :], ACT.Copy)
            nc.scalar.activation(kT[:, :, kcol:kcol + P], st[:, TILES3:2 * TILES3, :],
                                 ACT.Copy).then_inc(q["qkT_ready"], 1)

    def act_norm_guess(act, n):
        if on(n + 2):
            at_least(act, q["sumsq_ready"], n + 3)
            at_least(act, q["rnorm_ready"], n + 2)
            nc.scalar.activation(log_sum[:], sumsq[:], ACT.Ln).then_inc(q["log_ready"], 1)
            at_least(act, q["log_ready"], n + 3)
            nc.scalar.activation(guess[:], log_sum[:], ACT.Exp, scale=-0.5).then_inc(q["guess_ready"], 1)

    def act_copy_probs(act, u, k):
        if on(u):
            at_least(act, q["probsT_ready"], u + 1)
            if first:
                nc.scalar.activation(probsT[:, 0:TILES3, :].rearrange("p t e -> p (t e)"),
                                     score_banks[k][:, 0, 0:TILES3 * P], ACT.Copy).then_inc(q["probsT_copied_a"], 1)
            else:
                nc.scalar.activation(probsT[:].rearrange("p t e -> p (t e)"),
                                     score_banks[k][:, 0, 0:TILES3 * P], ACT.Copy).then_inc(q["probsT_copied_a"], 1)

    def act_step(act, b, k, odd):
        n = 2 * b + k
        if first:
            act_squares(act, n)
            act_copy_probs(act, n - 1, 1 - k)
            act_transposed_stacks(act, n, k)
            act_norm_guess(act, n)
            act_exp(act, n, k)
            act_values(act, n, k)
            act_stacks(act, n)
            return
        act_values(act, n, k)
        act_exp(act, n, k)
        act_transposed_stacks(act, n, k)
        act_stacks(act, n)
        act_copy_probs(act, n, k)

    def dve_max(v, n, k):
        if on(n):
            at_least(v, q["scores_ready"], n + 1)
            v.tensor_reduce(negmax[:].rearrange("p (g h) -> p g h", g=2),
                            score_banks[k][:, :, 0:half].rearrange("p g (h j) -> p g h j", j=KEYS), AX.X, ALU.max,
                            negate=True).then_inc(q["negmax_ready"], 1)

    def dve_divide(v, n, b, k):
        if on(n - 1):
            at_least(v, q["pv_ready"], n)
            pv = o_bank[:, 0:heads * vd].rearrange("p (h e) -> p h e", e=vd)
            v.reciprocal(rsum[:], pv[:, :, d]).then_inc(q["rsum_ready"], 1)
            at_least(v, q["rsum_ready"], n)
            at_least(v, q["oT_ready"], b - 1 if k == 0 else b)
            v.tensor_tensor(o_tm[:, (k + 1) % 2, :].rearrange("p (h e) -> p h e", e=d), pv[:, :, 0:d],
                            rsum[:, :, None].to_broadcast([P, heads, d]), ALU.mult).then_inc(q["o_ready"], 1)

    def dve_statistics(v, n, b):
        if on(n - 4):
            at_least(v, q["x_ready"], b - 1)
            for i in range(PER_IMAGE):
                last = v.bn_stats(stat6[:, i, :], x_new[:, i, :])
            last.then_inc(q["bn_ready"], 1)
            img = bass.ds(2 * (b - 2), PER_IMAGE)
            v.tensor_scalar(x_all[:, img, :], x_new[:], 1.0, None, ALU.mult)
            at_least(v, q["bn_ready"], b - 1)
            v.tensor_scalar(s["ln_half"][:, img, :], stat6[:], 1.0, None, ALU.mult).then_inc(q["stat_ready"], 1)

    def dve_residual(v, u, b):
        if on(u - 3):
            at_least(v, q["proj_out_ready"], b)
            img = bass.ds(2 * (b - 1), PER_IMAGE)
            v.tensor_tensor(x_new[:], x_all[:, img, :],
                            o_bank[:, OT_AT:OT_AT + 2 * C].rearrange("p (i c) -> p i c", i=PER_IMAGE),
                            ALU.add).then_inc(q["x_ready"], 1)

    def dve_output(v, u, b):
        if on(u - 1):
            at_least(v, q["oT_ready"], b)
            at_least(v, q["proj_out_ready"], b - 1)
            v.tensor_copy(oT[0:C, :], o_bank[0:C, OT_AT:OT_AT + T]).then_inc(q["oT_copied"], 1)

    def dve_sum_squares(v, n):
        if on(n + 2):
            at_least(v, q["squares_ready"], n + 3)
            v.tensor_reduce(sumsq[:], sq[:].rearrange("p (h e) -> p h e", e=d), AX.X,
                            ALU.add).then_inc(q["squares_summed"], 1)

    def dve_bound_squares(v, n):
        if on(n + 2):
            at_least(v, q["squares_summed"], n + 3)
            v.tensor_scalar(sumsq[:], sumsq[:], 1e-24, None, ALU.max).then_inc(q["sumsq_ready"], 1)

    def dve_scale(v, n):
        if on(n + 2):
            at_least(v, q["guess_ready"], n + 3)
            v.scalar_tensor_tensor(newton[:], guess[:], -0.5, guess[:], ALU.mult,
                                   ALU.mult).then_inc(q["newton_step"], 1)
            v.tensor_tensor(guess_scaled[:], guess[:], s["head_scale"][:], ALU.mult)
            at_least(v, q["newton_step"], 2 * n + 5)
            v.tensor_tensor(newton[:], newton[:], sumsq[:], ALU.mult).then_inc(q["newton_step"], 1)
            at_least(v, q["newton_step"], 2 * n + 6)
            v.scalar_tensor_tensor(rnorm[:], newton[:], 1.5, guess_scaled[:], ALU.add,
                                   ALU.mult).then_inc(q["rnorm_ready"], 1)
            at_least(v, q["stack_ready"], n + 2)
            at_least(v, q["rnorm_ready"], n + 3)
            v.tensor_tensor(qk[:], qk_bank[:, 0:2 * C].rearrange("p (h e) -> p h e", e=d),
                            rnorm[:, :, None].to_broadcast([P, 2 * heads, d]), ALU.mult).then_inc(q["qk_ready"], 1)

    def dve_step(v, b, k, odd):
        n = 2 * b + k
        dve_max(v, n, k)
        if first:
            dve_sum_squares(v, n)
            if on(n - 1):
                at_least(v, q["probsT_ready"], n)
                v.tensor_copy(probsT[:, TILES3:, :].rearrange("p t e -> p (t e)"),
                              score_banks[1 - k][:, 1, 0:TILES3 * P]).then_inc(q["probsT_copied_b"], 1)
            if k == 0:
                dve_residual(v, n - 1, b - 1)
                dve_bound_squares(v, n)
                dve_statistics(v, n, b)
            else:
                dve_output(v, n - 1, b)
                dve_bound_squares(v, n)
                if on(n + 3):
                    at_least(v, q["v_proj_ready"], n + 1)
                    v.tensor_scalar(xnT[0:C, odd * T:(odd + 1) * T], s["xT_all"][:, b + 2, :],
                                    s["gn_scale"][:, bass.ds(b + 2, 1)], s["gn_shift"][:, bass.ds(b + 2, 1)],
                                    ALU.mult, ALU.add).then_inc(q["xnT_ready"], 1)
            dve_scale(v, n)
            dve_divide(v, n, b, k)
            return
        if on(n + 2):
            at_least(v, q["stack_ready"], n + 2)
            at_least(v, q["qk_proj_ready"], n + 3)
            v.tensor_tensor(qk[:].rearrange("p (a h) e -> p a (h e)", a=2),
                            qk_bank[:, 0:2 * C].rearrange("p (a e) -> p a e", a=2),
                            s["fac1"][:, :, None].to_broadcast([P, 2, C]), ALU.mult).then_inc(q["qk_ready"], 1)
        dve_divide(v, n, b, k)
        if k == 0:
            dve_statistics(v, n, b)
        if k == 1 and on(n + 3):
            at_least(v, q["v_proj_ready"], n + 3)
            at_least(v, q["xnT_ps"], b + 3)
            v.tensor_copy(xnT[0:C, halo:].rearrange("c (i t) -> c i t", i=PER_IMAGE),
                          score_banks[0][0:C, :, half:half + P]).then_inc(q["xnT_ready"], 1)
        if k == 1:
            dve_residual(v, n, b)
        else:
            dve_output(v, n, b)
        if k == 0 and on(n + 4):
            normalise(v, b + 2)

    def normalise(v, img):
        at_least(v, q["xnT_ps"], img)
        for i in range(PER_IMAGE):
            u = 2 * img + i
            last = v.tensor_scalar(xn_tm[:, i, :], x_all[:, u, :], s["ln_mean"][:, bass.ds(u, 1)],
                                   s["ln_rstd"][:, bass.ds(u, 1)],
                                   ALU.subtract, ALU.mult)
        last.then_inc(q["xn_ready"], 1)

    ahead = 2

    def act_stacks(act, n):
        if on(n + ahead):
            at_least(act, q["qk_ready"], n + ahead + 1)
            at_least(act, q["stackT_ready"], n + ahead)
            nc.scalar.activation(stack[:, heads:, 0:2 * d].rearrange("p h (e d) -> p h e d", d=d),
                                 qk[:, heads:, None, :].to_broadcast([P, heads, 2, d]), ACT.Copy).then_inc(q["k_hi"], 1)

    def pool_step(pool, b, k, odd):
        n = 2 * b + k
        if on(n + ahead):
            at_least(pool, q["qk_ready"], n + ahead + 1)
            at_least(pool, q["stackT_ready"], n + ahead)
            nc.gpsimd.tensor_tensor(stack[:, 0:heads, 0:3 * d].rearrange("p h (e d) -> p h e d", d=d)[:, :, 0:3:2, :],
                                    qk[:, 0:heads, None, :].to_broadcast([P, heads, 2, d]),
                                    ones[:, 0:1, None, None].to_broadcast([P, heads, 2, d]),
                                    ALU.mult).then_inc(q["q_hi"], 1)
            at_least(pool, q["q_hi"], n + ahead + 1)
            nc.gpsimd.tensor_tensor(stack[:, 0:heads, d:2 * d], qk[:, 0:heads, :], stack[:, 0:heads, 0:d], ALU.subtract)
            at_least(pool, q["k_hi"], n + ahead + 1)
            nc.gpsimd.tensor_tensor(stack[:, heads:, 2 * d:3 * d], qk[:, heads:, :], stack[:, heads:, 0:d],
                                    ALU.subtract).then_inc(q["stack_ready"], 1)

    return {"pe": pe_step, "act": act_step, "dve": dve_step, "pool": pool_step, "normalise": normalise, "q": q}


def steps(eng, step, first, end):
    for n in range(first, end):
        step(eng, n // 2, n % 2, n // 2 % 2)


def middle_steps(eng, step):
    with eng.Fori(1, (B - 2) // 2) as i:
        for odd in range(2):
            step(eng, 2 * i + odd, 0, odd)
            step(eng, 2 * i + odd, 1, odd)


def whole_program(nc, s, setup, layers, moe):
    a0, a1 = layers
    q0, q1, qm = a0["q"], a1["q"], moe["q"]
    N = UNITS

    w1_split = q0["w1_split"]

    with nc.Block() as block:
        @block.gpsimd
        def _(pool):
            setup["pool"](pool)
            setup["tables_ready"](pool)
            steps(pool, a0["pool"], -2, 4)
            middle_steps(pool, a0["pool"])
            steps(pool, a0["pool"], N - 4, N - 2)
            pool.wait_ge(w1_split, 1)
            nc.gpsimd.tensor_tensor(s["w1_lo"][:], s["w1"][:], s["w1_hi"][:], ALU.subtract).then_inc(w1_split, 1)
            pool.wait_ge(w1_split, 2)
            pool.wait_ge(s["experts_loaded"], 16 * 4)
            split_expert_bias(pool, nc, s, q0["b2_split"])
            steps(pool, a1["pool"], -3, 4)
            middle_steps(pool, a1["pool"])
            steps(pool, a1["pool"], N - 4, N)
            moe["pool"](pool)

        @block.sync
        def _(sp):
            setup["sync"](sp)
            moe["sync"](sp)

        @block.vector
        def _(v):
            setup["dve"](v)
            setup["tables_ready"](v)
            steps(v, a0["dve"], -3, -2)
            setup["second_attention"](v)
            steps(v, a0["dve"], -2, -1)
            setup["bias_sum"](v)
            setup["bias_split"](v, 0)
            steps(v, a0["dve"], -1, 0)
            setup["bias_split"](v, 1)
            steps(v, a0["dve"], 0, 4)
            setup["scales"](v)
            middle_steps(v, a0["dve"])
            norm_statistics(v, s, q1, 0, q0["stat_ready"])
            steps(v, a0["dve"], N - 4, N - 2)
            norm_root(v, s, q1, 0)
            a1["normalise"](v, 0)
            steps(v, a0["dve"], N - 2, N)
            for i in range(3):
                steps(v, a1["dve"], i - 3, i - 2)
                steps(v, a0["dve"], N + i, N + i + 1)
            norm_statistics(v, s, q1, 1, q0["stat_ready"])
            steps(v, a1["dve"], 0, 2)
            norm_root(v, s, q1, 1)
            steps(v, a1["dve"], 2, 4)
            middle_steps(v, a1["dve"])
            norm_statistics(v, s, qm, 0, q1["stat_ready"])
            steps(v, a1["dve"], N - 4, N - 3)
            norm_root(v, s, qm, 0)
            moe["normalise"](v, 0)
            steps(v, a1["dve"], N - 3, N - 2)
            moe["normalise"](v, 1)
            steps(v, a1["dve"], N - 2, N - 1)
            moe["dve_inputs"](v, 0)
            steps(v, a1["dve"], N - 1, N)
            moe["dve_inputs"](v, 1)
            steps(v, a1["dve"], N, N + 3)
            norm_statistics(v, s, qm, 1, q1["stat_ready"])
            moe["dve_gates"](v, 0)
            norm_root(v, s, qm, 1)
            moe["dve"](v)

        @block.scalar
        def _(act):
            setup["act"](act)
            setup["tables_ready"](act)
            steps(act, a0["act"], -2, -1)
            setup["act_bias"](act, 0)
            steps(act, a0["act"], -1, 0)
            setup["act_bias"](act, 1)
            steps(act, a0["act"], 0, 4)
            act.wait_ge(s["w1_loaded"], 16)
            nc.scalar.activation(s["w1_hi"][:], s["w1"][:], ACT.Copy).then_inc(w1_split, 1)
            middle_steps(act, a0["act"])
            steps(act, a0["act"], N - 4, N - 3)
            norm_guess(act, nc, s, q1, 0)
            steps(act, a0["act"], N - 3, N + 1)
            steps(act, a1["act"], -3, 1)
            norm_guess(act, nc, s, q1, 1)
            steps(act, a1["act"], 1, 4)
            middle_steps(act, a1["act"])
            norm_guess(act, nc, s, qm, 0)
            steps(act, a1["act"], N - 4, N - 1)
            moe["act_inputs"](act, 0)
            steps(act, a1["act"], N - 1, N)
            moe["act_inputs"](act, 1)
            moe["act"](act)

        @block.tensor
        def _(pe):
            setup["pe"](pe)
            setup["tables_ready"](pe)
            setup["weights_ready"](pe)
            steps(pe, a0["pe"], -2, 0)
            for n in range(2):
                pe.wait_ge(s["bias_split"], n + 1)
                steps(pe, a0["pe"], n, n + 1)
            steps(pe, a0["pe"], 2, 4)
            middle_steps(pe, a0["pe"])
            steps(pe, a0["pe"], N - 4, N)
            steps(pe, a1["pe"], -3, -2)
            steps(pe, a0["pe"], N, N + 1)
            pe.wait_ge(q0["qk_ready"], N)
            pe.wait_ge(q0["v_ready"], N)
            steps(pe, a1["pe"], -2, -1)
            steps(pe, a0["pe"], N + 1, N + 2)
            steps(pe, a1["pe"], -1, 0)
            steps(pe, a0["pe"], N + 2, N + 3)
            steps(pe, a1["pe"], 0, 1)
            pe.wait_ge(q0["x_ready"], B)
            steps(pe, a1["pe"], 1, 4)
            middle_steps(pe, a1["pe"])
            steps(pe, a1["pe"], N - 4, N - 1)
            pe.wait_ge(q1["qk_ready"], N)
            moe["pe_inputs"](pe, 0)
            steps(pe, a1["pe"], N - 1, N)
            moe["pe_inputs"](pe, 1)
            pe.wait_ge(q1["v_ready"], N)
            pe.wait_ge(s["experts_loaded"], 16 * 4)
            moe["pe_gates"](pe, 0)
            steps(pe, a1["pe"], N, N + 1)
            moe["pe_gates"](pe, 1)
            steps(pe, a1["pe"], N + 1, N + 2)
            pe.wait_ge(q1["x_ready"], B)
            moe["pe"](pe)


def split_expert_bias(pool, nc, s, step):
    ident, hi, lo = s["ident"], s["b2_hi"][:], s["b2_lo"][:]
    nc.gpsimd.tensor_copy(hi, s["b2_f"][:]).then_inc(step, 1)
    pool.wait_ge(step, 1)
    nc.gpsimd.tensor_tensor(lo, s["b2_f"][:], hi, ALU.subtract).then_inc(step, 1)
    pool.wait_ge(step, 2)
    nc.gpsimd.tensor_scalar(hi, hi, ident[0:2, 0:1], None, ALU.mult).then_inc(step, 1)
    nc.gpsimd.tensor_scalar(lo, lo, ident[0:2, 1:2], None, ALU.mult).then_inc(step, 1)
    pool.wait_ge(step, 4)
    nc.gpsimd.tensor_tensor(s["b2_rows"][:].rearrange("p e c -> p (e c)"), hi, lo, ALU.add).then_inc(step, 1)
    pool.wait_ge(step, 5)


def experts(nc, sb, sem, s, out):
    HBUF = 3
    LAG = 2
    x_all, bank, score_banks = s["x_all"], s["bank"], s["score_banks"]
    ident = s["ident"]
    w1_hi, w1_lo, w2, w_gate = (s[n] for n in ("w1_hi", "w1_lo", "w2", "w_gate"))
    b2_rows, ones2, xT_hi, xT_lo = (s[n] for n in ("b2_rows", "ones2", "moe_hi", "moe_lo"))
    earlier = s["earlier"]
    xn = [sb(f"moe_xn{k}", [P, CT, C]) for k in range(2)]
    hidden = [sb(f"hidden{i}", [P, CHUNK]) for i in range(HBUF)]
    xT = s["moe_xT"]
    acc = [sb(f"acc{k}", [P, CT, C]) for k in range(2)]
    gates = sb("gates", [P, UNITS, EXPERTS])
    pe_ = sb("gate_exp", [P, UNITS, EXPERTS])
    shifted = sb("gate_shifted", [P, UNITS, EXPERTS])
    gmax = sb("gate_max", [P, UNITS])
    above = sb("gate_above", [P, UNITS, EXPERTS, EXPERTS])
    tied = sb("gate_tied", [P, UNITS, EXPERTS, EXPERTS])
    rank = sb("gate_rank", [P, UNITS, EXPERTS])
    gsum = sb("gate_sum", [P, UNITS])
    h_bank = [score_banks[0][:, 0, :], score_banks[0][:, 1, :], bank[3][:]]
    y_bank = [score_banks[1][:, 0, :], score_banks[1][:, 1, :]]
    x_bank, g_bank = [bank[0], bank[2]], bank[1]
    out_v = out.rearrange("b h w c -> (b h w) c").rearrange("(u p) c -> p u c", p=P)
    BATCHES = ((0, 2), (2, CHUNKS))

    names = ("ln_step", "ln_logged", "ln_guessed", "ln_newton_step", "xn_ready", "xn_pool_ready", "xT_ps",
             "xhi_ready", "xlo_ready",
             "scores", "gate_step", "gate_exp", "gates_ready", "hidden_ps", "hidden_ready", "hidden_used",
             "y_used")
    q = {n: sem("moe_" + n) for n in names}
    stored = [sem(f"moe_stored{k}") for k in range(2)]
    GSTEPS = 12

    def inputs_at(c, m):
        return 2 + 3 * c + (m - 2) // 3 if isinstance(c, int) and c < 2 and m in (2, 5, 8) else None

    def gates_at(c, m):
        return inputs_at(c, m - 2)

    def pe_inputs(pe, c):
        if c < 2:
            pe.wait_ge(q["xn_ready"], c + 1)
        else:
            pe.wait_ge(q["xn_pool_ready"], c - 1)
            pe.wait_ge(q["xlo_ready"], c - 1)
        for j in range(CT):
            last = pe.transpose(x_bank[c % 2][0:C, j * P:(j + 1) * P], xn[c % 2][:, j, :], ident)
        last.then_inc(q["xT_ps"], 1)

    def pe_gates(pe, c):
        pe.wait_ge(q["xlo_ready"], c + 1)
        if c == BATCHES[1][0]:
            pe.wait_ge(q["gate_step"], 2)
        for j in range(CT):
            u = CT * c + j
            to = g_bank[:, u * EXPERTS:(u + 1) * EXPERTS]
            last = pe.matmul(to, xT[c % 2][:, j * P:(j + 1) * P], w_gate[:], start=True, stop=True)
        last.then_inc(q["scores"], 1)

    def pe_first(pe, c, m):
        w = slice(m * P, (m + 1) * P)
        pe.matmul(h_bank[m % HBUF], w1_hi[:, w], xT_hi[:, c, :], start=True, stop=False)
        pe.matmul(h_bank[m % HBUF], w1_hi[:, w], xT_lo[:, c, :], start=False, stop=False)
        pe.matmul(h_bank[m % HBUF], w1_lo[:, w], xT_hi[:, c, :], start=False, stop=True).then_inc(q["hidden_ps"], 1)

    def pe_second(pe, c, m):
        e, i = divmod(m, HC)
        y = y_bank[e % 2][:, 0:CT * C]
        if i == 0:
            at_least(pe, q["y_used"], EXPERTS * c + e - 1)
            pe.matmul(y.rearrange("p (j c) -> p j c", j=CT), ones2[:], b2_rows[:, e, None, :].to_broadcast([2, CT, C]),
                      start=True, stop=False, skip_group_check=True)
        at_least(pe, q["hidden_ready"], NH * c + m + 1)
        for j in range(CT):
            yj, t = y[:, j * C:(j + 1) * C], slice(j * P, (j + 1) * P)
            last = pe.matmul(yj, hidden[m % HBUF][:, t], w2[:, m, :], start=False, stop=(i == HC - 1),
                             skip_group_check=True)
        last.then_inc(q["hidden_used"], 1)

    def pe_chunk(pe, c):
        for m in range(NH):
            pe_first(pe, c, m)
            if inputs_at(c, m) is not None:
                pe_inputs(pe, inputs_at(c, m))
            if gates_at(c, m) is not None:
                pe_gates(pe, gates_at(c, m))
            if m >= LAG:
                pe_second(pe, c, m - LAG)
            elif not isinstance(c, int) or c > 0:
                pe_second(pe, c - 1, NH + m - LAG)

    def act_inputs(act, c):
        act.wait_ge(q["xT_ps"], c + 1)
        nc.scalar.activation(xT_hi[0:C, c, :], x_bank[c % 2][0:C, :], ACT.Copy)
        if c >= 2:
            act.wait_ge(q["scores"], c - 1)
        nc.scalar.activation(xT[c % 2][0:C, :], x_bank[c % 2][0:C, :], ACT.Copy).then_inc(q["xhi_ready"], 1)

    def act_gate(act, batch):
        first, end = (CT * c for c in BATCHES[batch])
        act.wait_ge(q["gate_step"], GSTEPS * batch + 2)
        nc.scalar.activation(pe_[:, first:end, :], shifted[:, first:end, :], ACT.Exp).then_inc(q["gate_exp"], 1)

    def act_chunk(act, c):
        for m in range(NH):
            G = NH * c + m
            at_least(act, q["hidden_ps"], G + 1)
            at_least(act, q["hidden_used"], G + 1 - HBUF)
            nc.scalar.activation(hidden[m % HBUF][:], h_bank[m % HBUF], ACT.Gelu).then_inc(q["hidden_ready"], 1)
            if inputs_at(c, m) is not None:
                act_inputs(act, inputs_at(c, m))

    def normalise(eng, vector, c, done):
        for j in range(CT):
            u = CT * c + j
            last = vector.tensor_scalar(xn[c % 2][:, j, :], x_all[:, u, :], s["ln_mean"][:, u:u + 1],
                                        s["ln_rstd"][:, u:u + 1], ALU.subtract, ALU.mult)
        last.then_inc(done, 1)

    def dve_inputs(v, c):
        v.wait_ge(q["xhi_ready"], c + 1)
        v.tensor_tensor(xT_lo[0:C, c, :], x_bank[c % 2][0:C, :], xT_hi[0:C, c, :],
                        ALU.subtract).then_inc(q["xlo_ready"], 1)

    def dve_gates(v, batch):
        first, end = (CT * c for c in BATCHES[batch])
        u, G, n = slice(first, end), GSTEPS * batch, end - first
        sc = g_bank[:, first * EXPERTS:end * EXPERTS].rearrange("p (j e) -> p j e", e=EXPERTS)
        v.wait_ge(q["scores"], BATCHES[batch][1])
        v.tensor_reduce(gmax[:, u], sc, AX.X, ALU.max).then_inc(q["gate_step"], 1)
        v.wait_ge(q["gate_step"], G + 1)
        v.tensor_tensor(shifted[:, u, :], sc, gmax[:, u, None].to_broadcast([P, n, EXPERTS]),
                        ALU.subtract).then_inc(q["gate_step"], 1)

    def dve_topk(v, batch):
        first, end = (CT * c for c in BATCHES[batch])
        u, G, n = slice(first, end), GSTEPS * batch, end - first
        p, ab, ti, gs = pe_[:, u, :], above[:, u], tied[:, u], gsum[:, u]
        v.wait_ge(q["gate_exp"], batch + 1)
        v.tensor_reduce(gs, p, AX.X, ALU.add).then_inc(q["gate_step"], 1)
        v.wait_ge(q["gate_step"], G + 3)
        v.reciprocal(gs, gs).then_inc(q["gate_step"], 1)
        v.wait_ge(q["gate_step"], G + 4)
        v.tensor_tensor(p, p, gsum[:, u, None].to_broadcast([P, n, EXPERTS]), ALU.mult).then_inc(q["gate_step"], 1)
        v.wait_ge(q["gate_step"], G + 5)
        for e in range(EXPERTS):
            mine = pe_[:, u, e:e + 1].to_broadcast([P, n, EXPERTS])
            v.tensor_tensor(above[:, u, e, :], p, mine, ALU.is_gt)
            last = v.tensor_tensor(tied[:, u, e, :], p, mine, ALU.is_equal)
        last.then_inc(q["gate_step"], 1)
        v.wait_ge(q["gate_step"], G + 6)
        v.tensor_tensor(ti, ti, earlier[:, None].to_broadcast([P, n, EXPERTS, EXPERTS]),
                        ALU.mult).then_inc(q["gate_step"], 1)
        v.wait_ge(q["gate_step"], G + 7)
        v.tensor_tensor(ab, ab, ti, ALU.add).then_inc(q["gate_step"], 1)
        v.wait_ge(q["gate_step"], G + 8)
        v.tensor_reduce(rank[:, u, :], ab, AX.X, ALU.add).then_inc(q["gate_step"], 1)
        v.wait_ge(q["gate_step"], G + 9)
        v.scalar_tensor_tensor(p, rank[:, u, :], float(TOP), p, ALU.is_lt, ALU.mult).then_inc(q["gate_step"], 1)
        v.wait_ge(q["gate_step"], G + 10)
        v.tensor_reduce(gs, p, AX.X, ALU.add).then_inc(q["gate_step"], 1)
        v.wait_ge(q["gate_step"], G + 11)
        v.tensor_scalar(gs, gs, 1e-9, None, ALU.add).then_inc(q["gate_step"], 1)
        v.wait_ge(q["gate_step"], G + 12)
        v.reciprocal(gmax[:, u], gs).then_inc(q["gates_ready"], 1)
        v.wait_ge(q["gates_ready"], 2 * batch + 1)
        v.tensor_tensor(gates[:, u, :], p, gmax[:, u, None].to_broadcast([P, n, EXPERTS]),
                        ALU.mult).then_inc(q["gates_ready"], 1)

    def dve_add(v, c, k, e):
        at_least(v, q["hidden_used"], NH * c + HC * (e + 1))
        if isinstance(c, int) and c < BATCHES[0][1]:
            v.wait_ge(q["gates_ready"], 2)
        if e == 0:
            at_least(v, stored[k], 16 * ((c - k) // 2))
        else:
            at_least(v, q["y_used"], EXPERTS * c + e)
        for j in range(CT):
            u = CT * c + j
            onto = x_all[:, u, :] if e == 0 else acc[k][:, j, :]
            last = v.scalar_tensor_tensor(acc[k][:, j, :], y_bank[e % 2][:, j * C:(j + 1) * C],
                                          gates[:, u, e:e + 1], onto, ALU.mult, ALU.add)
        last.then_inc(q["y_used"], 1)

    def dve_chunk(v, c, k):
        for m in range(NH):
            if inputs_at(c, m) is not None:
                dve_inputs(v, inputs_at(c, m))
            if m % HC == 2:
                e = m // HC - 1
                if e >= 0:
                    dve_add(v, c, k, e)
                elif not isinstance(c, int) or c > 0:
                    dve_add(v, c - 1, 1 - k, EXPERTS - 1)
            if isinstance(c, int) and c == 0 and m == 0:
                dve_topk(v, 0)
        if isinstance(c, int) and c == 1:
            dve_gates(v, 1)
            dve_topk(v, 1)
            v.wait_ge(q["gates_ready"], 4)

    def chunks(eng, step):
        step(eng, 0, 0)
        step(eng, 1, 1)
        with eng.Fori(1, CHUNKS // 2) as cc:
            step(eng, 2 * cc, 0)
            step(eng, 2 * cc + 1, 1)

    def pool_program(pool):
        for c in range(2, CHUNKS):
            if c == 2:
                pool.wait_ge(q["ln_newton_step"], 3)
            if CT * (c + 1) > NORM_PARTS[0][1]:
                pool.wait_ge(q["ln_newton_step"], 6)
            pool.wait_ge(q["xT_ps"], c - 1)
            normalise(pool, nc.gpsimd, c, q["xn_pool_ready"])
            pool.wait_ge(q["xn_pool_ready"], c - 1)

    def sync_program(sp):
        with sp.Fori(0, CHUNKS // 2) as cc:
            for k in range(2):
                c = 2 * cc + k
                sp.wait_ge(q["y_used"], EXPERTS * (c + 1))
                sp.dma_start(out_v[:, bass.ds(CT * c, CT), :], acc[k][:]).then_inc(stored[k], 16)
        for k in range(2):
            sp.wait_ge(stored[k], 16 * (CHUNKS // 2))

    def dve_program(v):
        chunks(v, dve_chunk)
        dve_add(v, CHUNKS - 1, 1, EXPERTS - 1)

    def act_program(act):
        norm_guess(act, nc, s, q, 1)
        act_gate(act, 0)
        act_chunk(act, 0)
        act_chunk(act, 1)
        act_gate(act, 1)
        with act.Fori(1, CHUNKS // 2) as cc:
            act_chunk(act, 2 * cc)
            act_chunk(act, 2 * cc + 1)

    def pe_program(pe):
        pe.wait_ge(s["w1_loaded"], 16)
        pe_chunk(pe, 0)
        pe_chunk(pe, 1)
        with pe.Fori(1, CHUNKS // 2) as cc:
            pe_chunk(pe, 2 * cc)
            pe_chunk(pe, 2 * cc + 1)
        for m in range(NH - LAG, NH):
            pe_second(pe, CHUNKS - 1, m)

    def normalise_first(v, c):
        normalise(v, nc.vector, c, q["xn_ready"])

    return {"q": q, "pool": pool_program, "sync": sync_program, "dve": dve_program, "act": act_program,
            "pe": pe_program, "pe_inputs": pe_inputs, "act_inputs": act_inputs, "dve_inputs": dve_inputs,
            "pe_gates": pe_gates, "dve_gates": dve_gates, "normalise": normalise_first}


def shape_constants():
    i = np.arange(P)
    perms = np.zeros((P, 5, P), np.float32)
    perms[i, 0, i] = 1
    row, col = i // HW, i % HW
    for tile in range(PER_IMAGE):
        r, c = (tile * WIN + row - SHIFT) % HW, (col - SHIFT) % HW
        perms[i, 1 + tile, r // WIN * KEYS + c // WIN * (KEYS // 2) + r % SHIFT * WIN + c % WIN] = 1
    w, r, c = i // KEYS, i % KEYS // WIN, i % WIN
    wcol = (w * WIN + c + SHIFT) % HW
    perms[i, 3, r * HW + wcol] = 1
    perms[i, 4, (r + SHIFT) % WIN * HW + wcol] = 1
    ch = np.arange(-(WIN - 1), WIN, dtype=np.float32)
    tab = np.stack(np.meshgrid(ch, ch, indexing="ij"), -1) / np.float32(WIN - 1) * np.float32(8)
    tab = np.sign(tab) * np.log2(np.abs(tab) + np.float32(1)) / np.float32(3)
    tab = tab[::-1, ::-1].reshape(-1, 2).astype(np.float32)
    rel = np.concatenate([tab.T, np.ones((1, tab.shape[0]), np.float32)])
    region = np.zeros((HW, HW), np.int64)
    cuts = (slice(0, HW - WIN), slice(HW - WIN, HW - SHIFT), slice(HW - SHIFT, HW))
    for m, hs in enumerate(cuts):
        for n, ws in enumerate(cuts):
            region[hs, ws] = 3 * m + n
    win = region.reshape(2, WIN, 2, WIN).transpose(0, 2, 1, 3).reshape(2, 2, KEYS)
    wmask = np.where(win[:, :, :, None] != win[:, :, None, :], -100.0, 0.0).astype(np.float32)
    wmask = wmask.reshape(2, P, KEYS).transpose(1, 0, 2)
    back = (QBLOCK + i % QBLOCK)[:, None] - np.arange(KEYS)[None]
    seen = (back >= 0) & (back <= BAND)
    seen = np.stack([seen & ~((i < QBLOCK)[:, None] & (np.arange(KEYS) < QBLOCK)[None]), seen], 1)
    bmask = np.where(seen, 0.0, MASKED).astype(np.float32)
    group = np.arange(C) // (C // GROUPS)
    gavg = (group[:, None] == group[None]).astype(np.float32) / np.float32(2 * C // GROUPS)
    earlier = (np.arange(EXPERTS)[None] < np.arange(EXPERTS)[:, None]).astype(np.float32)
    return {"permutations": perms, "rel_table": rel, "win_mask": wmask, "band_mask": bmask, "group_avg": gavg,
            "earlier": earlier}


def kernel(x, L0_conv_qkv_w, L0_conv_qkv_b, L0_conv_proj_w, L0_conv_proj_b, L0_conv_logit_scale, L0_conv_cpb_w1,
           L0_conv_cpb_b1, L0_conv_cpb_w2, L1_attn_qkv_w, L1_attn_qkv_b, L1_attn_proj_w, L1_attn_proj_b, L1_attn_gate,
           L1_ffn_gate_w, L1_ffn_gate_b, L1_ffn_w1, L1_ffn_b1, L1_ffn_w2, L1_ffn_b2):
    import concourse.bacc as bacc
    from concourse.bass_utils import run_bass_kernel_spmd

    cat = np.concatenate
    order = [4 * t + 2 * g + r for g in range(2) for t in range(TILES3) for r in range(2)]
    b0 = np.array(L0_conv_qkv_b)
    b0 = cat([b0[:C], np.zeros(C, np.float32), b0[2 * C:]])
    arrays = {
        "x": np.array(x),
        "w_qkv0": cat([np.array(L0_conv_qkv_w).T, b0[None]]),
        "w_proj0": cat([np.array(L0_conv_proj_w).T, np.array(L0_conv_proj_b)[None]]),
        "w_qkv1": cat([np.array(L1_attn_qkv_w), np.array(L1_attn_qkv_b)[None]]),
        "w_proj1": cat([np.array(L1_attn_proj_w), np.array(L1_attn_proj_b)[None]]),
        "gate_vec": np.array(L1_attn_gate)[:, None],
        "logit_scale": np.array(L0_conv_logit_scale).reshape(HEADS0),
        "cpb_w1": cat([np.array(L0_conv_cpb_w1).T, np.array(L0_conv_cpb_b1)[None]]),
        "cpb_w2": np.array(L0_conv_cpb_w2).T[:, order],
        "w1": cat([np.array(L1_ffn_w1).transpose(1, 0, 2).reshape(C, EXPERTS * HID),
                   np.array(L1_ffn_b1).reshape(1, EXPERTS * HID)]),
        "w2": np.array(L1_ffn_w2).reshape(NH, P, C).transpose(1, 0, 2),
        "b2": np.array(L1_ffn_b2).reshape(EXPERTS * C),
        "w_gate": cat([np.array(L1_ffn_gate_w), np.array(L1_ffn_gate_b)[None]]),
    }
    arrays.update(shape_constants())
    nc = bacc.Bacc("TRN2", target_bir_lowering=False, num_devices=1)
    feed, dram = {}, {}
    for name, value in arrays.items():
        feed["in_" + name] = np.ascontiguousarray(value)
        dram[name] = nc.dram_tensor("in_" + name, value.shape, mybir.dt.from_np(value.dtype), kind="ExternalInput").ap()
    out = nc.dram_tensor("out_0", (B, HW, HW, C), F32, kind="ExternalOutput").ap()
    build(nc, dram, out)
    result = run_bass_kernel_spmd(nc, [feed], core_ids=[0])
    return result.results[0]["out_0"]
```
